# Optimizing a Trainium2 kernel written in Bass

```python
import numpy as np
import jax
import jax.numpy as jnp

def _softmax(x, axis=-1):
    return jax.nn.softmax(x, axis=axis)

def _gelu(x):
    return jax.nn.gelu(x, approximate=True)

def _silu(x):
    return jax.nn.silu(x)

def _sigmoid(x):
    return jax.nn.sigmoid(x)

def _layernorm(x, axis=-1, eps=1e-05):
    m = jnp.mean(x, axis=axis, keepdims=True)
    v = jnp.var(x, axis=axis, keepdims=True)
    return (x - m) / jnp.sqrt(v + eps)

def _scatter_add(tgt, idx, src, axis=0):
    return tgt.at[idx].add(src)

def _segment_sum(src, seg, n):
    return jax.ops.segment_sum(src, seg, n)
kernel_name = 'mk_cond_seq_d4_seqx_r2_c7c7e1'

def setup_inputs(seed: int=0):
    np.random.seed(seed)
    _w = jnp.asarray

    def _rec_inputs():
        import jax
        import jax.numpy as jnp
        _rk = jax.random.key(seed)
        x = -0.000125 + 0.9999 * jax.random.normal(jax.random.fold_in(_rk, 1), (4, 1024, 512), jnp.float32)
        _lenS = 1024 - jax.random.randint(jax.random.fold_in(_rk, 7), (4,), 0, max(1, 1024 // 4) + 1, jnp.int32)
        _lenS2 = 1024 - jax.random.randint(jax.random.fold_in(_rk, 8), (4,), 0, max(1, 1024 // 4) + 1, jnp.int32)
        itok_B_0_15 = jax.random.randint(jax.random.fold_in(_rk, 11), (4,), 0, 16, jnp.int32)
        condB_theta = jax.random.uniform(jax.random.fold_in(_rk, 12), (4,), jnp.float32, 0.0, 0.983423)
        condB_phi = jax.random.uniform(jax.random.fold_in(_rk, 13), (4,), jnp.float32, 0.0, 0.961312)
        itok_B_34_63 = jax.random.randint(jax.random.fold_in(_rk, 15), (4,), 34, 64, jnp.int32)
        fside_Bx16xSxS_0 = -1.47943e-05 + 1.00017 * jax.random.normal(jax.random.fold_in(_rk, 16), (4, 16, 1024, 1024), jnp.float32)
        condB_gatescore = jax.random.uniform(jax.random.fold_in(_rk, 17), (4,), jnp.float32, 0.0, 0.581427)
        _validS = jnp.arange(1024)[None, :] < _lenS[:, None]
        _validS2 = jnp.arange(1024)[None, :] < _lenS2[:, None]
        _causal = jnp.tril(jnp.ones((1024, 1024), dtype=bool))
        mask_Bx1xSxS_bk0 = jnp.logical_not(jnp.broadcast_to(_validS[:, None, None, :], (4, 1, 1024, 1024)))
        return (x, itok_B_0_15, condB_theta, condB_phi, itok_B_34_63, fside_Bx16xSxS_0, condB_gatescore, mask_Bx1xSxS_bk0)
    x, itok_B_0_15, condB_theta, condB_phi, itok_B_34_63, fside_Bx16xSxS_0, condB_gatescore, mask_Bx1xSxS_bk0 = _rec_inputs()

    def _L0_cond_setup():
        import jax, jax.numpy as jnp
        import numpy as np
        B, S, D = (32, 512, 512)
        A = 128
        E = 16
        LN_EPS = 1e-05
        key = jax.random.key(seed)
        ks = jax.random.split(key, 10)
        s = lambda fan_in: 1.0 / np.sqrt(fan_in)
        return {'hidden_states': jax.random.normal(ks[0], (B, S, D), dtype=jnp.float32), 'domain_id': jax.random.randint(ks[1], (B,), 0, E, dtype=jnp.int64), 'down_W': jax.random.uniform(ks[2], (A, D), jnp.float32, -s(D), s(D)), 'down_b': jax.random.uniform(ks[3], (A,), jnp.float32, -s(D), s(D)), 'up_W': jax.random.uniform(ks[4], (D, A), jnp.float32, -s(A), s(A)), 'up_b': jax.random.uniform(ks[5], (D,), jnp.float32, -s(A), s(A)), 'expert_W': jax.random.uniform(ks[6], (E, A, A), jnp.float32, -s(A), s(A)), 'expert_b': jax.random.uniform(ks[7], (E, A), jnp.float32, -s(A), s(A)), 'domain_emb': jax.random.normal(ks[8], (E, A), dtype=jnp.float32), 'ln_gamma': jnp.ones((D,), jnp.float32), 'ln_beta': jnp.zeros((D,), jnp.float32)}
    _L0_cond_all = _L0_cond_setup()
    _L0_cond_in = {k: v for k, v in _L0_cond_all.items() if k in ('down_W', 'down_b', 'up_W', 'up_b', 'expert_W', 'expert_b', 'domain_emb', 'ln_gamma', 'ln_beta')}
    del _L0_cond_all

    def _L1_cond_setup():
        import jax, jax.numpy as jnp
        import numpy as np
        key = jax.random.key(seed)
        k1, k2, k3 = jax.random.split(key, 3)
        B, N, D = (16, 2048, 512)
        embeddings = jax.random.normal(k1, (B, N, D), dtype=jnp.float32)
        theta = jax.random.uniform(k2, (B,), dtype=jnp.float32)
        phi = jax.random.uniform(k3, (B,), dtype=jnp.float32)
        return {'embeddings': embeddings, 'theta': theta, 'phi': phi}
    _L1_cond_all = _L1_cond_setup()
    _L1_cond_in = {k: v for k, v in _L1_cond_all.items() if k in ()}
    del _L1_cond_all

    def _L2_cond_setup():
        import jax, jax.numpy as jnp
        import numpy as np
        import math
        D_MODEL = 512
        N_HEAD = 16
        HEAD_DIM = D_MODEL // N_HEAD
        D_FF = 2048
        NUM_STEPS = 100.0
        RESCALE = 4000.0
        EPS = 1e-05

        def _sin_emb(t):
            half = D_MODEL // 2
            x = t.astype(jnp.float32) / NUM_STEPS * RESCALE
            freqs = jnp.exp(jnp.arange(half, dtype=jnp.float32) * (-math.log(10000.0) / (half - 1)))
            e = x[:, None] * freqs[None, :]
            return jnp.concatenate([jnp.sin(e), jnp.cos(e)], axis=-1)

        def _ln(x):
            m = jnp.mean(x, axis=-1, keepdims=True)
            v = jnp.var(x, axis=-1, keepdims=True)
            return (x - m) / jnp.sqrt(v + EPS)

        def _gelu2(x):
            return x * jax.nn.sigmoid(1.702 * x)
        key = jax.random.key(seed)
        ks = jax.random.split(key, 24)
        B, S, D, F = (4, 256, D_MODEL, D_FF)
        std = 0.02
        inp = {'src': jax.random.normal(ks[0], (B, S, D), dtype=jnp.float32), 'src_mask': jax.random.randint(ks[1], (B, 1, S, S), 0, 2).astype(bool), 'timestep': jax.random.randint(ks[2], (B,), 0, 100, dtype=jnp.int32), 'attention_bias': jax.random.normal(ks[3], (B, N_HEAD, S, S), dtype=jnp.float32), 'W_ada': jax.random.normal(ks[4], (D, 2 * D), dtype=jnp.float32) * std, 'b_ada': jnp.zeros((2 * D,), dtype=jnp.float32), 'Wq': jax.random.normal(ks[5], (D, D), dtype=jnp.float32) * std, 'bq': jnp.zeros((D,), dtype=jnp.float32), 'Wk': jax.random.normal(ks[6], (D, D), dtype=jnp.float32) * std, 'bk': jnp.zeros((D,), dtype=jnp.float32), 'Wv': jax.random.normal(ks[7], (D, D), dtype=jnp.float32) * std, 'bv': jnp.zeros((D,), dtype=jnp.float32), 'Wo': jax.random.normal(ks[8], (D, D), dtype=jnp.float32) * std, 'bo': jnp.zeros((D,), dtype=jnp.float32), 'W1': jax.random.normal(ks[9], (D, F), dtype=jnp.float32) * std, 'b1': jnp.zeros((F,), dtype=jnp.float32), 'W2': jax.random.normal(ks[10], (F, D), dtype=jnp.float32) * std, 'b2': jnp.zeros((D,), dtype=jnp.float32), 'g2': jnp.ones((D,), dtype=jnp.float32), 'beta2': jnp.zeros((D,), dtype=jnp.float32)}
        return inp
    _L2_cond_all = _L2_cond_setup()
    _L2_cond_in = {k: v for k, v in _L2_cond_all.items() if k in ('W_ada', 'b_ada', 'Wq', 'bq', 'Wk', 'bk', 'Wv', 'bv', 'Wo', 'bo', 'W1', 'b1', 'W2', 'b2', 'g2', 'beta2')}
    del _L2_cond_all

    def _L3_cond_setup():
        import jax, jax.numpy as jnp
        import numpy as np
        D_MODEL = 512
        N_HEADS = 16
        D_HEAD = D_MODEL // N_HEADS
        D_FF = 2048
        EPS = 1e-05

        def layernorm(x, gamma, beta):
            mu = jnp.mean(x, axis=-1, keepdims=True)
            var = jnp.var(x, axis=-1, keepdims=True)
            return (x - mu) * jax.lax.rsqrt(var + EPS) * gamma + beta
        key = jax.random.key(seed)
        ks = jax.random.split(key, 16)
        B, T = (4, 1024)
        s = 1.0 / np.sqrt(D_MODEL)
        sf = 1.0 / np.sqrt(D_FF)
        return {'x': jax.random.normal(ks[0], (B, T, D_MODEL), jnp.float32), 'gate_score': jax.random.uniform(ks[1], (B,), jnp.float32), 'Wq': jax.random.normal(ks[2], (D_MODEL, D_MODEL), jnp.float32) * s, 'bq': jnp.zeros((D_MODEL,), jnp.float32), 'Wk': jax.random.normal(ks[3], (D_MODEL, D_MODEL), jnp.float32) * s, 'bk': jnp.zeros((D_MODEL,), jnp.float32), 'Wv': jax.random.normal(ks[4], (D_MODEL, D_MODEL), jnp.float32) * s, 'bv': jnp.zeros((D_MODEL,), jnp.float32), 'Wo': jax.random.normal(ks[5], (D_MODEL, D_MODEL), jnp.float32) * s, 'bo': jnp.zeros((D_MODEL,), jnp.float32), 'W1': jax.random.normal(ks[6], (D_MODEL, D_FF), jnp.float32) * s, 'b1': jnp.zeros((D_FF,), jnp.float32), 'W2': jax.random.normal(ks[7], (D_FF, D_MODEL), jnp.float32) * sf, 'b2': jnp.zeros((D_MODEL,), jnp.float32), 'gamma1': jnp.ones((D_MODEL,), jnp.float32), 'beta1': jnp.zeros((D_MODEL,), jnp.float32), 'gamma2': jnp.ones((D_MODEL,), jnp.float32), 'beta2': jnp.zeros((D_MODEL,), jnp.float32)}
    _L3_cond_all = _L3_cond_setup()
    _L3_cond_in = {k: v for k, v in _L3_cond_all.items() if k in ('Wq', 'bq', 'Wk', 'bk', 'Wv', 'bv', 'Wo', 'bo', 'W1', 'b1', 'W2', 'b2', 'gamma1', 'beta1', 'gamma2', 'beta2')}
    del _L3_cond_all
    return {'x': x, 'itok_B_0_15': itok_B_0_15, 'condB_theta': condB_theta, 'condB_phi': condB_phi, 'itok_B_34_63': itok_B_34_63, 'fside_Bx16xSxS_0': fside_Bx16xSxS_0, 'condB_gatescore': condB_gatescore, 'mask_Bx1xSxS_bk0': mask_Bx1xSxS_bk0, 'L0_cond_down_W': _L0_cond_in['down_W'], 'L0_cond_down_b': _L0_cond_in['down_b'], 'L0_cond_up_W': _L0_cond_in['up_W'], 'L0_cond_up_b': _L0_cond_in['up_b'], 'L0_cond_expert_W': _L0_cond_in['expert_W'], 'L0_cond_expert_b': _L0_cond_in['expert_b'], 'L0_cond_domain_emb': _L0_cond_in['domain_emb'], 'L0_cond_ln_gamma': _L0_cond_in['ln_gamma'], 'L0_cond_ln_beta': _L0_cond_in['ln_beta'], 'L2_cond_W_ada': _L2_cond_in['W_ada'], 'L2_cond_b_ada': _L2_cond_in['b_ada'], 'L2_cond_Wq': _L2_cond_in['Wq'], 'L2_cond_bq': _L2_cond_in['bq'], 'L2_cond_Wk': _L2_cond_in['Wk'], 'L2_cond_bk': _L2_cond_in['bk'], 'L2_cond_Wv': _L2_cond_in['Wv'], 'L2_cond_bv': _L2_cond_in['bv'], 'L2_cond_Wo': _L2_cond_in['Wo'], 'L2_cond_bo': _L2_cond_in['bo'], 'L2_cond_W1': _L2_cond_in['W1'], 'L2_cond_b1': _L2_cond_in['b1'], 'L2_cond_W2': _L2_cond_in['W2'], 'L2_cond_b2': _L2_cond_in['b2'], 'L2_cond_g2': _L2_cond_in['g2'], 'L2_cond_beta2': _L2_cond_in['beta2'], 'L3_cond_Wq': _L3_cond_in['Wq'], 'L3_cond_bq': _L3_cond_in['bq'], 'L3_cond_Wk': _L3_cond_in['Wk'], 'L3_cond_bk': _L3_cond_in['bk'], 'L3_cond_Wv': _L3_cond_in['Wv'], 'L3_cond_bv': _L3_cond_in['bv'], 'L3_cond_Wo': _L3_cond_in['Wo'], 'L3_cond_bo': _L3_cond_in['bo'], 'L3_cond_W1': _L3_cond_in['W1'], 'L3_cond_b1': _L3_cond_in['b1'], 'L3_cond_W2': _L3_cond_in['W2'], 'L3_cond_b2': _L3_cond_in['b2'], 'L3_cond_gamma1': _L3_cond_in['gamma1'], 'L3_cond_beta1': _L3_cond_in['beta1'], 'L3_cond_gamma2': _L3_cond_in['gamma2'], 'L3_cond_beta2': _L3_cond_in['beta2']}

def reference(x, itok_B_0_15, condB_theta, condB_phi, itok_B_34_63, fside_Bx16xSxS_0, condB_gatescore, mask_Bx1xSxS_bk0, L0_cond_down_W, L0_cond_down_b, L0_cond_up_W, L0_cond_up_b, L0_cond_expert_W, L0_cond_expert_b, L0_cond_domain_emb, L0_cond_ln_gamma, L0_cond_ln_beta, L2_cond_W_ada, L2_cond_b_ada, L2_cond_Wq, L2_cond_bq, L2_cond_Wk, L2_cond_bk, L2_cond_Wv, L2_cond_bv, L2_cond_Wo, L2_cond_bo, L2_cond_W1, L2_cond_b1, L2_cond_W2, L2_cond_b2, L2_cond_g2, L2_cond_beta2, L3_cond_Wq, L3_cond_bq, L3_cond_Wk, L3_cond_bk, L3_cond_Wv, L3_cond_bv, L3_cond_Wo, L3_cond_bo, L3_cond_W1, L3_cond_b1, L3_cond_W2, L3_cond_b2, L3_cond_gamma1, L3_cond_beta1, L3_cond_gamma2, L3_cond_beta2):
    import jax
    import jax.numpy as jnp

    def _L0_cond_ref(hidden_states, domain_id, down_W, down_b, up_W, up_b, expert_W, expert_b, domain_emb, ln_gamma, ln_beta):
        import jax, jax.numpy as jnp
        import numpy as np
        B, S, D = (32, 512, 512)
        A = 128
        E = 16
        LN_EPS = 1e-05
        residual = hidden_states
        hidden = jnp.einsum('bsd,ad->bsa', hidden_states, down_W) + down_b
        hidden = jax.nn.gelu(hidden, approximate=False)
        valid = (domain_id >= 0) & (domain_id < E)
        idx = jnp.clip(domain_id, 0, E - 1)
        Wsel = expert_W[idx]
        bsel = expert_b[idx]
        expert_out = jnp.einsum('bsa,boa->bso', hidden, Wsel) + bsel[:, None, :]
        domain_output = jnp.where(valid[:, None, None], expert_out, hidden)
        hidden = domain_output + domain_emb[idx][:, None, :]
        hidden = jnp.einsum('bsa,da->bsd', hidden, up_W) + up_b
        x = hidden + residual
        mu = jnp.mean(x, axis=-1, keepdims=True)
        var = jnp.mean(jnp.square(x - mu), axis=-1, keepdims=True)
        return (x - mu) * jax.lax.rsqrt(var + LN_EPS) * ln_gamma + ln_beta

    def _L1_cond_ref(embeddings, theta, phi):
        import jax, jax.numpy as jnp
        import numpy as np
        B, N, D = embeddings.shape
        e = embeddings.reshape(B, N, D // 4, 4)
        ct = jnp.cos(theta)[:, None, None]
        st = jnp.sin(theta)[:, None, None]
        cp = jnp.cos(phi)[:, None, None]
        sp = jnp.sin(phi)[:, None, None]
        x0, x1, x2, x3 = (e[..., 0], e[..., 1], e[..., 2], e[..., 3])
        out = jnp.stack([x0 * ct + x1 * st, -x0 * st + x1 * ct, x2 * cp + x3 * sp, -x2 * sp + x3 * cp], axis=-1)
        return out.reshape(B, N, D)

    def _L2_cond_ref(src, src_mask, timestep, attention_bias, W_ada, b_ada, Wq, bq, Wk, bk, Wv, bv, Wo, bo, W1, b1, W2, b2, g2, beta2):
        import jax, jax.numpy as jnp
        import numpy as np
        import math
        D_MODEL = 512
        N_HEAD = 16
        HEAD_DIM = D_MODEL // N_HEAD
        D_FF = 2048
        NUM_STEPS = 100.0
        RESCALE = 4000.0
        EPS = 1e-05

        def _sin_emb(t):
            half = D_MODEL // 2
            x = t.astype(jnp.float32) / NUM_STEPS * RESCALE
            freqs = jnp.exp(jnp.arange(half, dtype=jnp.float32) * (-math.log(10000.0) / (half - 1)))
            e = x[:, None] * freqs[None, :]
            return jnp.concatenate([jnp.sin(e), jnp.cos(e)], axis=-1)

        def _ln(x):
            m = jnp.mean(x, axis=-1, keepdims=True)
            v = jnp.var(x, axis=-1, keepdims=True)
            return (x - m) / jnp.sqrt(v + EPS)

        def _gelu2(x):
            return x * jax.nn.sigmoid(1.702 * x)
        B, S, D = src.shape
        emb = jax.nn.silu(_sin_emb(timestep)) @ W_ada + b_ada
        scale, shift = jnp.split(emb[:, None, :], 2, axis=-1)
        x = _ln(src) * (1.0 + scale) + shift
        q = (x @ Wq + bq).reshape(B, S, N_HEAD, HEAD_DIM).transpose(0, 2, 1, 3)
        k = (x @ Wk + bk).reshape(B, S, N_HEAD, HEAD_DIM).transpose(0, 2, 1, 3)
        v = (x @ Wv + bv).reshape(B, S, N_HEAD, HEAD_DIM).transpose(0, 2, 1, 3)
        scores = jnp.einsum('bhqd,bhkd->bhqk', q / math.sqrt(HEAD_DIM), k)
        scores = scores + attention_bias
        scores = jnp.where(src_mask, -jnp.inf, scores.astype(jnp.float32))
        probs = jax.nn.softmax(scores, axis=-1).astype(v.dtype)
        ctx = jnp.einsum('bhqk,bhkd->bhqd', probs, v)
        ctx = ctx.transpose(0, 2, 1, 3).reshape(B, S, D)
        x = x + (ctx @ Wo + bo)
        h = _ln(x) * g2 + beta2
        ff = _gelu2(h @ W1 + b1) @ W2 + b2
        return x + ff

    def _L3_cond_ref(x, gate_score, Wq, bq, Wk, bk, Wv, bv, Wo, bo, W1, b1, W2, b2, gamma1, beta1, gamma2, beta2):
        import jax, jax.numpy as jnp
        import numpy as np
        D_MODEL = 512
        N_HEADS = 16
        D_HEAD = D_MODEL // N_HEADS
        D_FF = 2048
        EPS = 1e-05

        def layernorm(x, gamma, beta):
            mu = jnp.mean(x, axis=-1, keepdims=True)
            var = jnp.var(x, axis=-1, keepdims=True)
            return (x - mu) * jax.lax.rsqrt(var + EPS) * gamma + beta
        B, T, C = x.shape
        h = layernorm(x, gamma1, beta1)
        Q = (h @ Wq + bq).reshape(B, T, N_HEADS, D_HEAD).transpose(0, 2, 1, 3)
        K = (h @ Wk + bk).reshape(B, T, N_HEADS, D_HEAD).transpose(0, 2, 1, 3)
        V = (h @ Wv + bv).reshape(B, T, N_HEADS, D_HEAD).transpose(0, 2, 1, 3)
        scores = jnp.einsum('bhqd,bhkd->bhqk', Q, K) / np.sqrt(D_HEAD)
        causal = jnp.tril(jnp.ones((T, T), dtype=bool))
        scores = jnp.where(causal, scores, -jnp.inf)
        attn = jax.nn.softmax(scores, axis=-1)
        ctx = jnp.einsum('bhqk,bhkd->bhqd', attn, V)
        ctx = ctx.transpose(0, 2, 1, 3).reshape(B, T, C)
        attn_out = ctx @ Wo + bo
        x1 = x + attn_out
        h2 = layernorm(x1, gamma2, beta2)
        ff = jax.nn.gelu(h2 @ W1 + b1, approximate=False) @ W2 + b2
        x2 = x1 + ff
        g = gate_score[:, None, None]
        return x + g * (x2 - x)
    x = _L0_cond_ref(x, itok_B_0_15, L0_cond_down_W, L0_cond_down_b, L0_cond_up_W, L0_cond_up_b, L0_cond_expert_W, L0_cond_expert_b, L0_cond_domain_emb, L0_cond_ln_gamma, L0_cond_ln_beta)
    x = _L1_cond_ref(x, condB_theta, condB_phi)
    x = _L2_cond_ref(x, mask_Bx1xSxS_bk0, itok_B_34_63, fside_Bx16xSxS_0, L2_cond_W_ada, L2_cond_b_ada, L2_cond_Wq, L2_cond_bq, L2_cond_Wk, L2_cond_bk, L2_cond_Wv, L2_cond_bv, L2_cond_Wo, L2_cond_bo, L2_cond_W1, L2_cond_b1, L2_cond_W2, L2_cond_b2, L2_cond_g2, L2_cond_beta2)
    x = _L3_cond_ref(x, condB_gatescore, L3_cond_Wq, L3_cond_bq, L3_cond_Wk, L3_cond_bk, L3_cond_Wv, L3_cond_bv, L3_cond_Wo, L3_cond_bo, L3_cond_W1, L3_cond_b1, L3_cond_W2, L3_cond_b2, L3_cond_gamma1, L3_cond_beta1, L3_cond_gamma2, L3_cond_beta2)
    return x

_drawn_inputs = setup_inputs


def setup_inputs(seed=0):
    import zlib

    import numpy as np

    out = dict(_drawn_inputs(seed))
    spreads = {'L0_cond_ln_gamma': (1.0, 0.2),
     'L0_cond_ln_beta': (0.0, 0.1),
     'L2_cond_b_ada': (0.0, 0.1),
     'L2_cond_bq': (0.0, 0.8),
     'L2_cond_bk': (0.0, 2.0),
     'L2_cond_bv': (0.0, 0.1),
     'L2_cond_bo': (0.0, 0.1),
     'L2_cond_b1': (0.0, 0.1),
     'L2_cond_b2': (0.0, 0.1),
     'L2_cond_g2': (1.0, 0.2),
     'L2_cond_beta2': (0.0, 0.348),
     'L3_cond_bq': (0.0, 2.0),
     'L3_cond_bk': (0.0, 2.0),
     'L3_cond_bv': (0.0, 0.1),
     'L3_cond_bo': (0.0, 0.1),
     'L3_cond_b1': (0.0, 0.428),
     'L3_cond_b2': (0.0, 0.273),
     'L3_cond_gamma1': (1.0, 0.2),
     'L3_cond_beta1': (0.0, 0.1),
     'L3_cond_gamma2': (1.0, 0.2),
     'L3_cond_beta2': (0.0, 0.411)}
    factors = {'fside_Bx16xSxS_0': 7.582, 'L0_cond_down_b': 8.0, 'L2_cond_Wq': 8.0, 'L2_cond_Wk': 8.0}
    for name, (base, spread) in spreads.items():
        noise = np.random.default_rng([zlib.crc32(name.encode()), seed]).standard_normal(out[name].shape)
        drawn = base * np.exp(spread * noise) if base else spread * noise
        out[name] = jnp.asarray(drawn.astype(out[name].dtype))
    for name, factor in factors.items():
        out[name] = (out[name] * factor).astype(out[name].dtype)
    return out
```

```python
import math
from contextlib import ExitStack

import concourse.bass as bass
import concourse.mybir as mybir
import numpy as np

ALU = mybir.AluOpType
ACT = mybir.ActivationFunctionType
F32 = mybir.dt.float32
F32R = mybir.dt.float32r
BF16 = mybir.dt.bfloat16
I32 = mybir.dt.int32
U8 = mybir.dt.uint8

P = 128
B = 4
S = 1024
D = 512
A = 128
E = 16
H = 16
DH = D // H
F = 2048
DC = D // P
FC = F // P
TB = 512
TT = TB // P
NB = B * S // TB
BPS = S // TB
HG = P // DH
G = H // HG
NBG = B * G
KT = S // P
QP = S // 256
EPS = 1e-5
MASKED = -1e30
DMA = 16


def need(eng, semaphore, value):
    if isinstance(value, int) and value <= 0:
        return
    eng.wait_ge(semaphore, value)


def apart(eng):
    eng.nop(nofuse=True)


class Chain:

    def __init__(self, eng, semaphore, start=0):
        self.eng, self.semaphore, self.start, self.count = eng, semaphore, start, 0

    def link(self, instruction):
        instruction.then_inc(self.semaphore, 1)
        self.count += 1
        self.wait()

    def wait(self):
        self.eng.wait_ge(self.semaphore, self.start + self.count)


def product(pe, out, stationary, moving, first, last):
    (sh, sl), (mh, ml) = stationary, moving
    pe.matmul(out, sh, mh, start=first, stop=False)
    pe.matmul(out, sh, ml, start=False, stop=False)
    return pe.matmul(out, sl, mh, start=False, stop=last)


class Kernel:
    def __init__(self, nc, ins, out):
        self.nc, self.ins, self.out = nc, ins, out
        self.ctx = ExitStack()
        dram = lambda name, shape: nc.dram_tensor(name, shape, F32, kind="Internal").ap()
        self.rows = [dram(f"rows{n}", [B * S, D]) for n in range(2)]
        self.qk = [{n: dram(f"{n}{layer}", [B * D, S]) for n in ("qh", "ql", "kh", "kl")} for layer in range(2)]
        self.v = [dram(f"v{layer}", [NBG, S, P]) for layer in range(2)]
        self.attended = [dram(f"attended{layer}", [B * D, S]) for layer in range(2)]

    def sem(self, name):
        return self.ctx.enter_context(self.nc.semaphore(name))

    def build(self):
        nc = self.nc
        with self.ctx:
            sb = lambda name, shape, dt: self.ctx.enter_context(nc.sbuf_tensor(name, shape, dt))
            self.weight_sems = ([self.sem(f"weights_loaded{i}") for i in range(2)], self.sem("weights_scaled"),
                                self.sem("weights_rounded"), self.sem("weights_split"))
            self.weights_done = (0, 0, [0, 0])
            self.ident = sb("ident", [P, P], F32)
            self.ident16 = sb("ident16", [P, P], BF16)
            self.psum = self.ctx.enter_context(nc.psum_tensor("psum", [P, 8, 512], F32))
            with ExitStack() as memory:
                self.constants(memory)
                self.front(memory)
            with ExitStack() as memory:
                self.attention(memory, 0)
            with ExitStack() as memory:
                self.feed_forward(memory, 0)
            with ExitStack() as memory:
                self.project(memory)
            with ExitStack() as memory:
                self.attention(memory, 1)
            with ExitStack() as memory:
                self.feed_forward(memory, 1)


    def constants(self, memory):
        nc, ins = self.nc, self.ins
        sb = lambda name, shape, dt=F32: memory.enter_context(nc.sbuf_tensor(name, shape, dt))
        self.scale1 = sb("ada_scale", [P, B, D])
        self.shift = sb("ada_shift", [P, B, D])
        self.rot_own = sb("rot_own", [P, B, D])
        self.rot_other = sb("rot_other", [P, B, D])
        self.rot_beta = sb("rot_beta", [P, B, D])
        self.expert_h = sb("expert_h", [P, B, A], F32R)
        self.expert_l = sb("expert_l", [P, B, A], F32R)
        self.expert_bias = sb("expert_bias", [P, B])
        NA = 4 * B + 2 * B
        with ExitStack() as own:
            tb = lambda name, shape, dt=F32: own.enter_context(nc.sbuf_tensor(f"const_{name}", shape, dt))
            w_ada = tb("w_ada", [P, DC, 2 * D])
            b_ada = tb("b_ada", [P, 2 * D])
            gamma = tb("gamma0", [P, D])
            beta = tb("beta0", [P, D])
            experts = tb("experts", [P, E, A])
            expert_b = tb("expert_b", [P, E])
            domain = tb("domain", [P, E])
            freqs = tb("freqs", [P, 4])
            iota = tb("iota", [P, E])
            steps_i = tb("steps_i", [P, B], I32)
            steps = tb("steps", [P, B])
            ids_i = tb("ids_i", [P, B], I32)
            ids = tb("ids", [P, B])
            clipped = tb("clipped", [P, B])
            valid = tb("valid", [P, B])
            valid2 = tb("valid2", [P, B])
            onehot = tb("onehot", [P, B, E])
            onehot_valid = tb("onehot_valid", [P, B, E])
            angle = tb("angle", [P, NA])
            turns = tb("turns", [P, NA])
            reduced = tb("reduced", [P, NA])
            flipped = tb("flipped", [P, NA])
            sine = tb("sine", [P, NA])
            cosine = tb("cosine", [P, NA])
            minus_sine = tb("minus_sine", [P, NA])
            emb = tb("emb", [P, 4, B])
            emb_act = tb("emb_act", [P, 4, B])
            spread = tb("spread", [P, B, 4, P])
            chosen = tb("chosen", [P, B, A])
            part = tb("part", [P, E])
            bsum = tb("bsum", [P, 2 * B])
            loaded = self.sem("const_loaded")
            ident_steps = self.sem("ident_steps")
            vec = self.sem("const_vector")
            reduced_done = self.sem("angles_reduced")
            sines_done = self.sem("sines_done")
            emb_ready = self.sem("emb_ready")
            spread_done = self.sem("emb_spread")
            ada_done = self.sem("ada_products")
            ada_used = self.sem("ada_products_used")
            loads = [
                (steps_i[:, :], ins["timestep"].partition_broadcast(P)),
                (ids_i[:, :], ins["domain_id"].partition_broadcast(P)),
                (angle[:, 16:20], ins["theta"].partition_broadcast(P)),
                (angle[:, 20:24], ins["phi"].partition_broadcast(P)),
                (freqs[:, :], ins["freqs"]),
                (iota[:, :], ins["iota"].partition_broadcast(P)),
                (gamma[:, :], ins["L0_ln_gamma"].partition_broadcast(P)),
                (beta[:, :], ins["L0_ln_beta"].partition_broadcast(P)),
                (experts[:, :, :], ins["L0_expert_WT"]),
                (expert_b[:, :], ins["L0_expert_bT"]),
                (domain[:, :], ins["L0_domain_embT"]),
                (w_ada[:, :, :], ins["L2_W_ada"].rearrange("(c p) n -> p c n", p=P)),
                (b_ada[:, :], ins["L2_b_ada"].partition_broadcast(P)),
            ]
            ident, ident16, psum = self.ident, self.ident16, self.psum
            with nc.Block() as block:

                @block.sync
                def _(sp):
                    for dst, src in loads:
                        sp.dma_start(dst, src).then_inc(loaded, DMA)

                @block.gpsimd
                def _(pool):
                    pool.memset(ident[:, :], 0.0).then_inc(ident_steps, 1)
                    pool.memset(ident16[:, :], 0.0).then_inc(ident_steps, 1)
                    pool.wait_ge(ident_steps, 2)
                    for m in (ident, ident16):
                        pool.affine_select(out=m[:, :], in_=m[:, :], compare_op=ALU.not_equal, fill=1.0, base=0,
                                           pattern=[[-1, P]], channel_multiplier=1).then_inc(ident_steps, 1)

                @block.vector
                def _(dve):
                    chain = Chain(dve, vec)
                    link = chain.link
                    dve.wait_ge(loaded, DMA * len(loads))
                    dve.wait_ge(ident_steps, 4)
                    link(dve.tensor_copy(steps[:, :], steps_i[:, :]))
                    link(dve.tensor_scalar(steps[:, :], steps[:, :], 40.0, None, ALU.mult))
                    for b in range(B):
                        link(dve.tensor_scalar(angle[:, 0:16].rearrange("p (c b) -> p c b", b=B)[:, :, b],
                                               freqs[:, :], steps[:, b:b + 1], None, ALU.mult))
                    link(dve.tensor_scalar(turns[:, :], angle[:, :], 1 / (2 * math.pi), 12582912.0, ALU.mult, ALU.add))
                    link(dve.tensor_scalar(turns[:, :], turns[:, :], 12582912.0, None, ALU.subtract))
                    link(dve.scalar_tensor_tensor(out=reduced[:, :], in0=turns[:, :], scalar=-6.28125, in1=angle[:, :],
                                                  op0=ALU.mult, op1=ALU.add))
                    link(dve.scalar_tensor_tensor(out=reduced[:, :], in0=turns[:, :], scalar=-(2 * math.pi - 6.28125),
                                                  in1=reduced[:, :], op0=ALU.mult, op1=ALU.add))
                    link(dve.tensor_scalar(reduced[:, :], reduced[:, :], 3.1415925, -3.1415925, ALU.min, ALU.max))
                    link(dve.tensor_scalar(flipped[:, :], reduced[:, :], -1.0, None, ALU.mult))
                    link(dve.tensor_tensor(flipped[:, :], flipped[:, :], reduced[:, :], ALU.max))
                    dve.tensor_scalar(flipped[:, :], flipped[:, :], -1.0, math.pi / 2, ALU.mult,
                                      ALU.add).then_inc(reduced_done, 1)
                    link(dve.tensor_copy(ids[:, :], ids_i[:, :]))
                    link(dve.tensor_scalar(clipped[:, :], ids[:, :], 0.0, float(E - 1), ALU.max, ALU.min))
                    link(dve.tensor_tensor(valid[:, :], clipped[:, :], ids[:, :], ALU.is_equal))
                    link(dve.tensor_scalar(valid2[:, :], valid[:, :], -1.0, 1.0, ALU.mult, ALU.add))
                    for b in range(B):
                        link(dve.tensor_scalar(onehot[:, b, :], iota[:, :], clipped[:, b:b + 1], None, ALU.is_equal))
                        link(dve.tensor_scalar(onehot_valid[:, b, :], onehot[:, b, :], valid[:, b:b + 1], None,
                                               ALU.mult))
                        link(dve.tensor_scalar(chosen[:, b, :], ident[:, :], valid2[:, b:b + 1], None, ALU.mult))
                    for e in range(E):
                        for b in range(B):
                            last = dve.scalar_tensor_tensor(out=chosen[:, b, :], in0=experts[:, e, :],
                                                            scalar=onehot_valid[:, b, e:e + 1], in1=chosen[:, b, :],
                                                            op0=ALU.mult, op1=ALU.add)
                            last.then_inc(vec, 1)
                            chain.count += 1
                        chain.wait()
                    for b in range(B):
                        link(dve.tensor_copy(self.expert_h[:, b, :], chosen[:, b, :]))
                        link(dve.tensor_tensor(self.expert_l[:, b, :], chosen[:, b, :],
                                               self.expert_h[:, b, :].bitcast(F32), ALU.subtract))
                        link(dve.tensor_tensor_reduce(out=part[:, :], in0=expert_b[:, :], in1=onehot_valid[:, b, :],
                                                      scale=1.0, scalar=0.0, op0=ALU.mult, op1=ALU.add,
                                                      accum_out=bsum[:, b:b + 1]))
                        link(dve.tensor_tensor_reduce(out=part[:, :], in0=domain[:, :], in1=onehot[:, b, :],
                                                      scale=1.0, scalar=0.0, op0=ALU.mult, op1=ALU.add,
                                                      accum_out=bsum[:, B + b:B + b + 1]))
                    link(dve.tensor_tensor(self.expert_bias[:, :], bsum[:, 0:B], bsum[:, B:2 * B], ALU.add))
                    dve.wait_ge(sines_done, 2)
                    link(dve.tensor_copy(emb[:, 0:2, :].rearrange("p c b -> p (c b)"), sine[:, 0:8]))
                    dve.tensor_copy(emb[:, 2:4, :].rearrange("p c b -> p (c b)"), cosine[:, 8:16]).then_inc(emb_ready, 1)
                    dve.wait_ge(sines_done, 3)
                    link(dve.memset(spread[:, :, :, :], 0.0))
                    for b in range(B):
                        for c in range(4):
                            dve.tensor_scalar(spread[:, b, c, :], spread[:, b, c, :], emb_act[:, c, b:b + 1], None,
                                              ALU.add).then_inc(spread_done, 1)
                    link(dve.tensor_scalar(minus_sine[:, :], sine[:, :], -1.0, None, ALU.mult))
                    lanes = lambda ap: ap.rearrange("p (n f) -> p n f", f=4)
                    for b in range(B):
                        for lane in range(4):
                            col = 16 + B * (lane // 2) + b
                            cos = cosine[:, col:col + 1]
                            sin = (sine if lane % 2 == 0 else minus_sine)[:, col:col + 1]
                            own_g, other_g = lanes(gamma[:, :])[:, :, lane], lanes(gamma[:, :])[:, :, lane ^ 1]
                            own_b, other_b = lanes(beta[:, :])[:, :, lane], lanes(beta[:, :])[:, :, lane ^ 1]
                            link(dve.tensor_scalar(lanes(self.rot_own[:, b, :])[:, :, lane], own_g, cos, None, ALU.mult))
                            link(dve.tensor_scalar(lanes(self.rot_other[:, b, :])[:, :, lane], other_g, sin, None,
                                                   ALU.mult))
                            target = lanes(self.rot_beta[:, b, :])[:, :, lane]
                            link(dve.tensor_scalar(target, own_b, cos, None, ALU.mult))
                            link(dve.scalar_tensor_tensor(out=target, in0=other_b, scalar=sin, in1=target,
                                                          op0=ALU.mult, op1=ALU.add))
                    for b in range(B):
                        dve.wait_ge(ada_done, b + 1)
                        banks = 2 * (b % 2)
                        link(dve.scalar_tensor_tensor(out=self.scale1[:, b, :], in0=psum[:, banks, :], scalar=1.0,
                                                      in1=b_ada[:, 0:D], op0=ALU.add, op1=ALU.add))
                        link(dve.tensor_tensor(self.shift[:, b, :], psum[:, banks + 1, :], b_ada[:, D:2 * D], ALU.add))
                        dve.sem_inc(ada_used, 1)

                @block.scalar
                def _(act):
                    act.wait_ge(reduced_done, 1)
                    act.activation(sine[:, :], reduced[:, :], ACT.Sin).then_inc(sines_done, 1)
                    act.activation(cosine[:, :], flipped[:, :], ACT.Sin).then_inc(sines_done, 1)
                    act.wait_ge(emb_ready, 1)
                    act.activation(emb_act[:, :, :], emb[:, :, :], ACT.Silu).then_inc(sines_done, 1)

                @block.tensor
                def _(pe):
                    pe.wait_ge(loaded, DMA * len(loads))
                    for b in range(B):
                        pe.wait_ge(spread_done, 4 * (b + 1))
                        need(pe, ada_used, b - 1)
                        for half in range(2):
                            for c in range(DC):
                                mm = pe.matmul(psum[:, 2 * (b % 2) + half, :], spread[:, b, c, :],
                                               w_ada[:, c, D * half:D * (half + 1)], start=c == 0, stop=c == DC - 1)
                        mm.then_inc(ada_done, 1)


    def split_weights(self, memory, name, matrices):
        nc = self.nc
        width = 2048
        pieces = []
        for src, high, low, scale in matrices:
            n = high.shape[1]
            for at in range(0, n, width):
                to = min(at + width, n)
                pieces.append((src, at, to, high, low, scale))
        loaded, scaled, rounded, split = self.weight_sems
        done, scales, loads = self.weights_done
        self.weights_done = (done + len(pieces), scales + sum(p[5] != 1.0 for p in pieces),
                             [loads[i] + len(pieces[i::2]) for i in range(2)])
        with ExitStack() as own:
            stage = own.enter_context(nc.sbuf_tensor(f"{name}_stage", [P, 2, width], F32))
            with nc.Block() as block:

                @block.sync
                def _(sp):
                    for i, (src, at, to, *_) in enumerate(pieces):
                        if i >= 2:
                            sp.wait_ge(split, done + i - 1)
                        piece, what = stage[:, i % 2, 0:to - at], src(at, to)
                        if len(what.shape) == 3:
                            piece = piece.rearrange("p (c n) -> p c n", c=what.shape[1])
                        sp.dma_start(piece, what).then_inc(loaded[i % 2], DMA)

                @block.scalar
                def _(act):
                    for i, (_, at, to, high, _, scale) in enumerate(pieces):
                        piece = stage[:, i % 2, 0:to - at]
                        act.wait_ge(loaded[i % 2], DMA * (loads[i % 2] + i // 2 + 1))
                        if scale != 1.0:
                            act.activation(piece, piece, ACT.Copy, scale=scale).then_inc(scaled, 1)
                            act.wait_ge(scaled, scales + 1 + sum(p[5] != 1.0 for p in pieces[:i]))
                        act.activation(high[:, at:to], piece, ACT.Copy).then_inc(rounded, 1)

                @block.vector
                def _(dve):
                    for i, (_, at, to, high, low, _) in enumerate(pieces):
                        dve.wait_ge(rounded, done + i + 1)
                        dve.tensor_tensor(low[:, at:to], stage[:, i % 2, 0:to - at], high[:, at:to].bitcast(F32),
                                          ALU.subtract).then_inc(split, 1)


    def attention(self, memory, layer):
        nc, psum, ident, ident16 = self.nc, self.psum, self.ident, self.ident16
        causal = layer == 1
        qk, v_dram, attended = self.qk[layer], self.v[layer], self.attended[layer]
        U = 8 * QP
        keys = lambda u: 2 * (u // 8 + 1) if causal else KT
        halves = lambda u: (keys(u) + 3) // 4
        by_dve = lambda u, half: half == 1 or causal and (u < 8 or u < 16 and u % 2 == 1)
        copies = lambda u, dve: sum(by_dve(x, half) == dve for x in range(u) for half in range(halves(x)))
        sb = lambda name, shape, dt=F32: memory.enter_context(nc.sbuf_tensor(f"{name}{layer}", shape, dt))
        q_stack = sb("q_stack", [P, HG, S], F32R)
        k_stack = sb("k_stack", [P, HG, S], F32R)
        values = sb("values", [P, KT, P])
        shifted = sb("shifted", [P, 2, S])
        least = sb("least", [P, 8])
        weights = sb("weights", [P, 2, S])
        total = sb("total", [P, 8])
        inverse = sb("inverse", [P, 8])
        normal = sb("normal", [P, 2, S])
        turned = sb("turned", [P, 2, HG, KT, 256])
        result = sb("result", [P, 2, 256])
        if causal:
            ahead = sb("ahead", [P, S + P])
        else:
            NBIAS = 4
            bias = sb("bias", [P, NBIAS, S])
            mask_u8 = sb("mask_u8", [P, KT, S], U8)
            mask = sb("mask", [P, KT, S], BF16)

        sem = lambda name: self.sem(f"{name}{layer}")
        qk_in = [sem(f"qk_in{j}") for j in range(HG)]
        values_in = sem("values_in")
        bias_in = [sem(f"bias_in{i}") for i in range(4)] if not causal else None
        mask_in, mask_made = sem("mask_in"), sem("mask_made")
        scored = sem("scored")
        biased = sem("biased")
        exped = sem("exped")
        inverted = sem("inverted")
        normed = sem("normed")
        transposed = sem("transposed")
        act_out = sem("act_out")
        dve_out = sem("dve_out")
        weighted = sem("weighted")
        result_out = sem("result_out")
        stored = [sem(f"attended_stored{i}") for i in range(2)]
        QK_DMAS = 8
        PIECES = 4
        SCORES = (0, 2)
        TURN = (4, 5)
        WEIGHT = (6, 7)

        def ahead_of(it, u, by):
            over, u2 = divmod(u + by, U)
            it2 = it + over
            return it2, u2, it2 * U + u2

        def copied(it, u, dve):
            return it * copies(U, dve) + copies(u, dve)

        def transposes_before(it, u):
            return copied(it, u, True) + copied(it, u, False)

        def turns(body):
            def run(eng):
                body(eng, 0, True, False)
                with eng.Fori(1, NBG - 1) as it:
                    body(eng, it, False, False)
                body(eng, NBG - 1, False, True)
            return run

        with nc.Block() as block:

            @block.sync
            def _(sp):
                def load_head(it, j):
                    for group in range(4):
                        part = slice(DH * group, DH * (group + 1))
                        rows = bass.ds(it * P + DH * j, DH)
                        q = qk["qh" if group < 2 else "ql"]
                        k = qk["kh" if group % 2 == 0 else "kl"]
                        sp.dma_start(q_stack[part, j, :].bitcast(F32), q[rows, :]).then_inc(qk_in[j], DMA)
                        sp.dma_start(k_stack[part, j, :].bitcast(F32), k[rows, :]).then_inc(qk_in[j], DMA)

                def load_values(it):
                    sp.dma_start(values[:, :, :],
                                 v_dram[it].rearrange("(k p) f -> p k f", p=P)).then_inc(values_in, DMA)

                def load_bias(it, u, number):
                    if causal:
                        return
                    need(sp, biased, number - 3)
                    tile = 2 * (u // 8) + u % 2
                    head = 4 * it + (u % 8) // 2
                    sp.dma_start(bias[:, u % 4, :], self.ins["bias"][head, P * tile:P * (tile + 1), :]
                                 ).then_inc(bias_in[u % 4], DMA)

                def load_mask(it):
                    sp.dma_start(mask_u8[:, :, :].bitcast(I32), self.ins["mask"][it // G].rearrange("(t p) k -> p t k", p=P)
                                 ).then_inc(mask_in, DMA)

                def store(it, pair):
                    number = it * QP + pair
                    sp.wait_ge(result_out, number + 1)
                    sp.dma_start(attended[bass.ds(it * P, P), 256 * pair:256 * (pair + 1)],
                                 result[:, pair % 2, :]).then_inc(stored[pair % 2], DMA)

                def body(sp, it, first, last):
                    for u in range(U):
                        if not (first and u == 0):
                            load_bias(it, u, it * U + u)
                        if u in (29, 31) and not last:
                            j = (u - 29) // 2
                            sp.wait_ge(scored, it * U + 24 + 2 * j + 2)
                            load_head(it + 1, j)
                        if u in (1, 3) and not first:
                            j = 2 + (u - 1) // 2
                            sp.wait_ge(scored, (it - 1) * U + 24 + 2 * j + 2)
                            load_head(it, j)
                        if u == 12 and not first:
                            sp.wait_ge(weighted, it * QP)
                            load_values(it)
                        if u == 8 and not causal and not last:
                            sp.wait_ge(mask_made, KT * (it + 1))
                            load_mask(it + 1)
                        if u % 8 == 5:
                            pair = u // 8 - 2
                            if pair >= 0:
                                store(it, pair)
                            elif not first:
                                store(it - 1, pair + QP)

                if not causal:
                    load_mask(0)
                load_head(0, 0)
                load_bias(0, 0, 0)
                for j in range(1, HG):
                    load_head(0, j)
                load_values(0)
                turns(body)(sp)
                store(NBG - 1, QP - 2)
                store(NBG - 1, QP - 1)
                for i in range(2):
                    sp.wait_ge(stored[i], DMA * NBG * QP // 2)

            @block.tensor
            def _(pe):
                def scores(it, u, number):
                    pair, j, half = u // 8, (u % 8) // 2, u % 2
                    tile, n = 2 * pair + half, keys(u) * P
                    if pair == 0 and half == 0:
                        pe.wait_ge(qk_in[j], DMA * QK_DMAS * (it + 1))
                    need(pe, biased, number - 1)
                    if not causal and j == 0:
                        pe.wait_ge(mask_made, it * KT + tile + 1)
                    bank = SCORES[half]
                    spans = [(at, min(at + 512, n)) for at in range(0, n, 512)]
                    if not causal:
                        for i, (at, to) in enumerate(spans):
                            pe.matmul(psum[:, bank + i, 0:to - at], ident16[:, :], mask[:, tile, at:to], start=True,
                                      stop=False)
                    for i, (at, to) in enumerate(spans):
                        mm = pe.matmul(psum[:, bank + i, 0:to - at], q_stack[:, j, P * tile:P * (tile + 1)],
                                       k_stack[:, j, at:to], start=causal, stop=True)
                    mm.then_inc(scored, 1)

                def transpose(it, u, number):
                    pe.wait_ge(normed, number + 1)
                    for half in range(halves(u)):
                        before = (u - 1) % U
                        while halves(before) <= half:
                            before = (before - 1) % U
                        dve = by_dve(before, half)
                        need(pe, dve_out if dve else act_out, copied(it, u, dve))
                        tiles = range(4 * half, min(4 * half + 4, keys(u)))
                        for k in tiles:
                            at = P * (k - tiles[0])
                            mm = pe.transpose(psum[:, TURN[half], at:at + P], normal[:, u % 2, P * k:P * (k + 1)],
                                              ident[:, :])
                        mm.then_inc(transposed, 1)

                def weigh(it, pair, piece):
                    number = it * QP + pair
                    last = 8 * pair + 7
                    n = keys(last)
                    if piece == 0:
                        need(pe, act_out, copied(it, last + 1, False))
                        need(pe, dve_out, copied(it, last + 1, True))
                        if pair == 0:
                            pe.wait_ge(values_in, DMA * (it + 1))
                        need(pe, result_out, number - 1)
                    span = range(n * piece // PIECES, n * (piece + 1) // PIECES)
                    for k in span:
                        for j in range(HG):
                            mm = pe.matmul(psum[DH * j:DH * (j + 1), WEIGHT[pair % 2], 0:256],
                                           values[:, k, DH * j:DH * (j + 1)], turned[:, pair % 2, j, k, :],
                                           start=k == 0, stop=k == n - 1,
                                           tile_position=(0, DH * j))
                    if piece == PIECES - 1:
                        mm.then_inc(weighted, 1)

                def body(pe, it, first, last):
                    for u in range(U):
                        transpose(it, u, it * U + u)
                        if not (last and u + 4 >= U):
                            scores(*ahead_of(it, u, 4))
                        if u % 8 < PIECES:
                            if u >= 8:
                                weigh(it, u // 8 - 1, u % 8)
                            elif not first:
                                weigh(it - 1, QP - 1, u % 8)

                for u in range(4):
                    scores(0, u, u)
                turns(body)(pe)
                for piece in range(PIECES):
                    weigh(NBG - 1, QP - 1, piece)

            @block.vector
            def _(dve):
                def add_bias(it, u, number):
                    n = keys(u) * P
                    dve.wait_ge(scored, number + 1)
                    need(dve, exped, number - 1)
                    if causal:
                        end = S if u % 2 else S + P
                        what = ahead[:, end - n:end]
                    else:
                        dve.wait_ge(bias_in[u % 4], DMA * (it * (U // 4) + u // 4 + 1))
                        what = bias[:, u % 4, 0:n]
                    bank = SCORES[u % 2]
                    apart(dve)
                    dve.tensor_tensor_reduce(
                        out=shifted[:, u % 2, 0:n], in0=psum[:, bank:bank + 2, :].rearrange("p b n -> p (b n)")[:, 0:n],
                        in1=what, scale=-1.0, scalar=3e38, op0=ALU.add, op1=ALU.min,
                        accum_out=least[:, u % 8:u % 8 + 1]).then_inc(biased, 1)

                def copy_transposed(it, u, number):
                    pair, j = u // 8, (u % 8) // 2
                    for half in range(halves(u)):
                        if not by_dve(u, half):
                            continue
                        dve.wait_ge(transposed, transposes_before(it, u) + half + 1)
                        need(dve, weighted, it * QP + pair - 1)
                        n = min(keys(u) - 4 * half, 4)
                        dve.tensor_copy(turned[:, pair % 2, j, 4 * half:4 * half + n, P * (u % 2):P * (u % 2 + 1)],
                                        psum[:, TURN[half], 0:P * n].rearrange("p (k q) -> p k q", k=n)
                                        ).then_inc(dve_out, 1)

                def invert(it, u, number):
                    dve.wait_ge(exped, number + 1)
                    dve.reciprocal(inverse[:, u % 8:u % 8 + 1], total[:, u % 8:u % 8 + 1]).then_inc(inverted, 1)

                def body(dve, it, first, last):
                    for u in range(U):
                        if not (last and u + 3 >= U):
                            add_bias(*ahead_of(it, u, 3))
                        copy_transposed(it, u, it * U + u)
                        if not (last and u + 2 >= U):
                            invert(*ahead_of(it, u, 2))

                if causal:
                    dve.wait_ge(mask_made, 2)
                for u in range(3):
                    add_bias(0, u, u)
                for u in range(2):
                    invert(0, u, u)
                turns(body)(dve)

            @block.scalar
            def _(act):
                def exponentiate(it, u, number):
                    n = keys(u) * P
                    act.wait_ge(biased, number + 1)
                    need(act, normed, number - 1)
                    act.activation(weights[:, u % 2, 0:n], shifted[:, u % 2, 0:n], ACT.Exp,
                                   bias=least[:, u % 8:u % 8 + 1], scale=-1.0,
                                   accum_out=total[:, u % 8:u % 8 + 1]).then_inc(exped, 1)

                def copy_transposed(it, u, number):
                    if by_dve(u, 0):
                        return
                    pair, j, half = u // 8, (u % 8) // 2, u % 2
                    act.wait_ge(transposed, transposes_before(it, u) + 1)
                    need(act, weighted, it * QP + pair - 1)
                    n = min(keys(u), 4)
                    act.activation(turned[:, pair % 2, j, 0:n, P * half:P * (half + 1)],
                                   psum[:, TURN[0], 0:P * n].rearrange("p (k q) -> p k q", k=n),
                                   ACT.Copy).then_inc(act_out, 1)

                def take_result(it, pair):
                    number = it * QP + pair
                    act.wait_ge(weighted, number + 1)
                    need(act, stored[pair % 2], DMA * (it * (QP // 2) + pair // 2))
                    act.activation(result[:, pair % 2, :], psum[:, WEIGHT[pair % 2], 0:256],
                                   ACT.Copy).then_inc(result_out, 1)

                def body(act, it, first, last):
                    for u in range(U):
                        if not (last and u + 2 >= U):
                            exponentiate(*ahead_of(it, u, 2))
                        copy_transposed(it, u, it * U + u)
                        if u % 8 == PIECES:
                            if u >= 8:
                                take_result(it, u // 8 - 1)
                            elif not first:
                                take_result(it - 1, QP - 1)

                for u in range(2):
                    exponentiate(0, u, u)
                turns(body)(act)
                take_result(NBG - 1, QP - 1)

            @block.gpsimd
            def _(pool):
                def normalise(it, u, number):
                    n = keys(u) * P
                    pool.wait_ge(inverted, number + 1)
                    _, u0, _ = ahead_of(0, u, -2)
                    before = transposes_before(it + (u - 2) // U, u0) + halves(u0)
                    need(pool, transposed, before)
                    apart(pool)
                    pool.tensor_scalar(normal[:, u % 2, 0:n], weights[:, u % 2, 0:n], inverse[:, u % 8:u % 8 + 1],
                                       1.0, ALU.mult, ALU.mult).then_inc(normed, 1)

                def make_mask(it, tile):
                    if tile == 0:
                        pool.wait_ge(mask_in, DMA * (it + 1))
                    apart(pool)
                    pool.tensor_scalar(mask[:, tile, :], mask_u8[:, tile, :], MASKED, 1.0, ALU.mult,
                                       ALU.mult).then_inc(mask_made, 1)

                def body(pool, it, first, last):
                    for u in range(U):
                        if not (last and u + 1 >= U):
                            normalise(*ahead_of(it, u, 1))
                        if u % 8 >= 6 and not causal and not last:
                            pool.wait_ge(scored, it * U + u + 1)
                            make_mask(it + 1, 2 * (u // 8) + u % 2)

                if causal:
                    pool.memset(ahead[:, :], 0.0).then_inc(mask_in, 1)
                    pool.wait_ge(mask_in, 1)
                    pool.affine_select(out=ahead[:, S - P:S + P], in_=ahead[:, S - P:S + P], compare_op=ALU.is_ge,
                                       fill=MASKED, base=0, pattern=[[-1, 2 * P]],
                                       channel_multiplier=1).then_inc(mask_made, 2)
                else:
                    for tile in range(KT):
                        make_mask(0, tile)
                normalise(0, 0, 0)
                turns(body)(pool)


    def projection(self, memory, layer):
        psum = self.psum
        sb = lambda name, shape, dt=F32: memory.enter_context(self.nc.sbuf_tensor(f"{name}{layer}", shape, dt))
        sem = lambda name: self.sem(f"{name}{layer}")
        w = {}
        for name in "qkv":
            w[name] = (sb(f"w{name}_h", [P, DC * D], F32R), sb(f"w{name}_l", [P, DC * D], F32R))
        xt = [(sb(f"xt_h_{i}_", [P, DC, TB], F32R), sb(f"xt_l_{i}_", [P, DC, TB], F32R)) for i in range(2)]
        qk_bias = sb("qk_bias", [P, 2 * DC])
        v_bias = sb("v_bias", [P, D])
        out_h = sb("out_h", [P, 2, TB], F32)
        out_l = sb("out_l", [P, 2, TB], F32)
        out_v = sb("out_v", [P, 2, D], F32)
        projected = sem("projected")
        high_out = sem("high_out")
        taken = sem("taken")
        qk_stored = [sem(f"qk_stored{i}") for i in range(2)]
        v_stored = [sem(f"v_stored{i}") for i in range(2)]
        xt_low = sem("xt_low")
        BANKS = (6, 7)
        qk, v = self.qk[layer], self.v[layer]

        class Pieces:
            pass

        def pe(pe, n, half, i):
            if i == 0:
                pe.wait_ge(xt_low, DC * (n + 1))
            need(pe, taken, 12 * n + i - 1)
            out = psum[:, BANKS[i % 2], :]
            h, l = xt[half]
            for c in range(DC):
                if i < 8:
                    wh, wl = w["qk"[i // 4]]
                    at = slice(D * c + P * (i % 4), D * c + P * (i % 4) + P)
                    mm = product(pe, out, (wh[:, at], wl[:, at]), (h[:, c, :], l[:, c, :]), c == 0, c == DC - 1)
                else:
                    wh, wl = w["v"]
                    at, row = slice(P * (i - 8), P * (i - 7)), slice(D * c, D * (c + 1))
                    mm = product(pe, out, (h[:, c, at], l[:, c, at]), (wh[:, row], wl[:, row]), c == 0, c == DC - 1)
            mm.then_inc(projected, 1)

        def act(act, n, half, i):
            if i >= 8:
                return
            act.wait_ge(projected, 12 * n + i + 1)
            need(act, qk_stored[i % 2], 2 * DMA * (4 * n + i // 2))
            act.activation(out_h[:, i % 2, :].bitcast(F32R), psum[:, BANKS[i % 2], :], ACT.Identity,
                           bias=qk_bias[:, i:i + 1]).then_inc(high_out, 1)

        def dve(dve, n, half, i):
            bank = psum[:, BANKS[i % 2], :]
            if i < 8:
                dve.wait_ge(high_out, 8 * n + i + 1)
                dve.scalar_tensor_tensor(out=out_l[:, i % 2, :], in0=bank, scalar=qk_bias[:, i:i + 1],
                                         in1=out_h[:, i % 2, :], op0=ALU.add, op1=ALU.subtract).then_inc(taken, 1)
            else:
                dve.wait_ge(projected, 12 * n + i + 1)
                need(dve, v_stored[i % 2], DMA * (2 * n + (i - 8) // 2))
                dve.tensor_tensor(out_v[:, i % 2, :], bank, v_bias[:, :], ALU.add).then_inc(taken, 1)

        def sp(sp, n, b, half, i):
            sp.wait_ge(taken, 12 * n + i + 1)
            if i < 8:
                rows = bass.ds(b * D + P * (i % 4), P)
                for part, src in (("h", out_h), ("l", out_l)):
                    sp.dma_start(qk["qk"[i // 4] + part][rows, TB * half:TB * (half + 1)],
                                 src[:, i % 2, :]).then_inc(qk_stored[i % 2], DMA)
            else:
                at = TB * half + P * (i - 8)
                sp.dma_start(v[bass.ds(b * G, G), at:at + P, :].rearrange("g p d -> p g d"),
                             out_v[:, i % 2, :].rearrange("p (g d) -> p g d", g=G)).then_inc(v_stored[i % 2], DMA)

        def sp_end(sp):
            for i in range(2):
                sp.wait_ge(qk_stored[i], 2 * DMA * 4 * NB)
                sp.wait_ge(v_stored[i], DMA * 2 * NB)

        pieces = Pieces()
        pieces.pe, pieces.act, pieces.dve, pieces.sp, pieces.sp_end = pe, act, dve, sp, sp_end
        pieces.xt, pieces.xt_low, pieces.projected = xt, xt_low, projected
        pieces.bias_scaled = sem("bias_scaled")
        pieces.w, pieces.qk_bias, pieces.v_bias = w, qk_bias, v_bias
        return pieces

    def projection_weights(self, memory, name, prefix, proj, more=()):
        matrices = list(more)
        for which in "qkv":
            src = self.ins[f"{prefix}W{which}"].rearrange("(c p) n -> c p n", p=P)
            high, low = proj.w[which]
            matrices.append(((lambda at, to, src=src: src[at // D:to // D].rearrange("c p n -> p c n")),
                             high, low, 1 / math.sqrt(DH) if which == "q" else 1.0))
        self.split_weights(memory, name, matrices)


    def front(self, memory):
        nc, ins, psum, ident = self.nc, self.ins, self.psum, self.ident
        sb = lambda name, shape, dt=F32: memory.enter_context(nc.sbuf_tensor(name, shape, dt))
        sem = self.sem
        proj = self.projection(memory, 0)
        down = (sb("down_h", [P, DC * A], F32R), sb("down_l", [P, DC * A], F32R))
        up = (sb("up_h", [P, D], F32R), sb("up_l", [P, D], F32R))
        down_src = ins["L0_down_WT"].rearrange("(c p) a -> p c a", p=P)
        self.projection_weights(memory, "front", "L2_", proj, [
            ((lambda at, to: down_src), *down, 1.0), ((lambda at, to: ins["L0_up_WT"]), *up, 1.0)])
        x_t = sb("x_t", [P, DC, TB])
        x_th, x_tl = sb("x_th", [P, DC, TB], F32R), sb("x_tl", [P, DC, TB], F32R)
        x_rows = sb("x_rows", [P, TT, D])
        y = sb("y", [P, TT, D])
        hidden = sb("hidden", [P, TB])
        hidden_h, hidden_l = sb("hidden_h", [P, TB], F32R), sb("hidden_l", [P, TB], F32R)
        mixed_h, mixed_l = sb("mixed_h", [P, TB], F32R), sb("mixed_l", [P, TB], F32R)
        expert = (sb("expert_now_h", [P, A], F32R), sb("expert_now_l", [P, A], F32R))
        scratch = sb("front_scratch", [P, 2, D])
        down_b, up_b = sb("down_b", [P, 1]), sb("up_b", [P, D])
        stats = sb("front_stats", [P, TT, 6])
        moments = sb("front_moments", [P, 2, TT, 2])
        deviation = sb("front_deviation", [P, 2, TT])
        rstd = sb("front_rstd", [P, 2, TT])

        biases_in = sem("front_biases_in")
        x_t_in, rows_in = sem("x_t_in"), sem("x_rows_in")
        x_high, x_low = sem("x_high"), sem("x_low")
        rows_biased = sem("rows_biased")
        down_done, hidden_made = sem("down_done"), sem("hidden_made")
        hidden_high, hidden_low = sem("hidden_high"), sem("hidden_low")
        expert_staged, expert_done = sem("expert_staged"), sem("expert_done")
        mixed_high, mixed_low = sem("mixed_high"), sem("mixed_low")
        up_done, up_taken = sem("up_done"), sem("up_taken")
        variance_ready, deviation_ready = sem("variance_ready"), sem("deviation_ready")
        vec = sem("front_vector")
        LINKS = 2 * 2 * TT + 2 + 5 * TT + TT
        rows_ready = sem("front_rows_ready")
        rows_stored = sem("front_rows_stored")
        turned, xt_high = sem("front_turned"), sem("front_xt_high")
        xt_low = proj.xt_low

        with nc.Block() as block:

            def schedule(eng, front, project):
                front(eng, 0, 0, 0, lambda i: None)

                def body(eng, i):
                    for half in range(BPS):
                        n = i * BPS + half
                        b, half2 = (i, half + 1) if half + 1 < BPS else (i + 1, 0)
                        front(eng, n + 1, b, half2, lambda k: project(eng, n, i, half, k))
                body(eng, 0)
                with eng.Fori(1, B - 1) as i:
                    body(eng, i)
                i, n = B - 1, (B - 1) * BPS
                front(eng, n + 1, i, 1, lambda k: project(eng, n, i, 0, k))
                for k in range(12):
                    project(eng, n + 1, i, 1, k)

            @block.sync
            def _(sp):
                sp.dma_start(down_b[:, :], ins["L0_down_b"]).then_inc(biases_in, DMA)
                sp.dma_start(up_b[:, :], ins["L0_up_b"].partition_broadcast(P)).then_inc(biases_in, DMA)
                sp.dma_start(proj.qk_bias[:, 0:DC], ins["L2_bq"]).then_inc(biases_in, DMA)
                sp.dma_start(proj.qk_bias[:, DC:2 * DC], ins["L2_bk"]).then_inc(biases_in, DMA)
                sp.dma_start(proj.v_bias[:, :], ins["L2_bv"].partition_broadcast(P)).then_inc(biases_in, DMA)

                def load_transposed(sp, n):
                    tokens = bass.ds(n * TB, TB)
                    need(sp, x_low, n)
                    sp.dma_start(x_t[:, :, :], ins["x_T"].rearrange("(c p) t -> p c t", p=P)[:, :, tokens]
                                 ).then_inc(x_t_in, DMA)

                def load_rows(sp, n):
                    tokens = bass.ds(n * TB, TB)
                    need(sp, up_taken, n * TT)
                    sp.dma_start(x_rows[:, :, :], ins["x"][tokens, :].rearrange("(t p) d -> p t d", p=P)
                                 ).then_inc(rows_in, DMA)

                def front(sp, n, b, half, project):
                    more = not (isinstance(n, int) and n == NB - 1)
                    for k in range(10):
                        project(k)
                        if k == 1 and more:
                            load_transposed(sp, n + 1)
                        if k == 6 and more:
                            load_rows(sp, n + 1)
                    for t in range(TT):
                        sp.wait_ge(rows_ready, n * TT + t + 1)
                        sp.dma_start(self.rows[0][bass.ds(n * TB + t * P, P), :], y[:, t, :]).then_inc(rows_stored, DMA)
                        if t < 2:
                            project(10 + t)

                load_transposed(sp, 0)
                load_rows(sp, 0)
                schedule(sp, front, proj.sp)
                proj.sp_end(sp)
                sp.wait_ge(rows_stored, DMA * TT * NB)

            @block.tensor
            def _(pe):
                def front(pe, n, b, half, project):
                    pe.wait_ge(x_low, n + 1)
                    need(pe, hidden_made, n)
                    for c in range(DC):
                        at = slice(A * c, A * (c + 1))
                        mm = product(pe, psum[:, 0, :], (down[0][:, at], down[1][:, at]), (x_th[:, c, :], x_tl[:, c, :]),
                                     c == 0, c == DC - 1)
                    mm.then_inc(down_done, 1)
                    project(0)
                    project(1)
                    pe.wait_ge(hidden_low, n + 1)
                    pe.wait_ge(expert_staged, 2 * (n + 1))
                    need(pe, mixed_low, n)
                    product(pe, psum[:, 1, :], (expert[0][:, :], expert[1][:, :]), (hidden_h[:, :], hidden_l[:, :]),
                            True, True).then_inc(expert_done, 1)
                    project(2)
                    pe.wait_ge(mixed_low, n + 1)
                    for t in range(TT):
                        need(pe, up_taken, n * TT + t - 1)
                        at = slice(P * t, P * (t + 1))
                        product(pe, psum[:, 2 + t % 2, :], (mixed_h[:, at], mixed_l[:, at]), (up[0][:, :], up[1][:, :]),
                                True, True).then_inc(up_done, 1)
                        if t == 1:
                            project(3)
                    for k in range(4, 12):
                        project(k)
                    pe.wait_ge(rows_ready, TT * (n + 1))
                    for c in range(DC):
                        need(pe, xt_low, n * DC + c - 1)
                        for t in range(TT):
                            mm = pe.transpose(psum[:, 4 + c % 2, P * t:P * (t + 1)], y[:, t, P * c:P * (c + 1)],
                                              ident[:, :])
                        mm.then_inc(turned, 1)

                schedule(pe, front, lambda pe, n, b, half, k: proj.pe(pe, n, half, k))

            @block.scalar
            def _(act):
                def front(act, n, b, half, project):
                    act.wait_ge(x_t_in, DMA * (n + 1))
                    need(act, down_done, n)
                    act.activation(x_th[:, :, :], x_t[:, :, :], ACT.Copy).then_inc(x_high, 1)
                    act.wait_ge(down_done, n + 1)
                    need(act, hidden_low, n)
                    act.activation(hidden[:, :], psum[:, 0, :], ACT.Gelu, bias=down_b[:, 0:1]).then_inc(hidden_made, 1)
                    act.wait_ge(hidden_made, n + 1)
                    need(act, expert_done, n)
                    act.activation(hidden_h[:, :], hidden[:, :], ACT.Copy).then_inc(hidden_high, 1)
                    project(0)
                    project(1)
                    act.wait_ge(expert_done, n + 1)
                    need(act, up_done, n * TT)
                    act.activation(mixed_h[:, :], psum[:, 1, :], ACT.Identity,
                                   bias=self.expert_bias[:, bass.ds(b, 1)]).then_inc(mixed_high, 1)
                    for k in range(2, 5):
                        project(k)
                    for i in range(2):
                        act.wait_ge(variance_ready, 2 * n + i + 1)
                        act.activation(deviation[:, i, :], deviation[:, i, :], ACT.Sqrt).then_inc(deviation_ready, 1)
                        if i == 0:
                            for k in range(5, 8):
                                project(k)
                    for c in range(DC):
                        act.wait_ge(turned, n * DC + c + 1)
                        if c == 0:
                            need(act, proj.projected, 12 * (n - 1))
                        act.activation(proj.xt[half][0][:, c, :], psum[:, 4 + c % 2, :], ACT.Copy).then_inc(xt_high, 1)

                act.wait_ge(biases_in, DMA * 5)
                act.wait_ge(proj.bias_scaled, 1)
                schedule(act, front, lambda act, n, b, half, k: proj.act(act, n, half, k))

            @block.gpsimd
            def _(pool):
                def front(pool, n, b, half, project):
                    pool.wait_ge(x_high, n + 1)
                    need(pool, down_done, n)
                    pool.tensor_tensor(x_tl[:, :, :], x_t[:, :, :], x_th[:, :, :].bitcast(F32), ALU.subtract
                                       ).then_inc(x_low, 1)
                    need(pool, expert_done, n)
                    pool.tensor_copy(expert[0][:, :], self.expert_h[:, b, :].bitcast(F32)).then_inc(expert_staged, 1)
                    pool.tensor_copy(expert[1][:, :], self.expert_l[:, b, :].bitcast(F32)).then_inc(expert_staged, 1)
                    pool.wait_ge(rows_in, DMA * (n + 1))
                    for t in range(TT):
                        pool.tensor_tensor(x_rows[:, t, :], x_rows[:, t, :], up_b[:, :], ALU.add
                                           ).then_inc(rows_biased, 1)

                pool.wait_ge(biases_in, DMA * 5)
                schedule(pool, front, lambda *a: None)

            @block.vector
            def _(dve):
                def front(dve, n, b, half, project):
                    chain = Chain(dve, vec, n * LINKS)
                    link = chain.link

                    def moments_of(i, t):
                        link(dve.bn_stats(stats[:, t, :], y[:, t, :]))
                        apart(dve)
                        link(dve.bn_aggr(moments[:, i, t, :], stats[:, t, :]))

                    def variance(i):
                        dve.tensor_scalar(deviation[:, i, :], moments[:, i, :, 1], EPS, None, ALU.add
                                          ).then_inc(variance_ready, 1)

                    def inverse_deviation(i):
                        dve.wait_ge(deviation_ready, 2 * n + i + 1)
                        link(dve.reciprocal(rstd[:, i, :], deviation[:, i, :]))

                    dve.wait_ge(hidden_high, n + 1)
                    dve.tensor_tensor(hidden_l[:, :], hidden[:, :], hidden_h[:, :].bitcast(F32), ALU.subtract
                                      ).then_inc(hidden_low, 1)
                    project(0)
                    project(1)
                    dve.wait_ge(mixed_high, n + 1)
                    dve.scalar_tensor_tensor(out=mixed_l[:, :], in0=psum[:, 1, :],
                                             scalar=self.expert_bias[:, bass.ds(b, 1)], in1=mixed_h[:, :].bitcast(F32),
                                             op0=ALU.add, op1=ALU.subtract).then_inc(mixed_low, 1)
                    project(2)
                    need(dve, turned, n * DC)
                    need(dve, rows_stored, DMA * TT * n)
                    for t in range(TT):
                        dve.wait_ge(up_done, n * TT + t + 1)
                        dve.wait_ge(rows_biased, n * TT + t + 1)
                        dve.tensor_tensor(y[:, t, :], psum[:, 2 + t % 2, :], x_rows[:, t, :], ALU.add
                                          ).then_inc(up_taken, 1)
                        dve.wait_ge(up_taken, n * TT + t + 1)
                        moments_of(0, t)
                        if t in (1, 3):
                            project(3 + t // 2)
                    variance(0)
                    project(5)
                    inverse_deviation(0)
                    for t in range(TT):
                        mean = moments[:, 0, t, 0:1]
                        own, other = scratch[:, 0, :], scratch[:, 1, :]
                        pairs = lambda ap: ap.rearrange("p (n two) -> p n two", two=2)
                        dve.scalar_tensor_tensor(out=own, in0=y[:, t, :], scalar=mean, in1=self.rot_own[:, b, :],
                                                 op0=ALU.subtract, op1=ALU.mult).then_inc(vec, 1)
                        chain.count += 1
                        for lane in range(2):
                            dve.scalar_tensor_tensor(out=pairs(other)[:, :, lane], in0=pairs(y[:, t, :])[:, :, 1 - lane],
                                                     scalar=mean, in1=pairs(self.rot_other[:, b, :])[:, :, lane],
                                                     op0=ALU.subtract, op1=ALU.mult).then_inc(vec, 1)
                            chain.count += 1
                        chain.wait()
                        link(dve.tensor_tensor(own, own, other, ALU.add))
                        link(dve.scalar_tensor_tensor(out=y[:, t, :], in0=own, scalar=rstd[:, 0, t:t + 1],
                                                      in1=self.rot_beta[:, b, :], op0=ALU.mult, op1=ALU.add))
                        moments_of(1, t)
                        if t < 3:
                            project(6 + t)
                    variance(1)
                    project(9)
                    inverse_deviation(1)
                    for t in range(TT):
                        shifted = scratch[:, t % 2, :]
                        link(dve.scalar_tensor_tensor(out=shifted, in0=y[:, t, :], scalar=moments[:, 1, t, 0:1],
                                                      in1=self.scale1[:, b, :], op0=ALU.subtract, op1=ALU.mult))
                        dve.scalar_tensor_tensor(out=y[:, t, :], in0=shifted, scalar=rstd[:, 1, t:t + 1],
                                                 in1=self.shift[:, b, :], op0=ALU.mult, op1=ALU.add
                                                 ).then_inc(rows_ready, 1)
                        if t < 2:
                            project(10 + t)
                    for c in range(DC):
                        dve.wait_ge(xt_high, n * DC + c + 1)
                        dve.tensor_tensor(proj.xt[half][1][:, c, :], psum[:, 4 + c % 2, :],
                                          proj.xt[half][0][:, c, :].bitcast(F32), ALU.subtract).then_inc(xt_low, 1)
                    assert chain.count == LINKS, chain.count

                dve.wait_ge(biases_in, DMA * 5)
                dve.tensor_scalar(proj.qk_bias[:, 0:DC], proj.qk_bias[:, 0:DC], 1 / math.sqrt(DH), None, ALU.mult
                                  ).then_inc(proj.bias_scaled, 1)
                dve.wait_ge(proj.bias_scaled, 1)
                schedule(dve, front, lambda dve, n, b, half, k: proj.dve(dve, n, half, k))


    def project(self, memory):
        nc, ins, psum, ident = self.nc, self.ins, self.psum, self.ident
        sb = lambda name, shape, dt=F32: memory.enter_context(nc.sbuf_tensor(name, shape, dt))
        sem = self.sem
        proj = self.projection(memory, 1)
        self.projection_weights(memory, "project", "L3_", proj)
        rows = sb("project_rows", [P, 2, TT, D])
        gamma, beta = sb("project_gamma", [P, DC]), sb("project_beta", [P, DC])
        affine = sb("project_affine", [P, 2, TB])
        stats = sb("project_stats", [P, TT, 6])
        moments = sb("project_moments", [P, TT, 2])
        deviation, rstd = sb("project_deviation", [P, TT]), sb("project_rstd", [P, TT])
        constants_in = sem("project_constants_in")
        rows_in = [sem(f"project_rows_in{i}") for i in range(2)]
        variance_ready, deviation_ready = sem("project_variance"), sem("project_deviation_ready")
        normed = sem("project_normed")
        turned = sem("project_turned")
        affine_made, high = sem("project_affine_made"), sem("project_high")
        vec = sem("project_vector")
        LINKS = 2 * TT + 1
        xt_low = proj.xt_low

        with nc.Block() as block:

            def schedule(eng, front, project):
                front(eng, 0, 0, 0, lambda k: None)

                def body(eng, i):
                    for half in range(BPS):
                        n = i * BPS + half
                        front(eng, n + 1, i + half, 1 - half, lambda k: project(eng, n, i, half, k))
                body(eng, 0)
                with eng.Fori(1, B - 1) as i:
                    body(eng, i)
                i, n = B - 1, (B - 1) * BPS
                front(eng, n + 1, i, 1, lambda k: project(eng, n, i, 0, k))
                for k in range(12):
                    project(eng, n + 1, i, 1, k)

            @block.sync
            def _(sp):
                for dst, src in ((gamma[:, :], ins["L3_gamma1"]), (beta[:, :], ins["L3_beta1"]),
                                 (proj.qk_bias[:, 0:DC], ins["L3_bq"]), (proj.qk_bias[:, DC:2 * DC], ins["L3_bk"]),
                                 (proj.v_bias[:, :], ins["L3_bv"].partition_broadcast(P))):
                    sp.dma_start(dst, src).then_inc(constants_in, DMA)

                def front(sp, n, turn, half, project):
                    need(sp, turned, DC * (n - 1))
                    sp.dma_start(rows[:, half, :, :],
                                 self.rows[1][bass.ds(n * TB, TB), :].rearrange("(t p) d -> p t d", p=P)
                                 ).then_inc(rows_in[half], DMA)
                    for k in range(12):
                        project(k)

                schedule(sp, front, proj.sp)
                proj.sp_end(sp)

            @block.vector
            def _(dve):
                def front(dve, n, turn, half, project):
                    chain = Chain(dve, vec, n * LINKS)
                    link = chain.link
                    project(0)
                    dve.wait_ge(rows_in[half], DMA * (turn + 1))
                    for t in range(TT):
                        link(dve.bn_stats(stats[:, t, :], rows[:, half, t, :]))
                        apart(dve)
                        link(dve.bn_aggr(moments[:, t, :], stats[:, t, :]))
                        project(1 + t)
                    need(dve, deviation_ready, n)
                    dve.tensor_scalar(deviation[:, :], moments[:, :, 1], EPS, None, ALU.add).then_inc(variance_ready, 1)
                    project(5)
                    dve.wait_ge(deviation_ready, n + 1)
                    link(dve.reciprocal(rstd[:, :], deviation[:, :]))
                    for t in range(TT):
                        dve.tensor_scalar(rows[:, half, t, :], rows[:, half, t, :], moments[:, t, 0:1], rstd[:, t:t + 1],
                                          ALU.subtract, ALU.mult).then_inc(normed, 1)
                        project(6 + t)
                    project(10)
                    project(11)
                    for c in range(DC):
                        dve.wait_ge(high, n * DC + c + 1)
                        dve.tensor_tensor(proj.xt[half][1][:, c, :], affine[:, c % 2, :],
                                          proj.xt[half][0][:, c, :].bitcast(F32), ALU.subtract).then_inc(xt_low, 1)
                    assert chain.count == LINKS

                dve.wait_ge(constants_in, DMA * 5)
                dve.tensor_scalar(proj.qk_bias[:, 0:DC], proj.qk_bias[:, 0:DC], 1 / math.sqrt(DH), None, ALU.mult
                                  ).then_inc(proj.bias_scaled, 1)
                schedule(dve, front, lambda dve, n, b, half, k: proj.dve(dve, n, half, k))

            @block.scalar
            def _(act):
                def front(act, n, turn, half, project):
                    for k in range(5):
                        project(k)
                    act.wait_ge(variance_ready, n + 1)
                    act.activation(deviation[:, :], deviation[:, :], ACT.Sqrt).then_inc(deviation_ready, 1)
                    for k in range(5, 12):
                        project(k)
                    for c in range(DC):
                        act.wait_ge(turned, n * DC + c + 1)
                        need(act, xt_low, n * DC + c - 1)
                        act.activation(affine[:, c % 2, :], psum[:, 4 + c % 2, :], ACT.Identity, bias=beta[:, c:c + 1],
                                       scale=gamma[:, c:c + 1]).then_inc(affine_made, 1)

                act.wait_ge(constants_in, DMA * 5)
                act.wait_ge(proj.bias_scaled, 1)
                schedule(act, front, lambda act, n, b, half, k: proj.act(act, n, half, k))

            @block.gpsimd
            def _(pool):
                def front(pool, n, turn, half, project):
                    for c in range(DC):
                        pool.wait_ge(affine_made, n * DC + c + 1)
                        if c == 0:
                            need(pool, proj.projected, 12 * (n - 1))
                        apart(pool)
                        pool.tensor_scalar(proj.xt[half][0][:, c, :], affine[:, c % 2, :], 1.0, 1.0, ALU.mult,
                                           ALU.mult).then_inc(high, 1)

                schedule(pool, front, lambda *a: None)

            @block.tensor
            def _(pe):
                def front(pe, n, turn, half, project):
                    for k in range(12):
                        project(k)
                    pe.wait_ge(normed, TT * (n + 1))
                    for c in range(DC):
                        need(pe, affine_made, n * DC + c - 1)
                        for t in range(TT):
                            mm = pe.transpose(psum[:, 4 + c % 2, P * t:P * (t + 1)], rows[:, half, t, P * c:P * (c + 1)],
                                              ident[:, :])
                        mm.then_inc(turned, 1)

                schedule(pe, front, lambda pe, n, b, half, k: proj.pe(pe, n, half, k))


    def feed_forward(self, memory, layer):
        nc, ins, psum, ident = self.nc, self.ins, self.psum, self.ident
        final = layer == 1
        pre = "L3_" if final else "L2_"
        sb = lambda name, shape, dt=F32: memory.enter_context(nc.sbuf_tensor(f"ff_{name}{layer}", shape, dt))
        sem = lambda name: self.sem(f"ff_{name}{layer}")
        wo = (sb("wo_h", [P, DC * D], F32R), sb("wo_l", [P, DC * D], F32R))
        w1 = (sb("w1_h", [P, DC * F], F32R), sb("w1_l", [P, DC * F], F32R))
        w2 = (sb("w2_h", [P, FC * D], F32R), sb("w2_l", [P, FC * D], F32R))
        chunks = lambda name: ins[pre + name].rearrange("(c p) n -> c p n", p=P)
        by_rows = lambda src: (lambda at, to: src[at // D:to // D].rearrange("c p n -> p c n"))
        self.split_weights(memory, f"ff{layer}", [
            (by_rows(chunks("Wo")), *wo, 1.0), ((lambda at, to: chunks("W1")[at // F]), *w1, 1.0),
            (by_rows(chunks("W2")), *w2, 1.0)])
        ctx_t = sb("ctx_t", [P, 2, TB])
        xt_h, xt_l = sb("xt_h", [P, DC, TB], F32R), sb("xt_l", [P, DC, TB], F32R)
        rows = sb("rows", [P, TT, D])
        normal = sb("normal", [P, TT, D])
        act_full = sb("act_full", [P, 2, TB])
        act_h, act_l = sb("act_h", [P, 2, TB], F32R), sb("act_l", [P, 2, TB], F32R)
        bo, b2 = sb("bo", [P, D]), sb("b2", [P, D])
        b1, gamma, beta = sb("b1", [P, FC]), sb("gamma", [P, DC]), sb("beta", [P, DC])
        gate = sb("gate", [P, B])
        outgoing = normal
        stats, moments = sb("stats", [P, TT, 6]), sb("moments", [P, TT, 2])
        deviation, rstd = sb("deviation", [P, TT]), sb("rstd", [P, TT])
        constants_in = sem("constants_in")
        ctx_in = [sem(f"ctx_in{i}") for i in range(2)]
        rows_in = sem("rows_in")
        again_in = sem("again_in")
        ctx_high, ctx_low = sem("ctx_high"), sem("ctx_low")
        out_done, out_taken = sem("out_done"), sem("out_taken")
        rows_biased = sem("rows_biased")
        variance_ready, deviation_ready = sem("variance_ready"), sem("deviation_ready")
        normed, turned = sem("normed"), sem("turned")
        affine_made, affine_high, affine_low = sem("affine_made"), sem("affine_high"), sem("affine_low")
        inner_done = sem("inner_done")
        act_made, act_high, act_low = sem("act_made"), sem("act_high"), sem("act_low")
        outer_done = sem("outer_done")
        finished = sem("finished")
        stored = sem("stored")
        vec = sem("vector")
        LINKS = 2 * TT + 1 + TT + (2 * TT if final else 0)
        source = self.rows[1] if final else self.rows[0]
        target = self.out if final else self.rows[1]
        constants = [(bo[:, :], ins[pre + "bo"].partition_broadcast(P)), (b2[:, :], ins[pre + "b2"].partition_broadcast(P)),
                     (b1[:, :], ins[pre + "b1"]), (gamma[:, :], ins[pre + ("gamma2" if final else "g2")]),
                     (beta[:, :], ins[pre + "beta2"])]
        if final:
            constants.append((gate[:, :], ins["gate"].partition_broadcast(P)))
        INNER, TURN = (4, 5), (6, 7)

        with nc.Block() as block:

            def blocks(eng, body):
                for half in range(BPS):
                    body(eng, half, 0, half)
                with eng.Fori(1, B) as b:
                    for half in range(BPS):
                        body(eng, b * BPS + half, b, half)

            @block.sync
            def _(sp):
                for dst, src in constants:
                    sp.dma_start(dst, src).then_inc(constants_in, DMA)

                def body(sp, n, b, half):
                    for c in range(DC):
                        need(sp, ctx_low, n * DC + c - 1)
                        sp.dma_start(ctx_t[:, c % 2, :],
                                     self.attended[layer][bass.ds(b * D + P * c, P), TB * half:TB * (half + 1)]
                                     ).then_inc(ctx_in[c % 2], DMA)
                        if c == 1:
                            need(sp, stored, DMA * TT * n)
                            sp.dma_start(rows[:, :, :],
                                         source[bass.ds(n * TB, TB), :].rearrange("(t p) d -> p t d", p=P)
                                         ).then_inc(rows_in, DMA)
                    if final:
                        sp.wait_ge(turned, DC * (n + 1))
                        sp.dma_start(normal[:, :, :],
                                     source[bass.ds(n * TB, TB), :].rearrange("(t p) d -> p t d", p=P)
                                     ).then_inc(again_in, DMA)
                    for t in range(TT):
                        sp.wait_ge(finished, n * TT + t + 1)
                        sp.dma_start(target[bass.ds(n * TB + P * t, P), :], rows[:, t, :]).then_inc(stored, DMA)

                blocks(sp, body)
                sp.wait_ge(stored, DMA * TT * NB)

            @block.tensor
            def _(pe):
                def inner(n, f):
                    need(pe, act_made, n * FC + f - 1)
                    for c in range(DC):
                        at = slice(F * c + P * f, F * c + P * (f + 1))
                        mm = product(pe, psum[:, INNER[f % 2], :], (w1[0][:, at], w1[1][:, at]),
                                     (xt_h[:, c, :], xt_l[:, c, :]), c == 0, c == DC - 1)
                    mm.then_inc(inner_done, 1)

                def outer(n, f):
                    pe.wait_ge(act_low, n * FC + f + 1)
                    for t in range(TT):
                        at, row = slice(P * t, P * (t + 1)), slice(D * f, D * (f + 1))
                        mm = product(pe, psum[:, t, :], (act_h[:, f % 2, at], act_l[:, f % 2, at]),
                                     (w2[0][:, row], w2[1][:, row]), f == 0, f == FC - 1)
                    mm.then_inc(outer_done, 1)

                def body(pe, n, b, half):
                    pe.wait_ge(ctx_low, DC * (n + 1))
                    for t in range(TT):
                        need(pe, finished, (n - 1) * TT + t + 1)
                        at = slice(P * t, P * (t + 1))
                        for c in range(DC):
                            row = slice(D * c, D * (c + 1))
                            mm = product(pe, psum[:, t, :], (xt_h[:, c, at], xt_l[:, c, at]), (wo[0][:, row], wo[1][:, row]),
                                         c == 0, c == DC - 1)
                        mm.then_inc(out_done, 1)
                    pe.wait_ge(normed, TT * (n + 1))
                    for c in range(DC):
                        need(pe, affine_made, n * DC + c - 1)
                        for t in range(TT):
                            mm = pe.transpose(psum[:, TURN[c % 2], P * t:P * (t + 1)], normal[:, t, P * c:P * (c + 1)],
                                              ident[:, :])
                        mm.then_inc(turned, 1)
                    pe.wait_ge(affine_low, DC * (n + 1))
                    inner(n, 0)
                    for f in range(1, FC):
                        inner(n, f)
                        outer(n, f - 1)
                    outer(n, FC - 1)

                blocks(pe, body)

            @block.scalar
            def _(act):
                def body(act, n, b, half):
                    for c in range(DC):
                        act.wait_ge(ctx_in[c % 2], DMA * (2 * n + c // 2 + 1))
                        if c == 0:
                            need(act, inner_done, n * FC)
                        act.activation(xt_h[:, c, :], ctx_t[:, c % 2, :], ACT.Copy).then_inc(ctx_high, 1)
                    act.wait_ge(variance_ready, n + 1)
                    act.activation(deviation[:, :], deviation[:, :], ACT.Sqrt).then_inc(deviation_ready, 1)
                    for c in range(DC):
                        act.wait_ge(turned, n * DC + c + 1)
                        need(act, affine_low, n * DC + c - 1)
                        if c < 2:
                            need(act, act_low, n * FC)
                        act.activation(act_full[:, c % 2, :], psum[:, TURN[c % 2], :], ACT.Identity,
                                       bias=beta[:, c:c + 1], scale=gamma[:, c:c + 1]).then_inc(affine_made, 1)
                    for f in range(FC):
                        act.wait_ge(inner_done, n * FC + f + 1)
                        if f < 2:
                            act.wait_ge(affine_low, DC * (n + 1))
                        need(act, act_low, n * FC + f - 1)
                        act.activation(act_full[:, f % 2, :], psum[:, INNER[f % 2], :],
                                       ACT.Gelu if final else ACT.Gelu_apprx_sigmoid, bias=b1[:, f:f + 1]
                                       ).then_inc(act_made, 1)

                act.wait_ge(constants_in, DMA * len(constants))
                blocks(act, body)

            @block.gpsimd
            def _(pool):
                def body(pool, n, b, half):
                    pool.wait_ge(rows_in, DMA * (n + 1))
                    for t in range(TT):
                        pool.tensor_tensor(rows[:, t, :], rows[:, t, :], bo[:, :], ALU.add).then_inc(rows_biased, 1)
                    for c in range(DC):
                        pool.wait_ge(affine_made, n * DC + c + 1)
                        if c == 0:
                            pool.wait_ge(out_done, TT * (n + 1))
                        apart(pool)
                        pool.tensor_scalar(xt_h[:, c, :], act_full[:, c % 2, :], 1.0, 1.0, ALU.mult, ALU.mult
                                           ).then_inc(affine_high, 1)
                    for f in range(FC):
                        pool.wait_ge(act_made, n * FC + f + 1)
                        need(pool, outer_done, n * FC + f - 1)
                        apart(pool)
                        pool.tensor_scalar(act_h[:, f % 2, :], act_full[:, f % 2, :], 1.0, 1.0, ALU.mult, ALU.mult
                                           ).then_inc(act_high, 1)

                pool.wait_ge(constants_in, DMA * len(constants))
                blocks(pool, body)

            @block.vector
            def _(dve):
                def body(dve, n, b, half):
                    chain = Chain(dve, vec, n * LINKS)
                    link = chain.link
                    for c in range(DC):
                        dve.wait_ge(ctx_high, n * DC + c + 1)
                        dve.tensor_tensor(xt_l[:, c, :], ctx_t[:, c % 2, :], xt_h[:, c, :].bitcast(F32), ALU.subtract
                                          ).then_inc(ctx_low, 1)
                    for t in range(TT):
                        dve.wait_ge(out_done, n * TT + t + 1)
                        dve.wait_ge(rows_biased, n * TT + t + 1)
                        dve.tensor_tensor(rows[:, t, :], psum[:, t, :], rows[:, t, :], ALU.add).then_inc(out_taken, 1)
                        dve.wait_ge(out_taken, n * TT + t + 1)
                        link(dve.bn_stats(stats[:, t, :], rows[:, t, :]))
                        apart(dve)
                        link(dve.bn_aggr(moments[:, t, :], stats[:, t, :]))
                    dve.tensor_scalar(deviation[:, :], moments[:, :, 1], EPS, None, ALU.add).then_inc(variance_ready, 1)
                    dve.wait_ge(deviation_ready, n + 1)
                    link(dve.reciprocal(rstd[:, :], deviation[:, :]))
                    for t in range(TT):
                        dve.tensor_scalar(normal[:, t, :], rows[:, t, :], moments[:, t, 0:1], rstd[:, t:t + 1],
                                          ALU.subtract, ALU.mult).then_inc(normed, 1)
                    for c in range(DC):
                        dve.wait_ge(affine_high, n * DC + c + 1)
                        dve.tensor_tensor(xt_l[:, c, :], act_full[:, c % 2, :], xt_h[:, c, :].bitcast(F32), ALU.subtract
                                          ).then_inc(affine_low, 1)
                    for t in range(TT):
                        link(dve.tensor_tensor(rows[:, t, :], rows[:, t, :], b2[:, :], ALU.add))
                    for f in range(FC):
                        dve.wait_ge(act_high, n * FC + f + 1)
                        dve.tensor_tensor(act_l[:, f % 2, :], act_full[:, f % 2, :], act_h[:, f % 2, :].bitcast(F32),
                                          ALU.subtract).then_inc(act_low, 1)
                    dve.wait_ge(outer_done, FC * (n + 1))
                    if final:
                        dve.wait_ge(again_in, DMA * (n + 1))
                    for t in range(TT):
                        if not final:
                            dve.tensor_tensor(rows[:, t, :], psum[:, t, :], rows[:, t, :], ALU.add).then_inc(finished, 1)
                            continue
                        link(dve.tensor_tensor(rows[:, t, :], psum[:, t, :], rows[:, t, :], ALU.add))
                        link(dve.tensor_tensor(rows[:, t, :], rows[:, t, :], normal[:, t, :], ALU.subtract))
                        dve.scalar_tensor_tensor(out=rows[:, t, :], in0=rows[:, t, :], scalar=gate[:, bass.ds(b, 1)],
                                                 in1=normal[:, t, :], op0=ALU.mult, op1=ALU.add).then_inc(finished, 1)
                    assert chain.count == LINKS, chain.count

                dve.wait_ge(constants_in, DMA * len(constants))
                blocks(dve, body)


def program(nc, ins, out):
    Kernel(nc, ins, out).build()


def kernel(**inputs):
    import concourse.bacc as bacc
    from concourse.bass_utils import run_bass_kernel_spmd

    a = {k: np.asarray(v) for k, v in inputs.items()}
    columns = lambda v: np.ascontiguousarray(v.reshape(-1, P).T)
    l0 = lambda name: a["L0_cond_" + name]
    half = D // 2
    freqs = np.exp(np.arange(half, dtype=np.float32) * np.float32(-math.log(10000.0) / (half - 1)))
    data = {
        "x": a["x"].reshape(B * S, D),
        "x_T": a["x"].reshape(B * S, D).T,
        "timestep": a["itok_B_34_63"], "domain_id": a["itok_B_0_15"],
        "theta": a["condB_theta"], "phi": a["condB_phi"], "gate": a["condB_gatescore"],
        "bias": a["fside_Bx16xSxS_0"].reshape(B * H, S, S),
        "mask": a["mask_Bx1xSxS_bk0"].reshape(B, S, S).view(np.int32),
        "freqs": np.tile(columns(freqs), (1, 2)), "iota": np.arange(E, dtype=np.float32),
        "L0_down_WT": l0("down_W").T, "L0_down_b": l0("down_b").reshape(A, 1),
        "L0_up_WT": l0("up_W").T, "L0_up_b": l0("up_b"),
        "L0_expert_WT": l0("expert_W").transpose(2, 0, 1), "L0_expert_bT": l0("expert_b").T,
        "L0_domain_embT": l0("domain_emb").T, "L0_ln_gamma": l0("ln_gamma"), "L0_ln_beta": l0("ln_beta"),
    }
    for name in ("W_ada", "b_ada", "Wq", "Wk", "Wv", "Wo", "W1", "W2", "bo", "b2", "bv"):
        data["L2_" + name] = a["L2_cond_" + name]
    for name in ("Wq", "Wk", "Wv", "Wo", "W1", "W2", "bo", "b2", "bv"):
        data["L3_" + name] = a["L3_cond_" + name]
    for name in ("bq", "bk", "b1", "g2", "beta2"):
        data["L2_" + name] = columns(a["L2_cond_" + name])
    for name in ("bq", "bk", "b1", "gamma1", "beta1", "gamma2", "beta2"):
        data["L3_" + name] = columns(a["L3_cond_" + name])
    data = {k: np.ascontiguousarray(v) for k, v in data.items()}

    nc = bacc.Bacc("TRN2", target_bir_lowering=False, num_devices=1)
    ins = {k: nc.dram_tensor(k, v.shape, mybir.dt.from_np(v.dtype), kind="ExternalInput").ap() for k, v in data.items()}
    out = nc.dram_tensor("out", (B * S, D), F32, kind="ExternalOutput").ap()
    program(nc, ins, out)
    result = run_bass_kernel_spmd(nc, [data], core_ids=[0])
    return result.results[0]["out"].reshape(B, S, D)
```

```python
import math
from contextlib import ExitStack

import concourse.bass as bass
import concourse.mybir as mybir
import numpy as np

ALU = mybir.AluOpType
ACT = mybir.ActivationFunctionType
F32 = mybir.dt.float32
F32R = mybir.dt.float32r
BF16 = mybir.dt.bfloat16
I32 = mybir.dt.int32
U8 = mybir.dt.uint8

P = 128
B = 4
S = 1024
D = 512
A = 128
E = 16
H = 16
DH = D // H
F = 2048
DC = D // P
FC = F // P
TB = 512
TT = TB // P
NB = B * S // TB
BPS = S // TB
HG = P // DH
G = H // HG
NBG = B * G
KT = S // P
QP = S // 256
EPS = 1e-5
MASKED = -1e30
DMA = 16


def need(eng, semaphore, value):
    if isinstance(value, int) and value <= 0:
        return
    eng.wait_ge(semaphore, value)


def apart(eng):
    eng.nop(nofuse=True)


class Chain:

    def __init__(self, eng, semaphore, start=0):
        self.eng, self.semaphore, self.start, self.count = eng, semaphore, start, 0

    def link(self, instruction):
        instruction.then_inc(self.semaphore, 1)
        self.count += 1
        self.wait()

    def wait(self):
        self.eng.wait_ge(self.semaphore, self.start + self.count)


def product(pe, out, stationary, moving, first, last):
    (sh, sl), (mh, ml) = stationary, moving
    pe.matmul(out, sh, mh, start=first, stop=False)
    pe.matmul(out, sh, ml, start=False, stop=False)
    return pe.matmul(out, sl, mh, start=False, stop=last)


class Weights:

    def __init__(self, kernel, groups):
        self.groups, self.loaded, self.split = groups, kernel.weights_loaded, kernel.weights_split
        self.scaled, self.rounded = kernel.weights_scaled, kernel.weights_rounded
        self.loads_before = list(kernel.weight_loads)
        self.scales_before, self.before = kernel.weight_scales, kernel.weight_pieces
        for g, group in enumerate(groups):
            kernel.weight_loads[g] += len(group)
            kernel.weight_scales += sum(piece[4] != 1.0 for piece in group)
            kernel.weight_pieces += len(group)

    def until(self, g):
        return self.before + sum(len(group) for group in self.groups[:g + 1])

    def load(self, sp, g):
        for source, _, _, raw, _ in self.groups[g]:
            sp.dma_start(raw, source).then_inc(self.loaded[g], DMA)

    def high_parts(self, act, g):
        act.wait_ge(self.loaded[g], DMA * (self.loads_before[g] + len(self.groups[g])))
        scales = self.scales_before + sum(piece[4] != 1.0 for group in self.groups[:g] for piece in group)
        for _, high, _, raw, scale in self.groups[g]:
            if scale != 1.0:
                scales += 1
                act.activation(raw, raw, ACT.Copy, scale=scale).then_inc(self.scaled, 1)
                act.wait_ge(self.scaled, scales)
            act.activation(high, raw, ACT.Copy).then_inc(self.rounded, 1)

    def low_parts(self, dve, g):
        first = self.until(g) - len(self.groups[g])
        for i, (_, high, low, raw, _) in enumerate(self.groups[g]):
            dve.wait_ge(self.rounded, first + i + 1)
            dve.tensor_tensor(low, raw, high.bitcast(F32), ALU.subtract).then_inc(self.split, 1)


class Kernel:
    def __init__(self, nc, ins, out):
        self.nc, self.ins, self.out = nc, ins, out
        self.ctx = ExitStack()
        dram = lambda name, shape: nc.dram_tensor(name, shape, F32, kind="Internal").ap()
        self.rows = [dram(f"rows{n}", [B * S, D]) for n in range(2)]
        self.qk = [{n: dram(f"{n}{layer}", [B * D, S]) for n in ("qh", "ql", "kh", "kl")} for layer in range(2)]
        self.v = [dram(f"v{layer}", [NBG, S, P]) for layer in range(2)]
        self.attended = [dram(f"attended{layer}", [B * D, S]) for layer in range(2)]

    def constants_by(self, loads):
        self.constant_loads += loads
        return self.constants_in, DMA * self.constant_loads

    def split_tensor(self, memory, name, shape):
        high = memory.enter_context(self.nc.sbuf_tensor(f"{name}_h", shape, F32R))
        with self.nc.sbuf_tensor(f"{name}_raw", shape, F32) as raw:
            pass
        low = memory.enter_context(self.nc.sbuf_tensor(f"{name}_l", shape, F32R))
        return high, low, raw

    def sem(self, name):
        return self.ctx.enter_context(self.nc.semaphore(name))

    def build(self):
        nc = self.nc
        with self.ctx:
            sb = lambda name, shape, dt: self.ctx.enter_context(nc.sbuf_tensor(name, shape, dt))
            self.constants_in, self.constant_loads = self.sem("constants_in"), 0
            self.weights_loaded = [self.sem(f"weights_loaded{g}") for g in range(5)]
            self.weights_scaled, self.weights_rounded = self.sem("weights_scaled"), self.sem("weights_rounded")
            self.weights_split = self.sem("weights_split")
            self.weight_loads, self.weight_scales, self.weight_pieces = [0] * 5, 0, 0
            self.ident = sb("ident", [P, P], F32)
            self.ident16 = sb("ident16", [P, P], BF16)
            self.psum = self.ctx.enter_context(nc.psum_tensor("psum", [P, 8, 512], F32))
            with ExitStack() as memory:
                self.constants(memory)
                self.front(memory)
            with ExitStack() as memory:
                self.attention(memory, 0)
            with ExitStack() as memory:
                self.feed_forward(memory, 0)
            with ExitStack() as memory:
                self.project(memory)
            with ExitStack() as memory:
                self.attention(memory, 1)
            with ExitStack() as memory:
                self.feed_forward(memory, 1)


    def constants(self, memory):
        nc, ins = self.nc, self.ins
        sb = lambda name, shape, dt=F32: memory.enter_context(nc.sbuf_tensor(name, shape, dt))
        self.scale1 = sb("ada_scale", [P, B, D])
        self.shift = sb("ada_shift", [P, B, D])
        self.rot_own = sb("rot_own", [P, B, D])
        self.rot_other = sb("rot_other", [P, B, D])
        self.rot_beta = sb("rot_beta", [P, B, D])
        self.expert_h = sb("expert_h", [P, B, A], F32R)
        self.expert_l = sb("expert_l", [P, B, A], F32R)
        self.expert_bias = sb("expert_bias", [P, B])
        NA = 4 * B + 2 * B
        with ExitStack() as own:
            tb = lambda name, shape, dt=F32: own.enter_context(nc.sbuf_tensor(f"const_{name}", shape, dt))
            w_ada = tb("w_ada", [P, DC, 2 * D])
            b_ada = tb("b_ada", [P, 2 * D])
            gamma = tb("gamma0", [P, D])
            beta = tb("beta0", [P, D])
            experts = tb("experts", [P, E, A])
            expert_b = tb("expert_b", [P, E])
            domain = tb("domain", [P, E])
            freqs = tb("freqs", [P, 4])
            iota = tb("iota", [P, E])
            steps_i = tb("steps_i", [P, B], I32)
            steps = tb("steps", [P, B])
            ids_i = tb("ids_i", [P, B], I32)
            ids = tb("ids", [P, B])
            clipped = tb("clipped", [P, B])
            valid = tb("valid", [P, B])
            valid2 = tb("valid2", [P, B])
            onehot = tb("onehot", [P, B, E])
            onehot_valid = tb("onehot_valid", [P, B, E])
            angle = tb("angle", [P, NA])
            turns = tb("turns", [P, NA])
            reduced = tb("reduced", [P, NA])
            flipped = tb("flipped", [P, NA])
            sine = tb("sine", [P, NA])
            cosine = tb("cosine", [P, NA])
            minus_sine = tb("minus_sine", [P, NA])
            emb = tb("emb", [P, 4, B])
            emb_act = tb("emb_act", [P, 4, B])
            spread = tb("spread", [P, B, 4, P])
            chosen = tb("chosen", [P, B, A])
            part = tb("part", [P, E])
            bsum = tb("bsum", [P, 2 * B])
            ident_steps = self.sem("ident_steps")
            vec = self.sem("const_vector")
            reduced_done = self.sem("angles_reduced")
            sines_done = self.sem("sines_done")
            emb_ready = self.sem("emb_ready")
            spread_done = self.sem("emb_spread")
            ada_done = self.sem("ada_products")
            ada_used = self.sem("ada_products_used")
            loads = [
                (steps_i[:, :], ins["timestep"].partition_broadcast(P)),
                (ids_i[:, :], ins["domain_id"].partition_broadcast(P)),
                (angle[:, 16:20], ins["theta"].partition_broadcast(P)),
                (angle[:, 20:24], ins["phi"].partition_broadcast(P)),
                (freqs[:, :], ins["freqs"]),
                (iota[:, :], ins["iota"].partition_broadcast(P)),
                (gamma[:, :], ins["L0_ln_gamma"].partition_broadcast(P)),
                (beta[:, :], ins["L0_ln_beta"].partition_broadcast(P)),
                (experts[:, :, :], ins["L0_expert_WT"]),
                (expert_b[:, :], ins["L0_expert_bT"]),
                (domain[:, :], ins["L0_domain_embT"]),
                (w_ada[:, :, :], ins["L2_W_ada"].rearrange("(c p) n -> p c n", p=P)),
                (b_ada[:, :], ins["L2_b_ada"].partition_broadcast(P)),
            ]
            loaded, all_loaded = self.constants_by(len(loads))
            ident, ident16, psum = self.ident, self.ident16, self.psum
            with nc.Block() as block:

                @block.sync
                def _(sp):
                    for dst, src in loads:
                        sp.dma_start(dst, src).then_inc(loaded, DMA)

                @block.gpsimd
                def _(pool):
                    pool.memset(ident[:, :], 0.0).then_inc(ident_steps, 1)
                    pool.memset(ident16[:, :], 0.0).then_inc(ident_steps, 1)
                    pool.wait_ge(ident_steps, 2)
                    for m in (ident, ident16):
                        pool.affine_select(out=m[:, :], in_=m[:, :], compare_op=ALU.not_equal, fill=1.0, base=0,
                                           pattern=[[-1, P]], channel_multiplier=1).then_inc(ident_steps, 1)

                @block.vector
                def _(dve):
                    chain = Chain(dve, vec)
                    link = chain.link
                    dve.wait_ge(loaded, all_loaded)
                    dve.wait_ge(ident_steps, 4)
                    link(dve.tensor_copy(steps[:, :], steps_i[:, :]))
                    link(dve.tensor_scalar(steps[:, :], steps[:, :], 40.0, None, ALU.mult))
                    for b in range(B):
                        link(dve.tensor_scalar(angle[:, 0:16].rearrange("p (c b) -> p c b", b=B)[:, :, b],
                                               freqs[:, :], steps[:, b:b + 1], None, ALU.mult))
                    link(dve.tensor_scalar(turns[:, :], angle[:, :], 1 / (2 * math.pi), 12582912.0, ALU.mult, ALU.add))
                    link(dve.tensor_scalar(turns[:, :], turns[:, :], 12582912.0, None, ALU.subtract))
                    link(dve.scalar_tensor_tensor(out=reduced[:, :], in0=turns[:, :], scalar=-6.28125, in1=angle[:, :],
                                                  op0=ALU.mult, op1=ALU.add))
                    link(dve.scalar_tensor_tensor(out=reduced[:, :], in0=turns[:, :], scalar=-(2 * math.pi - 6.28125),
                                                  in1=reduced[:, :], op0=ALU.mult, op1=ALU.add))
                    link(dve.tensor_scalar(reduced[:, :], reduced[:, :], 3.1415925, -3.1415925, ALU.min, ALU.max))
                    link(dve.tensor_scalar(flipped[:, :], reduced[:, :], -1.0, None, ALU.mult))
                    link(dve.tensor_tensor(flipped[:, :], flipped[:, :], reduced[:, :], ALU.max))
                    dve.tensor_scalar(flipped[:, :], flipped[:, :], -1.0, math.pi / 2, ALU.mult,
                                      ALU.add).then_inc(reduced_done, 1)
                    link(dve.tensor_copy(ids[:, :], ids_i[:, :]))
                    link(dve.tensor_scalar(clipped[:, :], ids[:, :], 0.0, float(E - 1), ALU.max, ALU.min))
                    link(dve.tensor_tensor(valid[:, :], clipped[:, :], ids[:, :], ALU.is_equal))
                    link(dve.tensor_scalar(valid2[:, :], valid[:, :], -1.0, 1.0, ALU.mult, ALU.add))
                    for b in range(B):
                        link(dve.tensor_scalar(onehot[:, b, :], iota[:, :], clipped[:, b:b + 1], None, ALU.is_equal))
                        link(dve.tensor_scalar(onehot_valid[:, b, :], onehot[:, b, :], valid[:, b:b + 1], None,
                                               ALU.mult))
                        link(dve.tensor_scalar(chosen[:, b, :], ident[:, :], valid2[:, b:b + 1], None, ALU.mult))
                    for e in range(E):
                        for b in range(B):
                            last = dve.scalar_tensor_tensor(out=chosen[:, b, :], in0=experts[:, e, :],
                                                            scalar=onehot_valid[:, b, e:e + 1], in1=chosen[:, b, :],
                                                            op0=ALU.mult, op1=ALU.add)
                            last.then_inc(vec, 1)
                            chain.count += 1
                        chain.wait()
                    for b in range(B):
                        link(dve.tensor_copy(self.expert_h[:, b, :], chosen[:, b, :]))
                        link(dve.tensor_tensor(self.expert_l[:, b, :], chosen[:, b, :],
                                               self.expert_h[:, b, :].bitcast(F32), ALU.subtract))
                        link(dve.tensor_tensor_reduce(out=part[:, :], in0=expert_b[:, :], in1=onehot_valid[:, b, :],
                                                      scale=1.0, scalar=0.0, op0=ALU.mult, op1=ALU.add,
                                                      accum_out=bsum[:, b:b + 1]))
                        link(dve.tensor_tensor_reduce(out=part[:, :], in0=domain[:, :], in1=onehot[:, b, :],
                                                      scale=1.0, scalar=0.0, op0=ALU.mult, op1=ALU.add,
                                                      accum_out=bsum[:, B + b:B + b + 1]))
                    link(dve.tensor_tensor(self.expert_bias[:, :], bsum[:, 0:B], bsum[:, B:2 * B], ALU.add))
                    dve.wait_ge(sines_done, 2)
                    link(dve.tensor_copy(emb[:, 0:2, :].rearrange("p c b -> p (c b)"), sine[:, 0:8]))
                    dve.tensor_copy(emb[:, 2:4, :].rearrange("p c b -> p (c b)"), cosine[:, 8:16]).then_inc(emb_ready, 1)
                    dve.wait_ge(sines_done, 3)
                    link(dve.memset(spread[:, :, :, :], 0.0))
                    for b in range(B):
                        for c in range(4):
                            dve.tensor_scalar(spread[:, b, c, :], spread[:, b, c, :], emb_act[:, c, b:b + 1], None,
                                              ALU.add).then_inc(spread_done, 1)
                    link(dve.tensor_scalar(minus_sine[:, :], sine[:, :], -1.0, None, ALU.mult))
                    lanes = lambda ap: ap.rearrange("p (n f) -> p n f", f=4)
                    for b in range(B):
                        for lane in range(4):
                            col = 16 + B * (lane // 2) + b
                            cos = cosine[:, col:col + 1]
                            sin = (sine if lane % 2 == 0 else minus_sine)[:, col:col + 1]
                            own_g, other_g = lanes(gamma[:, :])[:, :, lane], lanes(gamma[:, :])[:, :, lane ^ 1]
                            own_b, other_b = lanes(beta[:, :])[:, :, lane], lanes(beta[:, :])[:, :, lane ^ 1]
                            link(dve.tensor_scalar(lanes(self.rot_own[:, b, :])[:, :, lane], own_g, cos, None, ALU.mult))
                            link(dve.tensor_scalar(lanes(self.rot_other[:, b, :])[:, :, lane], other_g, sin, None,
                                                   ALU.mult))
                            target = lanes(self.rot_beta[:, b, :])[:, :, lane]
                            link(dve.tensor_scalar(target, own_b, cos, None, ALU.mult))
                            link(dve.scalar_tensor_tensor(out=target, in0=other_b, scalar=sin, in1=target,
                                                          op0=ALU.mult, op1=ALU.add))
                    for b in range(B):
                        dve.wait_ge(ada_done, b + 1)
                        banks = 2 * (b % 2)
                        link(dve.scalar_tensor_tensor(out=self.scale1[:, b, :], in0=psum[:, banks, :], scalar=1.0,
                                                      in1=b_ada[:, 0:D], op0=ALU.add, op1=ALU.add))
                        link(dve.tensor_tensor(self.shift[:, b, :], psum[:, banks + 1, :], b_ada[:, D:2 * D], ALU.add))
                        dve.sem_inc(ada_used, 1)

                @block.scalar
                def _(act):
                    act.wait_ge(reduced_done, 1)
                    act.activation(sine[:, :], reduced[:, :], ACT.Sin).then_inc(sines_done, 1)
                    act.activation(cosine[:, :], flipped[:, :], ACT.Sin).then_inc(sines_done, 1)
                    act.wait_ge(emb_ready, 1)
                    act.activation(emb_act[:, :, :], emb[:, :, :], ACT.Silu).then_inc(sines_done, 1)

                @block.tensor
                def _(pe):
                    pe.wait_ge(loaded, all_loaded)
                    for b in range(B):
                        pe.wait_ge(spread_done, 4 * (b + 1))
                        need(pe, ada_used, b - 1)
                        for half in range(2):
                            for c in range(DC):
                                mm = pe.matmul(psum[:, 2 * (b % 2) + half, :], spread[:, b, c, :],
                                               w_ada[:, c, D * half:D * (half + 1)], start=c == 0, stop=c == DC - 1)
                        mm.then_inc(ada_done, 1)



    def attention(self, memory, layer):
        nc, psum, ident, ident16 = self.nc, self.psum, self.ident, self.ident16
        causal = layer == 1
        qk, v_dram, attended = self.qk[layer], self.v[layer], self.attended[layer]
        U = 8 * QP
        keys = lambda u: 2 * (u // 8 + 1) if causal else KT
        halves = lambda u: (keys(u) + 3) // 4
        by_dve = lambda u, half: half == 1 or causal and (u < 8 or u < 16 and u % 2 == 1)
        turn_bank = lambda u, half: TURN[half if halves(u) > 1 else u % 2]
        copies = lambda u, dve: sum(by_dve(x, half) == dve for x in range(u) for half in range(halves(x)))
        sb = lambda name, shape, dt=F32: memory.enter_context(nc.sbuf_tensor(f"{name}{layer}", shape, dt))
        q_stack = sb("q_stack", [P, HG, S], F32R)
        k_stack = sb("k_stack", [P, HG, S], F32R)
        values = sb("values", [P, KT, P])
        shifted = sb("shifted", [P, 2, S])
        least = sb("least", [P, 8])
        weights = sb("weights", [P, 2, S])
        total = sb("total", [P, 8])
        inverse = sb("inverse", [P, 8])
        normal = sb("normal", [P, 2, S])
        turned = sb("turned", [P, 2, HG, KT, 256])
        result = sb("result", [P, 2, 256])
        if causal:
            ahead = sb("ahead", [P, S + P])
        else:
            NBIAS = 4
            bias = sb("bias", [P, NBIAS, S])
            mask_u8 = sb("mask_u8", [P, KT, S], U8)
            mask = sb("mask", [P, KT, S], BF16)

        sem = lambda name: self.sem(f"{name}{layer}")
        qk_in = [sem(f"qk_in{j}") for j in range(HG)]
        values_in = sem("values_in")
        bias_in = [sem(f"bias_in{i}") for i in range(4)] if not causal else None
        mask_in, mask_made = sem("mask_in"), sem("mask_made")
        scored = sem("scored")
        biased = sem("biased")
        exped = sem("exped")
        inverted = sem("inverted")
        normed = sem("normed")
        transposed = sem("transposed")
        act_out = sem("act_out")
        dve_out = sem("dve_out")
        weighted = sem("weighted")
        result_out = sem("result_out")
        stored = [sem(f"attended_stored{i}") for i in range(2)]
        QK_DMAS = 8
        PIECES = 4
        SCORES = (0, 2)
        TURN = (4, 5)
        WEIGHT = (6, 7)

        def ahead_of(it, u, by):
            over, u2 = divmod(u + by, U)
            it2 = it + over
            return it2, u2, it2 * U + u2

        def copied(it, u, dve):
            return it * copies(U, dve) + copies(u, dve)

        def transposes_before(it, u):
            return copied(it, u, True) + copied(it, u, False)

        def turns(body):
            def run(eng):
                body(eng, 0, True, False)
                with eng.Fori(1, NBG - 1) as it:
                    body(eng, it, False, False)
                body(eng, NBG - 1, False, True)
            return run

        with nc.Block() as block:

            @block.sync
            def _(sp):
                def load_head(it, j):
                    for group in range(4):
                        part = slice(DH * group, DH * (group + 1))
                        rows = bass.ds(it * P + DH * j, DH)
                        q = qk["qh" if group < 2 else "ql"]
                        k = qk["kh" if group % 2 == 0 else "kl"]
                        sp.dma_start(q_stack[part, j, :].bitcast(F32), q[rows, :]).then_inc(qk_in[j], DMA)
                        sp.dma_start(k_stack[part, j, :].bitcast(F32), k[rows, :]).then_inc(qk_in[j], DMA)

                def load_values(it):
                    sp.dma_start(values[:, :, :],
                                 v_dram[it].rearrange("(k p) f -> p k f", p=P)).then_inc(values_in, DMA)

                def load_bias(it, u, number):
                    if causal:
                        return
                    need(sp, biased, number - 3)
                    tile = 2 * (u // 8) + u % 2
                    head = 4 * it + (u % 8) // 2
                    sp.dma_start(bias[:, u % 4, :], self.ins["bias"][head, P * tile:P * (tile + 1), :]
                                 ).then_inc(bias_in[u % 4], DMA)

                def load_mask(it):
                    sp.dma_start(mask_u8[:, :, :].bitcast(I32), self.ins["mask"][it // G].rearrange("(t p) k -> p t k", p=P)
                                 ).then_inc(mask_in, DMA)

                def store(it, pair):
                    number = it * QP + pair
                    sp.wait_ge(result_out, number + 1)
                    sp.dma_start(attended[bass.ds(it * P, P), 256 * pair:256 * (pair + 1)],
                                 result[:, pair % 2, :]).then_inc(stored[pair % 2], DMA)

                def body(sp, it, first, last):
                    for u in range(U):
                        if not (first and u == 0):
                            load_bias(it, u, it * U + u)
                        if u in (29, 31) and not last:
                            j = (u - 29) // 2
                            sp.wait_ge(scored, it * U + 24 + 2 * j + 2)
                            load_head(it + 1, j)
                        if u in (1, 3) and not first:
                            j = 2 + (u - 1) // 2
                            sp.wait_ge(scored, (it - 1) * U + 24 + 2 * j + 2)
                            load_head(it, j)
                        if u == 12 and not first:
                            sp.wait_ge(weighted, it * QP)
                            load_values(it)
                        if u == 8 and not causal and not last:
                            sp.wait_ge(mask_made, KT * (it + 1))
                            load_mask(it + 1)
                        if u % 8 == 5:
                            pair = u // 8 - 2
                            if pair >= 0:
                                store(it, pair)
                            elif not first:
                                store(it - 1, pair + QP)

                if not causal:
                    load_mask(0)
                load_head(0, 0)
                load_bias(0, 0, 0)
                for j in range(1, HG):
                    load_head(0, j)
                load_values(0)
                turns(body)(sp)
                store(NBG - 1, QP - 2)
                store(NBG - 1, QP - 1)
                for i in range(2):
                    sp.wait_ge(stored[i], DMA * NBG * QP // 2)

            @block.tensor
            def _(pe):
                def scores(it, u, number):
                    pair, j, half = u // 8, (u % 8) // 2, u % 2
                    tile, n = 2 * pair + half, keys(u) * P
                    if pair == 0 and half == 0:
                        pe.wait_ge(qk_in[j], DMA * QK_DMAS * (it + 1))
                    need(pe, biased, number - 1)
                    if not causal and j == 0:
                        pe.wait_ge(mask_made, it * KT + tile + 1)
                    bank = SCORES[half]
                    spans = [(at, min(at + 512, n)) for at in range(0, n, 512)]
                    if not causal:
                        for i, (at, to) in enumerate(spans):
                            pe.matmul(psum[:, bank + i, 0:to - at], ident16[:, :], mask[:, tile, at:to], start=True,
                                      stop=False)
                    for i, (at, to) in enumerate(spans):
                        mm = pe.matmul(psum[:, bank + i, 0:to - at], q_stack[:, j, P * tile:P * (tile + 1)],
                                       k_stack[:, j, at:to], start=causal, stop=True)
                    mm.then_inc(scored, 1)

                def transpose(it, u, number):
                    pe.wait_ge(normed, number + 1)
                    for half in range(halves(u)):
                        by, what = 1, None
                        while what is None:
                            turn2, u2, _ = ahead_of(it, u, -by)
                            what = next((h for h in range(halves(u2)) if turn_bank(u2, h) == turn_bank(u, half)), None)
                            by += 1
                        dve = by_dve(u2, what)
                        need(pe, dve_out if dve else act_out,
                             copied(turn2, u2, dve) + sum(by_dve(u2, h) == dve for h in range(what + 1)))
                        tiles = range(4 * half, min(4 * half + 4, keys(u)))
                        for k in tiles:
                            at = P * (k - tiles[0])
                            mm = pe.transpose(psum[:, turn_bank(u, half), at:at + P], normal[:, u % 2, P * k:P * (k + 1)],
                                              ident[:, :])
                        mm.then_inc(transposed, 1)

                def weigh(it, pair, piece):
                    number = it * QP + pair
                    last = 8 * pair + 7
                    n = keys(last)
                    if piece == 0:
                        need(pe, act_out, copied(it, last + 1, False))
                        need(pe, dve_out, copied(it, last + 1, True))
                        if pair == 0:
                            pe.wait_ge(values_in, DMA * (it + 1))
                        need(pe, result_out, number - 1)
                    span = range(n * piece // PIECES, n * (piece + 1) // PIECES)
                    for k in span:
                        for j in range(HG):
                            mm = pe.matmul(psum[DH * j:DH * (j + 1), WEIGHT[pair % 2], 0:256],
                                           values[:, k, DH * j:DH * (j + 1)], turned[:, pair % 2, j, k, :],
                                           start=k == 0, stop=k == n - 1,
                                           tile_position=(0, DH * j))
                    if piece == PIECES - 1:
                        mm.then_inc(weighted, 1)

                def body(pe, it, first, last):
                    for u in range(U):
                        transpose(it, u, it * U + u)
                        if not (last and u + 4 >= U):
                            scores(*ahead_of(it, u, 4))
                        if u % 8 < PIECES:
                            if u >= 8:
                                weigh(it, u // 8 - 1, u % 8)
                            elif not first:
                                weigh(it - 1, QP - 1, u % 8)

                for u in range(4):
                    scores(0, u, u)
                turns(body)(pe)
                for piece in range(PIECES):
                    weigh(NBG - 1, QP - 1, piece)

            @block.vector
            def _(dve):
                def add_bias(it, u, number):
                    n = keys(u) * P
                    dve.wait_ge(scored, number + 1)
                    need(dve, exped, number - 1)
                    if causal:
                        end = S if u % 2 else S + P
                        what = ahead[:, end - n:end]
                    else:
                        dve.wait_ge(bias_in[u % 4], DMA * (it * (U // 4) + u // 4 + 1))
                        what = bias[:, u % 4, 0:n]
                    bank = SCORES[u % 2]
                    apart(dve)
                    dve.tensor_tensor_reduce(
                        out=shifted[:, u % 2, 0:n], in0=psum[:, bank:bank + 2, :].rearrange("p b n -> p (b n)")[:, 0:n],
                        in1=what, scale=-1.0, scalar=3e38, op0=ALU.add, op1=ALU.min,
                        accum_out=least[:, u % 8:u % 8 + 1]).then_inc(biased, 1)

                def copy_transposed(it, u, number):
                    pair, j = u // 8, (u % 8) // 2
                    for half in range(halves(u)):
                        if not by_dve(u, half):
                            continue
                        dve.wait_ge(transposed, transposes_before(it, u) + half + 1)
                        need(dve, weighted, it * QP + pair - 1)
                        n = min(keys(u) - 4 * half, 4)
                        dve.tensor_copy(turned[:, pair % 2, j, 4 * half:4 * half + n, P * (u % 2):P * (u % 2 + 1)],
                                        psum[:, turn_bank(u, half), 0:P * n].rearrange("p (k q) -> p k q", k=n)
                                        ).then_inc(dve_out, 1)

                def invert(it, u, number):
                    dve.wait_ge(exped, number + 1)
                    dve.reciprocal(inverse[:, u % 8:u % 8 + 1], total[:, u % 8:u % 8 + 1]).then_inc(inverted, 1)

                def body(dve, it, first, last):
                    for u in range(U):
                        if not (last and u + 3 >= U):
                            add_bias(*ahead_of(it, u, 3))
                        copy_transposed(it, u, it * U + u)
                        if not (last and u + 2 >= U):
                            invert(*ahead_of(it, u, 2))

                if causal:
                    dve.wait_ge(mask_made, 2)
                for u in range(3):
                    add_bias(0, u, u)
                for u in range(2):
                    invert(0, u, u)
                turns(body)(dve)

            @block.scalar
            def _(act):
                def exponentiate(it, u, number):
                    n = keys(u) * P
                    act.wait_ge(biased, number + 1)
                    need(act, normed, number - 1)
                    act.activation(weights[:, u % 2, 0:n], shifted[:, u % 2, 0:n], ACT.Exp,
                                   bias=least[:, u % 8:u % 8 + 1], scale=-1.0,
                                   accum_out=total[:, u % 8:u % 8 + 1]).then_inc(exped, 1)

                def copy_transposed(it, u, number):
                    if by_dve(u, 0):
                        return
                    pair, j, half = u // 8, (u % 8) // 2, u % 2
                    act.wait_ge(transposed, transposes_before(it, u) + 1)
                    need(act, weighted, it * QP + pair - 1)
                    n = min(keys(u), 4)
                    act.activation(turned[:, pair % 2, j, 0:n, P * half:P * (half + 1)],
                                   psum[:, turn_bank(u, 0), 0:P * n].rearrange("p (k q) -> p k q", k=n),
                                   ACT.Copy).then_inc(act_out, 1)

                def take_result(it, pair):
                    number = it * QP + pair
                    act.wait_ge(weighted, number + 1)
                    need(act, stored[pair % 2], DMA * (it * (QP // 2) + pair // 2))
                    act.activation(result[:, pair % 2, :], psum[:, WEIGHT[pair % 2], 0:256],
                                   ACT.Copy).then_inc(result_out, 1)

                def body(act, it, first, last):
                    for u in range(U):
                        if not (last and u + 2 >= U):
                            exponentiate(*ahead_of(it, u, 2))
                        copy_transposed(it, u, it * U + u)
                        if u % 8 == PIECES:
                            if u >= 8:
                                take_result(it, u // 8 - 1)
                            elif not first:
                                take_result(it - 1, QP - 1)

                for u in range(2):
                    exponentiate(0, u, u)
                turns(body)(act)
                take_result(NBG - 1, QP - 1)

            @block.gpsimd
            def _(pool):
                def normalise(it, u, number):
                    n = keys(u) * P
                    pool.wait_ge(inverted, number + 1)
                    _, u0, _ = ahead_of(0, u, -2)
                    before = transposes_before(it + (u - 2) // U, u0) + halves(u0)
                    need(pool, transposed, before)
                    apart(pool)
                    pool.tensor_scalar(normal[:, u % 2, 0:n], weights[:, u % 2, 0:n], inverse[:, u % 8:u % 8 + 1],
                                       1.0, ALU.mult, ALU.mult).then_inc(normed, 1)

                def make_mask(it, tile):
                    if tile == 0:
                        pool.wait_ge(mask_in, DMA * (it + 1))
                    apart(pool)
                    pool.tensor_scalar(mask[:, tile, :], mask_u8[:, tile, :], MASKED, 1.0, ALU.mult,
                                       ALU.mult).then_inc(mask_made, 1)

                def body(pool, it, first, last):
                    for u in range(U):
                        if not (last and u + 1 >= U):
                            normalise(*ahead_of(it, u, 1))
                        if u % 8 >= 6 and not causal and not last:
                            pool.wait_ge(scored, it * U + u + 1)
                            make_mask(it + 1, 2 * (u // 8) + u % 2)

                if causal:
                    pool.memset(ahead[:, :], 0.0).then_inc(mask_in, 1)
                    pool.wait_ge(mask_in, 1)
                    pool.affine_select(out=ahead[:, S - P:S + P], in_=ahead[:, S - P:S + P], compare_op=ALU.is_ge,
                                       fill=MASKED, base=0, pattern=[[-1, 2 * P]],
                                       channel_multiplier=1).then_inc(mask_made, 2)
                else:
                    for tile in range(KT):
                        make_mask(0, tile)
                normalise(0, 0, 0)
                turns(body)(pool)


    def projection(self, memory, layer):
        psum = self.psum
        sb = lambda name, shape, dt=F32: memory.enter_context(self.nc.sbuf_tensor(f"{name}{layer}", shape, dt))
        sem = lambda name: self.sem(f"{name}{layer}")
        w = {}
        for name in "qkv":
            w[name] = self.split_tensor(memory, f"w{name}{layer}", [P, DC, D])
        xt = [(sb(f"xt_h_{i}_", [P, DC, TB], F32R), sb(f"xt_l_{i}_", [P, DC, TB], F32R)) for i in range(2)]
        qk_bias = sb("qk_bias", [P, 2 * DC])
        v_bias = sb("v_bias", [P, D])
        out_h = sb("out_h", [P, 2, TB], F32)
        out_l = sb("out_l", [P, 2, TB], F32)
        out_v = sb("out_v", [P, 2, D], F32)
        projected = sem("projected")
        high_out = sem("high_out")
        taken = sem("taken")
        qk_stored = [sem(f"qk_stored{i}") for i in range(2)]
        v_stored = [sem(f"v_stored{i}") for i in range(2)]
        xt_low = sem("xt_low")
        BANKS = (6, 7)
        qk, v = self.qk[layer], self.v[layer]

        class Pieces:
            pass

        def weight_groups(prefix):
            return [[(self.ins[f"{prefix}W{which}"].rearrange("(c p) n -> p c n", p=P),
                      *(part[:, :, :] for part in w[which]), 1 / math.sqrt(DH) if which == "q" else 1.0)]
                    for which in "qkv"]

        def pe(pe, n, half, i):
            if isinstance(n, int) and n == 0 and i % 4 == 0:
                weights = pieces.weights
                pe.wait_ge(weights.split, weights.until(len(weights.groups) - 3 + i // 4))
            if i == 0:
                pe.wait_ge(xt_low, DC * (n + 1))
            need(pe, taken, 12 * n + i - 1)
            out = psum[:, BANKS[i % 2], :]
            h, l = xt[half]
            for c in range(DC):
                if i < 8:
                    wh, wl, _ = w["qk"[i // 4]]
                    at = slice(P * (i % 4), P * (i % 4 + 1))
                    mm = product(pe, out, (wh[:, c, at], wl[:, c, at]), (h[:, c, :], l[:, c, :]), c == 0, c == DC - 1)
                else:
                    wh, wl, _ = w["v"]
                    at = slice(P * (i - 8), P * (i - 7))
                    mm = product(pe, out, (h[:, c, at], l[:, c, at]), (wh[:, c, :], wl[:, c, :]), c == 0, c == DC - 1)
            mm.then_inc(projected, 1)

        def act(act, n, half, i):
            if i >= 8:
                return
            act.wait_ge(projected, 12 * n + i + 1)
            need(act, qk_stored[i % 2], 2 * DMA * (4 * n + i // 2))
            act.activation(out_h[:, i % 2, :].bitcast(F32R), psum[:, BANKS[i % 2], :], ACT.Identity,
                           bias=qk_bias[:, i:i + 1]).then_inc(high_out, 1)

        def dve(dve, n, half, i):
            bank = psum[:, BANKS[i % 2], :]
            if i < 8:
                dve.wait_ge(high_out, 8 * n + i + 1)
                dve.scalar_tensor_tensor(out=out_l[:, i % 2, :], in0=bank, scalar=qk_bias[:, i:i + 1],
                                         in1=out_h[:, i % 2, :], op0=ALU.add, op1=ALU.subtract).then_inc(taken, 1)
            else:
                dve.wait_ge(projected, 12 * n + i + 1)
                need(dve, v_stored[i % 2], DMA * (2 * n + (i - 8) // 2))
                dve.tensor_tensor(out_v[:, i % 2, :], bank, v_bias[:, :], ALU.add).then_inc(taken, 1)

        def sp(sp, n, b, half, i):
            sp.wait_ge(taken, 12 * n + i + 1)
            if i < 8:
                rows = bass.ds(b * D + P * (i % 4), P)
                for part, src in (("h", out_h), ("l", out_l)):
                    sp.dma_start(qk["qk"[i // 4] + part][rows, TB * half:TB * (half + 1)],
                                 src[:, i % 2, :]).then_inc(qk_stored[i % 2], DMA)
            else:
                at = TB * half + P * (i - 8)
                sp.dma_start(v[bass.ds(b * G, G), at:at + P, :].rearrange("g p d -> p g d"),
                             out_v[:, i % 2, :].rearrange("p (g d) -> p g d", g=G)).then_inc(v_stored[i % 2], DMA)

        def sp_end(sp):
            for i in range(2):
                sp.wait_ge(qk_stored[i], 2 * DMA * 4 * NB)
                sp.wait_ge(v_stored[i], DMA * 2 * NB)

        pieces = Pieces()
        pieces.pe, pieces.act, pieces.dve, pieces.sp, pieces.sp_end = pe, act, dve, sp, sp_end
        pieces.xt, pieces.xt_low, pieces.projected = xt, xt_low, projected
        pieces.bias_scaled = sem("bias_scaled")
        pieces.weight_groups, pieces.qk_bias, pieces.v_bias = weight_groups, qk_bias, v_bias
        return pieces


    def front(self, memory):
        nc, ins, psum, ident = self.nc, self.ins, self.psum, self.ident
        sb = lambda name, shape, dt=F32: memory.enter_context(nc.sbuf_tensor(name, shape, dt))
        sem = self.sem
        proj = self.projection(memory, 0)
        down = self.split_tensor(memory, "down", [P, DC, A])
        up = self.split_tensor(memory, "up", [P, D])
        weights = proj.weights = Weights(self, [
            [(ins["L0_down_WT"].rearrange("(c p) a -> p c a", p=P), *(part[:, :, :] for part in down), 1.0),
             (ins["L0_up_WT"], *(part[:, :] for part in up), 1.0)]] + proj.weight_groups("L2_"))
        x_t = sb("x_t", [P, DC, TB])
        x_th, x_tl = sb("x_th", [P, DC, TB], F32R), sb("x_tl", [P, DC, TB], F32R)
        x_rows = sb("x_rows", [P, TT, D])
        y = sb("y", [P, TT, D])
        hidden = sb("hidden", [P, TB])
        hidden_h, hidden_l = sb("hidden_h", [P, TB], F32R), sb("hidden_l", [P, TB], F32R)
        mixed_h, mixed_l = sb("mixed_h", [P, TB], F32R), sb("mixed_l", [P, TB], F32R)
        expert = (sb("expert_now_h", [P, A], F32R), sb("expert_now_l", [P, A], F32R))
        scratch = sb("front_scratch", [P, 2, D])
        down_b, up_b = sb("down_b", [P, 1]), sb("up_b", [P, D])
        stats = sb("front_stats", [P, TT, 6])
        moments = sb("front_moments", [P, 2, TT, 2])
        deviation = sb("front_deviation", [P, 2, TT])
        rstd = sb("front_rstd", [P, 2, TT])

        biases_in, biases_all = self.constants_by(5)
        x_t_in, rows_in = sem("x_t_in"), sem("x_rows_in")
        x_high, x_low = sem("x_high"), sem("x_low")
        rows_biased = sem("rows_biased")
        down_done, hidden_made = sem("down_done"), sem("hidden_made")
        hidden_high, hidden_low = sem("hidden_high"), sem("hidden_low")
        expert_staged, expert_done = sem("expert_staged"), sem("expert_done")
        mixed_high, mixed_low = sem("mixed_high"), sem("mixed_low")
        up_done, up_taken = sem("up_done"), sem("up_taken")
        variance_ready, deviation_ready = sem("variance_ready"), sem("deviation_ready")
        vec = sem("front_vector")
        LINKS = 2 * 2 * TT + 2 + 5 * TT + TT
        rows_ready = sem("front_rows_ready")
        rows_stored = sem("front_rows_stored")
        turned, xt_high = sem("front_turned"), sem("front_xt_high")
        xt_low = proj.xt_low

        with nc.Block() as block:

            def schedule(eng, front, project, splits=lambda g: None):
                splits(0)
                front(eng, 0, 0, 0, lambda k: splits(k + 1) if k < 3 else None)

                def body(eng, i):
                    for half in range(BPS):
                        n = i * BPS + half
                        b, half2 = (i, half + 1) if half + 1 < BPS else (i + 1, 0)
                        front(eng, n + 1, b, half2, lambda k: project(eng, n, i, half, k))
                body(eng, 0)
                with eng.Fori(1, B - 1) as i:
                    body(eng, i)
                i, n = B - 1, (B - 1) * BPS
                front(eng, n + 1, i, 1, lambda k: project(eng, n, i, 0, k))
                for k in range(12):
                    project(eng, n + 1, i, 1, k)

            @block.sync
            def _(sp):
                sp.dma_start(down_b[:, :], ins["L0_down_b"]).then_inc(biases_in, DMA)
                sp.dma_start(up_b[:, :], ins["L0_up_b"].partition_broadcast(P)).then_inc(biases_in, DMA)
                sp.dma_start(proj.qk_bias[:, 0:DC], ins["L2_bq"]).then_inc(biases_in, DMA)
                sp.dma_start(proj.qk_bias[:, DC:2 * DC], ins["L2_bk"]).then_inc(biases_in, DMA)
                sp.dma_start(proj.v_bias[:, :], ins["L2_bv"].partition_broadcast(P)).then_inc(biases_in, DMA)

                def load_transposed(sp, n):
                    tokens = bass.ds(n * TB, TB)
                    need(sp, x_low, n)
                    sp.dma_start(x_t[:, :, :], ins["x_T"].rearrange("(c p) t -> p c t", p=P)[:, :, tokens]
                                 ).then_inc(x_t_in, DMA)

                def load_rows(sp, n):
                    tokens = bass.ds(n * TB, TB)
                    need(sp, up_taken, n * TT)
                    sp.dma_start(x_rows[:, :, :], ins["x"][tokens, :].rearrange("(t p) d -> p t d", p=P)
                                 ).then_inc(rows_in, DMA)

                def front(sp, n, b, half, project):
                    more = not (isinstance(n, int) and n == NB - 1)
                    for k in range(10):
                        project(k)
                        if k == 1 and more:
                            load_transposed(sp, n + 1)
                        if k == 6 and more:
                            load_rows(sp, n + 1)
                    for t in range(TT):
                        sp.wait_ge(rows_ready, n * TT + t + 1)
                        sp.dma_start(self.rows[0][bass.ds(n * TB + t * P, P), :], y[:, t, :]).then_inc(rows_stored, DMA)
                        if t < 2:
                            project(10 + t)

                weights.load(sp, 0)
                load_transposed(sp, 0)
                load_rows(sp, 0)
                for g in range(1, 4):
                    weights.load(sp, g)
                schedule(sp, front, proj.sp)
                proj.sp_end(sp)
                sp.wait_ge(rows_stored, DMA * TT * NB)

            @block.tensor
            def _(pe):
                def front(pe, n, b, half, project):
                    if isinstance(n, int) and n == 0:
                        pe.wait_ge(weights.split, weights.until(0))
                    pe.wait_ge(x_low, n + 1)
                    need(pe, hidden_made, n)
                    for c in range(DC):
                        mm = product(pe, psum[:, 0, :], (down[0][:, c, :], down[1][:, c, :]), (x_th[:, c, :], x_tl[:, c, :]),
                                     c == 0, c == DC - 1)
                    mm.then_inc(down_done, 1)
                    project(0)
                    project(1)
                    pe.wait_ge(hidden_low, n + 1)
                    pe.wait_ge(expert_staged, 2 * (n + 1))
                    need(pe, mixed_low, n)
                    product(pe, psum[:, 1, :], (expert[0][:, :], expert[1][:, :]), (hidden_h[:, :], hidden_l[:, :]),
                            True, True).then_inc(expert_done, 1)
                    project(2)
                    pe.wait_ge(mixed_low, n + 1)
                    for t in range(TT):
                        need(pe, up_taken, n * TT + t - 1)
                        at = slice(P * t, P * (t + 1))
                        product(pe, psum[:, 2 + t % 2, :], (mixed_h[:, at], mixed_l[:, at]), (up[0][:, :], up[1][:, :]),
                                True, True).then_inc(up_done, 1)
                        if t == 1:
                            project(3)
                    for k in range(4, 12):
                        project(k)
                    pe.wait_ge(rows_ready, TT * (n + 1))
                    for c in range(DC):
                        need(pe, xt_low, n * DC + c - 1)
                        for t in range(TT):
                            mm = pe.transpose(psum[:, 4 + c % 2, P * t:P * (t + 1)], y[:, t, P * c:P * (c + 1)],
                                              ident[:, :])
                        mm.then_inc(turned, 1)

                schedule(pe, front, lambda pe, n, b, half, k: proj.pe(pe, n, half, k))

            @block.scalar
            def _(act):
                def front(act, n, b, half, project):
                    act.wait_ge(x_t_in, DMA * (n + 1))
                    need(act, down_done, n)
                    act.activation(x_th[:, :, :], x_t[:, :, :], ACT.Copy).then_inc(x_high, 1)
                    act.wait_ge(down_done, n + 1)
                    need(act, hidden_low, n)
                    act.activation(hidden[:, :], psum[:, 0, :], ACT.Gelu, bias=down_b[:, 0:1]).then_inc(hidden_made, 1)
                    act.wait_ge(hidden_made, n + 1)
                    need(act, expert_done, n)
                    act.activation(hidden_h[:, :], hidden[:, :], ACT.Copy).then_inc(hidden_high, 1)
                    project(0)
                    project(1)
                    act.wait_ge(expert_done, n + 1)
                    need(act, up_done, n * TT)
                    act.activation(mixed_h[:, :], psum[:, 1, :], ACT.Identity,
                                   bias=self.expert_bias[:, bass.ds(b, 1)]).then_inc(mixed_high, 1)
                    for k in range(2, 5):
                        project(k)
                    for i in range(2):
                        act.wait_ge(variance_ready, 2 * n + i + 1)
                        act.activation(deviation[:, i, :], deviation[:, i, :], ACT.Sqrt).then_inc(deviation_ready, 1)
                        if i == 0:
                            for k in range(5, 8):
                                project(k)
                    for c in range(DC):
                        act.wait_ge(turned, n * DC + c + 1)
                        if c == 0:
                            need(act, proj.projected, 12 * (n - 1))
                        act.activation(proj.xt[half][0][:, c, :], psum[:, 4 + c % 2, :], ACT.Copy).then_inc(xt_high, 1)

                act.wait_ge(biases_in, biases_all)
                act.wait_ge(proj.bias_scaled, 1)
                schedule(act, front, lambda act, n, b, half, k: proj.act(act, n, half, k),
                         lambda g: weights.high_parts(act, g))

            @block.gpsimd
            def _(pool):
                def front(pool, n, b, half, project):
                    pool.wait_ge(x_high, n + 1)
                    need(pool, down_done, n)
                    pool.tensor_tensor(x_tl[:, :, :], x_t[:, :, :], x_th[:, :, :].bitcast(F32), ALU.subtract
                                       ).then_inc(x_low, 1)
                    need(pool, expert_done, n)
                    pool.tensor_copy(expert[0][:, :], self.expert_h[:, b, :].bitcast(F32)).then_inc(expert_staged, 1)
                    pool.tensor_copy(expert[1][:, :], self.expert_l[:, b, :].bitcast(F32)).then_inc(expert_staged, 1)
                    pool.wait_ge(rows_in, DMA * (n + 1))
                    for t in range(TT):
                        pool.tensor_tensor(x_rows[:, t, :], x_rows[:, t, :], up_b[:, :], ALU.add
                                           ).then_inc(rows_biased, 1)

                pool.wait_ge(biases_in, biases_all)
                schedule(pool, front, lambda *a: None)

            @block.vector
            def _(dve):
                def front(dve, n, b, half, project):
                    chain = Chain(dve, vec, n * LINKS)
                    link = chain.link

                    def moments_of(i, t):
                        link(dve.bn_stats(stats[:, t, :], y[:, t, :]))
                        apart(dve)
                        link(dve.bn_aggr(moments[:, i, t, :], stats[:, t, :]))

                    def variance(i):
                        dve.tensor_scalar(deviation[:, i, :], moments[:, i, :, 1], EPS, None, ALU.add
                                          ).then_inc(variance_ready, 1)

                    def inverse_deviation(i):
                        dve.wait_ge(deviation_ready, 2 * n + i + 1)
                        link(dve.reciprocal(rstd[:, i, :], deviation[:, i, :]))

                    dve.wait_ge(hidden_high, n + 1)
                    dve.tensor_tensor(hidden_l[:, :], hidden[:, :], hidden_h[:, :].bitcast(F32), ALU.subtract
                                      ).then_inc(hidden_low, 1)
                    project(0)
                    project(1)
                    dve.wait_ge(mixed_high, n + 1)
                    dve.scalar_tensor_tensor(out=mixed_l[:, :], in0=psum[:, 1, :],
                                             scalar=self.expert_bias[:, bass.ds(b, 1)], in1=mixed_h[:, :].bitcast(F32),
                                             op0=ALU.add, op1=ALU.subtract).then_inc(mixed_low, 1)
                    project(2)
                    need(dve, turned, n * DC)
                    need(dve, rows_stored, DMA * TT * n)
                    for t in range(TT):
                        dve.wait_ge(up_done, n * TT + t + 1)
                        dve.wait_ge(rows_biased, n * TT + t + 1)
                        dve.tensor_tensor(y[:, t, :], psum[:, 2 + t % 2, :], x_rows[:, t, :], ALU.add
                                          ).then_inc(up_taken, 1)
                        dve.wait_ge(up_taken, n * TT + t + 1)
                        moments_of(0, t)
                        if t in (1, 3):
                            project(3 + t // 2)
                    variance(0)
                    project(5)
                    inverse_deviation(0)
                    for t in range(TT):
                        mean = moments[:, 0, t, 0:1]
                        own, other = scratch[:, 0, :], scratch[:, 1, :]
                        pairs = lambda ap: ap.rearrange("p (n two) -> p n two", two=2)
                        dve.scalar_tensor_tensor(out=own, in0=y[:, t, :], scalar=mean, in1=self.rot_own[:, b, :],
                                                 op0=ALU.subtract, op1=ALU.mult).then_inc(vec, 1)
                        chain.count += 1
                        for lane in range(2):
                            dve.scalar_tensor_tensor(out=pairs(other)[:, :, lane], in0=pairs(y[:, t, :])[:, :, 1 - lane],
                                                     scalar=mean, in1=pairs(self.rot_other[:, b, :])[:, :, lane],
                                                     op0=ALU.subtract, op1=ALU.mult).then_inc(vec, 1)
                            chain.count += 1
                        chain.wait()
                        link(dve.tensor_tensor(own, own, other, ALU.add))
                        link(dve.scalar_tensor_tensor(out=y[:, t, :], in0=own, scalar=rstd[:, 0, t:t + 1],
                                                      in1=self.rot_beta[:, b, :], op0=ALU.mult, op1=ALU.add))
                        moments_of(1, t)
                        if t < 3:
                            project(6 + t)
                    variance(1)
                    project(9)
                    inverse_deviation(1)
                    for t in range(TT):
                        shifted = scratch[:, t % 2, :]
                        link(dve.scalar_tensor_tensor(out=shifted, in0=y[:, t, :], scalar=moments[:, 1, t, 0:1],
                                                      in1=self.scale1[:, b, :], op0=ALU.subtract, op1=ALU.mult))
                        dve.scalar_tensor_tensor(out=y[:, t, :], in0=shifted, scalar=rstd[:, 1, t:t + 1],
                                                 in1=self.shift[:, b, :], op0=ALU.mult, op1=ALU.add
                                                 ).then_inc(rows_ready, 1)
                        if t < 2:
                            project(10 + t)
                    for c in range(DC):
                        dve.wait_ge(xt_high, n * DC + c + 1)
                        dve.tensor_tensor(proj.xt[half][1][:, c, :], psum[:, 4 + c % 2, :],
                                          proj.xt[half][0][:, c, :].bitcast(F32), ALU.subtract).then_inc(xt_low, 1)
                    assert chain.count == LINKS, chain.count

                dve.wait_ge(biases_in, biases_all)
                dve.tensor_scalar(proj.qk_bias[:, 0:DC], proj.qk_bias[:, 0:DC], 1 / math.sqrt(DH), None, ALU.mult
                                  ).then_inc(proj.bias_scaled, 1)
                dve.wait_ge(proj.bias_scaled, 1)
                schedule(dve, front, lambda dve, n, b, half, k: proj.dve(dve, n, half, k),
                         lambda g: weights.low_parts(dve, g))


    def project(self, memory):
        nc, ins, psum, ident = self.nc, self.ins, self.psum, self.ident
        sb = lambda name, shape, dt=F32: memory.enter_context(nc.sbuf_tensor(name, shape, dt))
        sem = self.sem
        proj = self.projection(memory, 1)
        weights = proj.weights = Weights(self, proj.weight_groups("L3_"))
        rows = sb("project_rows", [P, 2, TT, D])
        gamma, beta = sb("project_gamma", [P, DC]), sb("project_beta", [P, DC])
        affine = sb("project_affine", [P, 2, TB])
        stats = sb("project_stats", [P, TT, 6])
        moments = sb("project_moments", [P, TT, 2])
        deviation, rstd = sb("project_deviation", [P, TT]), sb("project_rstd", [P, TT])
        constants_in, constants_all = self.constants_by(5)
        rows_in = [sem(f"project_rows_in{i}") for i in range(2)]
        variance_ready, deviation_ready = sem("project_variance"), sem("project_deviation_ready")
        normed = sem("project_normed")
        turned = sem("project_turned")
        affine_made, high = sem("project_affine_made"), sem("project_high")
        vec = sem("project_vector")
        LINKS = 2 * TT + 1
        xt_low = proj.xt_low

        with nc.Block() as block:

            def schedule(eng, front, project, splits=lambda g: None):
                front(eng, 0, 0, 0, lambda k: splits(k - 1) if 1 <= k < 4 else None)

                def body(eng, i):
                    for half in range(BPS):
                        n = i * BPS + half
                        front(eng, n + 1, i + half, 1 - half, lambda k: project(eng, n, i, half, k))
                body(eng, 0)
                with eng.Fori(1, B - 1) as i:
                    body(eng, i)
                i, n = B - 1, (B - 1) * BPS
                front(eng, n + 1, i, 1, lambda k: project(eng, n, i, 0, k))
                for k in range(12):
                    project(eng, n + 1, i, 1, k)

            @block.sync
            def _(sp):
                for dst, src in ((gamma[:, :], ins["L3_gamma1"]), (beta[:, :], ins["L3_beta1"]),
                                 (proj.qk_bias[:, 0:DC], ins["L3_bq"]), (proj.qk_bias[:, DC:2 * DC], ins["L3_bk"]),
                                 (proj.v_bias[:, :], ins["L3_bv"].partition_broadcast(P))):
                    sp.dma_start(dst, src).then_inc(constants_in, DMA)

                def front(sp, n, turn, half, project):
                    need(sp, turned, DC * (n - 1))
                    sp.dma_start(rows[:, half, :, :],
                                 self.rows[1][bass.ds(n * TB, TB), :].rearrange("(t p) d -> p t d", p=P)
                                 ).then_inc(rows_in[half], DMA)
                    for k in range(12):
                        project(k)

                schedule(sp, front, proj.sp, lambda g: weights.load(sp, g))
                proj.sp_end(sp)

            @block.vector
            def _(dve):
                def front(dve, n, turn, half, project):
                    chain = Chain(dve, vec, n * LINKS)
                    link = chain.link
                    project(0)
                    dve.wait_ge(rows_in[half], DMA * (turn + 1))
                    for t in range(TT):
                        link(dve.bn_stats(stats[:, t, :], rows[:, half, t, :]))
                        apart(dve)
                        link(dve.bn_aggr(moments[:, t, :], stats[:, t, :]))
                        project(1 + t)
                    need(dve, deviation_ready, n)
                    dve.tensor_scalar(deviation[:, :], moments[:, :, 1], EPS, None, ALU.add).then_inc(variance_ready, 1)
                    project(5)
                    dve.wait_ge(deviation_ready, n + 1)
                    link(dve.reciprocal(rstd[:, :], deviation[:, :]))
                    for t in range(TT):
                        dve.tensor_scalar(rows[:, half, t, :], rows[:, half, t, :], moments[:, t, 0:1], rstd[:, t:t + 1],
                                          ALU.subtract, ALU.mult).then_inc(normed, 1)
                        project(6 + t)
                    project(10)
                    project(11)
                    for c in range(DC):
                        dve.wait_ge(high, n * DC + c + 1)
                        dve.tensor_tensor(proj.xt[half][1][:, c, :], affine[:, c % 2, :],
                                          proj.xt[half][0][:, c, :].bitcast(F32), ALU.subtract).then_inc(xt_low, 1)
                    assert chain.count == LINKS

                dve.wait_ge(constants_in, constants_all)
                dve.tensor_scalar(proj.qk_bias[:, 0:DC], proj.qk_bias[:, 0:DC], 1 / math.sqrt(DH), None, ALU.mult
                                  ).then_inc(proj.bias_scaled, 1)
                schedule(dve, front, lambda dve, n, b, half, k: proj.dve(dve, n, half, k),
                         lambda g: weights.low_parts(dve, g))

            @block.scalar
            def _(act):
                def front(act, n, turn, half, project):
                    for k in range(5):
                        project(k)
                    act.wait_ge(variance_ready, n + 1)
                    act.activation(deviation[:, :], deviation[:, :], ACT.Sqrt).then_inc(deviation_ready, 1)
                    for k in range(5, 12):
                        project(k)
                    for c in range(DC):
                        act.wait_ge(turned, n * DC + c + 1)
                        need(act, xt_low, n * DC + c - 1)
                        act.activation(affine[:, c % 2, :], psum[:, 4 + c % 2, :], ACT.Identity, bias=beta[:, c:c + 1],
                                       scale=gamma[:, c:c + 1]).then_inc(affine_made, 1)

                act.wait_ge(constants_in, constants_all)
                act.wait_ge(proj.bias_scaled, 1)
                schedule(act, front, lambda act, n, b, half, k: proj.act(act, n, half, k),
                         lambda g: weights.high_parts(act, g))

            @block.gpsimd
            def _(pool):
                def front(pool, n, turn, half, project):
                    for c in range(DC):
                        pool.wait_ge(affine_made, n * DC + c + 1)
                        if c == 0:
                            need(pool, proj.projected, 12 * (n - 1))
                        apart(pool)
                        pool.tensor_scalar(proj.xt[half][0][:, c, :], affine[:, c % 2, :], 1.0, 1.0, ALU.mult,
                                           ALU.mult).then_inc(high, 1)

                schedule(pool, front, lambda *a: None)

            @block.tensor
            def _(pe):
                def front(pe, n, turn, half, project):
                    for k in range(12):
                        project(k)
                    pe.wait_ge(normed, TT * (n + 1))
                    for c in range(DC):
                        need(pe, affine_made, n * DC + c - 1)
                        for t in range(TT):
                            mm = pe.transpose(psum[:, 4 + c % 2, P * t:P * (t + 1)], rows[:, half, t, P * c:P * (c + 1)],
                                              ident[:, :])
                        mm.then_inc(turned, 1)

                schedule(pe, front, lambda pe, n, b, half, k: proj.pe(pe, n, half, k))


    def feed_forward(self, memory, layer):
        nc, ins, psum, ident = self.nc, self.ins, self.psum, self.ident
        final = layer == 1
        pre = "L3_" if final else "L2_"
        sb = lambda name, shape, dt=F32: memory.enter_context(nc.sbuf_tensor(f"ff_{name}{layer}", shape, dt))
        sem = lambda name: self.sem(f"ff_{name}{layer}")
        wo, w1, w2 = (self.split_tensor(memory, f"ff_{name}{layer}", shape) for name, shape in
                      (("wo", [P, DC, D]), ("w1", [P, DC, F]), ("w2", [P, FC, D])))
        chunks = lambda name: ins[pre + name].rearrange("(c p) n -> p c n", p=P)
        groups = [[(chunks("Wo"), *(part[:, :, :] for part in wo), 1.0)]]
        for g in range(FC // 4):
            inner_at, outer_at = slice(4 * P * g, 4 * P * (g + 1)), slice(4 * g, 4 * (g + 1))
            groups.append([(chunks("W1")[:, :, inner_at], *(part[:, :, inner_at] for part in w1), 1.0),
                           (chunks("W2")[:, outer_at, :], *(part[:, outer_at, :] for part in w2), 1.0)])
        weights = Weights(self, groups)
        ctx_t = sb("ctx_t", [P, DC, P])
        ctx_h, ctx_l = sb("ctx_h", [P, DC, P], F32R), sb("ctx_l", [P, DC, P], F32R)
        xt_h, xt_l = sb("xt_h", [P, DC, TB], F32R), sb("xt_l", [P, DC, TB], F32R)
        rows = sb("rows", [P, 2, TT, D])
        normal = sb("normal", [P, TT, D])
        act_full = sb("act_full", [P, 2, TB])
        act_h, act_l = sb("act_h", [P, 2, TB], F32R), sb("act_l", [P, 2, TB], F32R)
        bo, b2 = sb("bo", [P, D]), sb("b2", [P, D])
        b1, gamma, beta = sb("b1", [P, FC]), sb("gamma", [P, DC]), sb("beta", [P, DC])
        gate, ungated = sb("gate", [P, B]), sb("ungated", [P, B])
        stats, moments = sb("stats", [P, TT, 6]), sb("moments", [P, TT, 2])
        deviation, rstd = sb("deviation", [P, TT]), sb("rstd", [P, TT])
        ungated_made = sem("ungated_made") if final else None
        ctx_in, rows_in = sem("ctx_in"), [sem(f"rows_in{i}") for i in range(2)]
        ctx_high, ctx_low = sem("ctx_high"), sem("ctx_low")
        out_done, out_taken = sem("out_done"), sem("out_taken")
        rows_biased = None if final else sem("rows_biased")
        variance_ready, deviation_ready = sem("variance_ready"), sem("deviation_ready")
        normed, turned = sem("normed"), sem("turned")
        affine_made, affine_high, affine_low = sem("affine_made"), sem("affine_high"), sem("affine_low")
        inner_done = sem("inner_done")
        act_made, act_high, act_low = sem("act_made"), sem("act_high"), sem("act_low")
        outer_done = sem("outer_done")
        shifted = None if final else sem("shifted")
        finished = sem("finished")
        stored = sem("stored")
        vec = sem("vector")
        LINKS = (5 if final else 2) * TT + 1
        source = self.rows[1] if final else self.rows[0]
        target = self.out if final else self.rows[1]
        constants = [(bo[:, :], ins[pre + "bo"].partition_broadcast(P)), (b2[:, :], ins[pre + "b2"].partition_broadcast(P)),
                     (b1[:, :], ins[pre + "b1"]), (gamma[:, :], ins[pre + ("gamma2" if final else "g2")]),
                     (beta[:, :], ins[pre + "beta2"])]
        if final:
            constants.append((gate[:, :], ins["gate"].partition_broadcast(P)))
        constants_in, constants_all = self.constants_by(len(constants))
        INNER, TURN, OUTPUT = (4, 5), (6, 7), 7
        AFTER = FC

        with nc.Block() as block:

            def schedule(eng, ahead, step, end=lambda *a: None, splits=lambda g: None):
                def body(eng, i, half, last):
                    n = i * BPS + half
                    next_b, next_half = (i, half + 1) if half + 1 < BPS else (i + 1, 0)
                    first = isinstance(n, int) and n == 0
                    for f in range(FC):
                        if first and f % 4 == 0 and f // 4 + 2 < len(groups):
                            splits(f // 4 + 2)
                        step(eng, n, i, half, f)
                        if not last:
                            ahead(eng, n + 1, next_b, next_half, f)
                    if not last:
                        ahead(eng, n + 1, next_b, next_half, AFTER)
                    end(eng, n, i, half)

                splits(0)
                for f in range(FC):
                    ahead(eng, 0, 0, 0, f)
                    if f == 12:
                        splits(1)
                ahead(eng, 0, 0, 0, AFTER)
                for half in range(BPS):
                    body(eng, 0, half, False)
                with eng.Fori(1, B - 1) as i:
                    for half in range(BPS):
                        body(eng, i, half, False)
                for half in range(BPS):
                    body(eng, B - 1, half, half == BPS - 1)

            @block.sync
            def _(sp):
                def load_rows(sp, n, b, half):
                    need(sp, stored, DMA * TT * (n - 1))
                    sp.dma_start(rows[:, half, :, :],
                                 source[bass.ds(n * TB, TB), :].rearrange("(t p) d -> p t d", p=P)
                                 ).then_inc(rows_in[half], DMA)

                def load_ctx(sp, n, b, half, t):
                    need(sp, ctx_low, n * TT + t)
                    at = TB * half + P * t
                    sp.dma_start(ctx_t[:, :, :], self.attended[layer][bass.ds(b * D, D), at:at + P]
                                 .rearrange("(c p) t -> p c t", p=P)).then_inc(ctx_in, DMA)

                def ahead(sp, n, b, half, f):
                    if f == 0:
                        load_ctx(sp, n, b, half, 0)
                        if not (isinstance(n, int) and n == 0):
                            load_rows(sp, n, b, half)
                    if f in (1, 4, 7):
                        load_ctx(sp, n, b, half, (f + 2) // 3)

                def end(sp, n, b, half):
                    for t in range(TT):
                        sp.wait_ge(finished, n * TT + t + 1)
                        sp.dma_start(target[bass.ds(n * TB + P * t, P), :], rows[:, half, t, :]).then_inc(stored, DMA)

                def load_weights(g):
                    if g == 0:
                        weights.load(sp, 0)
                        load_rows(sp, 0, 0, 0)
                        for dst, src in constants:
                            sp.dma_start(dst, src).then_inc(constants_in, DMA)
                        for later in range(1, len(groups)):
                            weights.load(sp, later)

                load_weights(0)
                schedule(sp, ahead, lambda *a: None, end)
                sp.wait_ge(stored, DMA * TT * NB)

            @block.tensor
            def _(pe):
                def inner(n, f):
                    if f == 0:
                        pe.wait_ge(affine_low, DC * (n + 1))
                    need(pe, act_made, n * FC + f - 1)
                    if isinstance(n, int) and n == 0 and f % 4 == 0:
                        pe.wait_ge(weights.split, weights.until(1 + f // 4))
                    at = slice(P * f, P * (f + 1))
                    for c in range(DC):
                        mm = product(pe, psum[:, INNER[f % 2], :], (w1[0][:, c, at], w1[1][:, c, at]),
                                     (xt_h[:, c, :], xt_l[:, c, :]), c == 0, c == DC - 1)
                    mm.then_inc(inner_done, 1)

                def outer(n, f):
                    pe.wait_ge(act_low, n * FC + f + 1)
                    for t in range(TT):
                        if f == 0:
                            need(pe, finished, (n - 1) * TT + t + 1)
                        at = slice(P * t, P * (t + 1))
                        mm = product(pe, psum[:, t, :], (act_h[:, f % 2, at], act_l[:, f % 2, at]),
                                     (w2[0][:, f, :], w2[1][:, f, :]), f == 0, f == FC - 1)
                    mm.then_inc(outer_done, 1)

                def output(n, t):
                    if isinstance(n, int) and n == 0 and t == 0:
                        pe.wait_ge(weights.split, weights.until(0))
                    pe.wait_ge(ctx_low, n * TT + t + 1)
                    need(pe, out_taken, n * TT + t)
                    if t == 0:
                        need(pe, affine_made, n * DC)
                    for c in range(DC):
                        mm = product(pe, psum[:, OUTPUT, :], (ctx_h[:, c, :], ctx_l[:, c, :]),
                                     (wo[0][:, c, :], wo[1][:, c, :]), c == 0, c == DC - 1)
                    mm.then_inc(out_done, 1)

                def turn(n, c):
                    if c == 0:
                        pe.wait_ge(normed, TT * (n + 1))
                    need(pe, affine_made, n * DC + c - 1)
                    for t in range(TT):
                        mm = pe.transpose(psum[:, TURN[c % 2], P * t:P * (t + 1)], normal[:, t, P * c:P * (c + 1)],
                                          ident[:, :])
                    mm.then_inc(turned, 1)

                def step(pe, n, b, half, f):
                    inner(n, f)
                    if 1 <= f < FC - 1:
                        outer(n, f - 1)

                def ahead(pe, n, b, half, f):
                    if f in (2, 5, 8, 11):
                        output(n, (f - 2) // 3)
                    if f == FC - 1:
                        turn(n, 0)
                        turn(n, 1)
                        if not (isinstance(n, int) and n == 0):
                            outer(n - 1, FC - 2)
                    if f == AFTER:
                        turn(n, 2)
                        turn(n, 3)

                def end(pe, n, b, half):
                    if isinstance(n, int) and n == NB - 1:
                        outer(n, FC - 2)
                    outer(n, FC - 1)

                schedule(pe, ahead, step, end)

            @block.scalar
            def _(act):
                def step(act, n, b, half, f):
                    act.wait_ge(inner_done, n * FC + f + 1)
                    if f < 2:
                        act.wait_ge(affine_low, DC * (n + 1))
                    need(act, act_low, n * FC + f - 1)
                    act.activation(act_full[:, f % 2, :], psum[:, INNER[f % 2], :],
                                   ACT.Gelu if final else ACT.Gelu_apprx_sigmoid, bias=b1[:, f:f + 1]
                                   ).then_inc(act_made, 1)

                def ahead(act, n, b, half, f):
                    if f in (1, 4, 7, 10):
                        t = (f - 1) // 3
                        act.wait_ge(ctx_in, DMA * (n * TT + t + 1))
                        need(act, out_done, n * TT + t)
                        act.activation(ctx_h[:, :, :], ctx_t[:, :, :], ACT.Copy).then_inc(ctx_high, 1)
                    if f == 13:
                        act.wait_ge(variance_ready, n + 1)
                        act.activation(deviation[:, :], deviation[:, :], ACT.Sqrt).then_inc(deviation_ready, 1)
                    if f == AFTER:
                        for c in range(DC):
                            act.wait_ge(turned, n * DC + c + 1)
                            if c < 2:
                                need(act, act_low, n * FC + c - 1)
                            need(act, affine_low, n * DC + c - 1)
                            act.activation(act_full[:, c % 2, :], psum[:, TURN[c % 2], :], ACT.Identity,
                                           bias=beta[:, c:c + 1], scale=gamma[:, c:c + 1]).then_inc(affine_made, 1)

                act.wait_ge(constants_in, constants_all)
                schedule(act, ahead, step, splits=lambda g: weights.high_parts(act, g))

            @block.gpsimd
            def _(pool):
                def step(pool, n, b, half, f):
                    pool.wait_ge(act_made, n * FC + f + 1)
                    need(pool, outer_done, n * FC + f - 1)
                    apart(pool)
                    pool.tensor_scalar(act_h[:, f % 2, :], act_full[:, f % 2, :], 1.0, 1.0, ALU.mult, ALU.mult
                                       ).then_inc(act_high, 1)
                    if not final and 5 <= f < 5 + TT:
                        t = f - 5
                        pool.wait_ge(normed, TT * (n + 1))
                        pool.tensor_tensor(rows[:, half, t, :], rows[:, half, t, :], b2[:, :], ALU.add
                                           ).then_inc(shifted, 1)

                def ahead(pool, n, b, half, f):
                    if not final and f in (1, 3, 5, 7):
                        if f == 1:
                            pool.wait_ge(rows_in[half], DMA * (b + 1))
                        t = f // 2
                        pool.tensor_tensor(rows[:, half, t, :], rows[:, half, t, :], bo[:, :], ALU.add
                                           ).then_inc(rows_biased, 1)
                    if f == AFTER:
                        for c in range(DC):
                            pool.wait_ge(affine_made, n * DC + c + 1)
                            if c == 0:
                                need(pool, inner_done, n * FC)
                            apart(pool)
                            pool.tensor_scalar(xt_h[:, c, :], act_full[:, c % 2, :], 1.0, 1.0, ALU.mult, ALU.mult
                                               ).then_inc(affine_high, 1)

                pool.wait_ge(constants_in, constants_all)
                schedule(pool, ahead, step)

            @block.vector
            def _(dve):
                def step(dve, n, b, half, f):
                    dve.wait_ge(act_high, n * FC + f + 1)
                    dve.tensor_tensor(act_l[:, f % 2, :], act_full[:, f % 2, :], act_h[:, f % 2, :].bitcast(F32),
                                      ALU.subtract).then_inc(act_low, 1)

                def take(n, b, half, t):
                    row, own = rows[:, half, t, :], normal[:, t, :]
                    chain = Chain(dve, vec, n * LINKS + t * (LINKS // TT))
                    link = chain.link
                    dve.wait_ge(out_done, n * TT + t + 1)
                    if t == 0:
                        need(dve, turned, n * DC)
                    if final:
                        if t == 0:
                            dve.wait_ge(rows_in[half], DMA * (b + 1))
                        dve.tensor_tensor(own, psum[:, OUTPUT, :], bo[:, :], ALU.add).then_inc(out_taken, 1)
                        dve.wait_ge(out_taken, n * TT + t + 1)
                        link(dve.scalar_tensor_tensor(out=row, in0=own, scalar=gate[:, bass.ds(b, 1)], in1=row,
                                                      op0=ALU.mult, op1=ALU.add))
                        link(dve.scalar_tensor_tensor(out=own, in0=own, scalar=ungated[:, bass.ds(b, 1)], in1=row,
                                                      op0=ALU.mult, op1=ALU.add))
                        link(dve.scalar_tensor_tensor(out=row, in0=b2[:, :], scalar=gate[:, bass.ds(b, 1)], in1=row,
                                                      op0=ALU.mult, op1=ALU.add))
                        link(dve.bn_stats(stats[:, t, :], own))
                    else:
                        dve.wait_ge(rows_biased, n * TT + t + 1)
                        dve.tensor_tensor(row, psum[:, OUTPUT, :], row, ALU.add).then_inc(out_taken, 1)
                        dve.wait_ge(out_taken, n * TT + t + 1)
                        link(dve.bn_stats(stats[:, t, :], row))
                    apart(dve)
                    link(dve.bn_aggr(moments[:, t, :], stats[:, t, :]))
                    assert chain.count == LINKS // TT

                def ahead(dve, n, b, half, f):
                    if f in (1, 4, 7, 10):
                        t = (f - 1) // 3
                        dve.wait_ge(ctx_high, n * TT + t + 1)
                        dve.tensor_tensor(ctx_l[:, :, :], ctx_t[:, :, :], ctx_h[:, :, :].bitcast(F32), ALU.subtract
                                          ).then_inc(ctx_low, 1)
                    if f in (3, 6, 9, 12):
                        take(n, b, half, f // 3 - 1)
                    if f == 12:
                        dve.tensor_scalar(deviation[:, :], moments[:, :, 1], EPS, None, ALU.add
                                          ).then_inc(variance_ready, 1)
                    if f == 14:
                        dve.wait_ge(deviation_ready, n + 1)
                        dve.reciprocal(rstd[:, :], deviation[:, :]).then_inc(vec, 1)
                        dve.wait_ge(vec, (n + 1) * LINKS)
                        for t in range(TT):
                            own = normal[:, t, :]
                            dve.tensor_scalar(own, own if final else rows[:, half, t, :], moments[:, t, 0:1],
                                              rstd[:, t:t + 1], ALU.subtract, ALU.mult).then_inc(normed, 1)
                    if f == AFTER:
                        for c in range(DC):
                            dve.wait_ge(affine_high, n * DC + c + 1)
                            dve.tensor_tensor(xt_l[:, c, :], act_full[:, c % 2, :], xt_h[:, c, :].bitcast(F32),
                                              ALU.subtract).then_inc(affine_low, 1)

                def end(dve, n, b, half):
                    dve.wait_ge(outer_done, FC * (n + 1))
                    for t in range(TT):
                        row = rows[:, half, t, :]
                        if final:
                            dve.scalar_tensor_tensor(out=row, in0=psum[:, t, :], scalar=gate[:, bass.ds(b, 1)], in1=row,
                                                     op0=ALU.mult, op1=ALU.add).then_inc(finished, 1)
                        else:
                            dve.wait_ge(shifted, n * TT + t + 1)
                            dve.tensor_tensor(row, psum[:, t, :], row, ALU.add).then_inc(finished, 1)

                dve.wait_ge(constants_in, constants_all)
                if final:
                    dve.tensor_scalar(ungated[:, :], gate[:, :], -1.0, 1.0, ALU.mult, ALU.add).then_inc(ungated_made, 1)
                    dve.wait_ge(ungated_made, 1)
                schedule(dve, ahead, step, end, splits=lambda g: weights.low_parts(dve, g))


def program(nc, ins, out):
    Kernel(nc, ins, out).build()


def kernel(**inputs):
    import concourse.bacc as bacc
    from concourse.bass_utils import run_bass_kernel_spmd

    a = {k: np.asarray(v) for k, v in inputs.items()}
    columns = lambda v: np.ascontiguousarray(v.reshape(-1, P).T)
    l0 = lambda name: a["L0_cond_" + name]
    half = D // 2
    freqs = np.exp(np.arange(half, dtype=np.float32) * np.float32(-math.log(10000.0) / (half - 1)))
    data = {
        "x": a["x"].reshape(B * S, D),
        "x_T": a["x"].reshape(B * S, D).T,
        "timestep": a["itok_B_34_63"], "domain_id": a["itok_B_0_15"],
        "theta": a["condB_theta"], "phi": a["condB_phi"], "gate": a["condB_gatescore"],
        "bias": a["fside_Bx16xSxS_0"].reshape(B * H, S, S),
        "mask": a["mask_Bx1xSxS_bk0"].reshape(B, S, S).view(np.int32),
        "freqs": np.tile(columns(freqs), (1, 2)), "iota": np.arange(E, dtype=np.float32),
        "L0_down_WT": l0("down_W").T, "L0_down_b": l0("down_b").reshape(A, 1),
        "L0_up_WT": l0("up_W").T, "L0_up_b": l0("up_b"),
        "L0_expert_WT": l0("expert_W").transpose(2, 0, 1), "L0_expert_bT": l0("expert_b").T,
        "L0_domain_embT": l0("domain_emb").T, "L0_ln_gamma": l0("ln_gamma"), "L0_ln_beta": l0("ln_beta"),
    }
    for name in ("W_ada", "b_ada", "Wq", "Wk", "Wv", "Wo", "W1", "W2", "bo", "b2", "bv"):
        data["L2_" + name] = a["L2_cond_" + name]
    for name in ("Wq", "Wk", "Wv", "Wo", "W1", "W2", "bo", "b2", "bv"):
        data["L3_" + name] = a["L3_cond_" + name]
    for name in ("bq", "bk", "b1", "g2", "beta2"):
        data["L2_" + name] = columns(a["L2_cond_" + name])
    for name in ("bq", "bk", "b1", "gamma1", "beta1", "gamma2", "beta2"):
        data["L3_" + name] = columns(a["L3_cond_" + name])
    data = {k: np.ascontiguousarray(v) for k, v in data.items()}

    nc = bacc.Bacc("TRN2", target_bir_lowering=False, num_devices=1)
    ins = {k: nc.dram_tensor(k, v.shape, mybir.dt.from_np(v.dtype), kind="ExternalInput").ap() for k, v in data.items()}
    out = nc.dram_tensor("out", (B * S, D), F32, kind="ExternalOutput").ap()
    program(nc, ins, out)
    result = run_bass_kernel_spmd(nc, [data], core_ids=[0])
    return result.results[0]["out"].reshape(B, S, D)
```

```python
import math
from contextlib import ExitStack

import concourse.bass as bass
import concourse.mybir as mybir
import numpy as np

ALU = mybir.AluOpType
ACT = mybir.ActivationFunctionType
F32 = mybir.dt.float32
F32R = mybir.dt.float32r
BF16 = mybir.dt.bfloat16
I32 = mybir.dt.int32
U8 = mybir.dt.uint8

P = 128
B = 4
S = 1024
D = 512
A = 128
E = 16
H = 16
DH = D // H
F = 2048
DC = D // P
FC = F // P
TB = 512
TT = TB // P
NB = B * S // TB
BPS = S // TB
HG = P // DH
G = H // HG
NBG = B * G
KT = S // P
QP = S // 256
EPS = 1e-5
MASKED = -1e30
DMA = 16


def need(eng, semaphore, value):
    if isinstance(value, int) and value <= 0:
        return
    eng.wait_ge(semaphore, value)


def apart(eng):
    eng.nop(nofuse=True)


class Chain:

    def __init__(self, eng, semaphore, start=0):
        self.eng, self.semaphore, self.start, self.count = eng, semaphore, start, 0

    def link(self, instruction):
        instruction.then_inc(self.semaphore, 1)
        self.count += 1
        self.wait()

    def wait(self):
        self.eng.wait_ge(self.semaphore, self.start + self.count)


def product(pe, out, stationary, moving, first, last):
    (sh, sl), (mh, ml) = stationary, moving
    pe.matmul(out, sh, mh, start=first, stop=False)
    pe.matmul(out, sh, ml, start=False, stop=False)
    return pe.matmul(out, sl, mh, start=False, stop=last)


class Weights:

    def __init__(self, kernel, groups):
        self.groups, self.loaded, self.split = groups, kernel.weights_loaded, kernel.weights_split
        self.scaled, self.rounded = kernel.weights_scaled, kernel.weights_rounded
        self.loads_before = list(kernel.weight_loads)
        self.scales_before, self.before = kernel.weight_scales, kernel.weight_pieces
        for g, group in enumerate(groups):
            kernel.weight_loads[g] += len(group)
            kernel.weight_scales += sum(piece[4] != 1.0 for piece in group)
            kernel.weight_pieces += len(group)

    def until(self, g):
        return self.before + sum(len(group) for group in self.groups[:g + 1])

    def load(self, sp, g):
        for source, _, _, raw, _ in self.groups[g]:
            sp.dma_start(raw, source).then_inc(self.loaded[g], DMA)

    def high_parts(self, act, g):
        act.wait_ge(self.loaded[g], DMA * (self.loads_before[g] + len(self.groups[g])))
        scales = self.scales_before + sum(piece[4] != 1.0 for group in self.groups[:g] for piece in group)
        for _, high, _, raw, scale in self.groups[g]:
            if scale != 1.0:
                scales += 1
                act.activation(raw, raw, ACT.Copy, scale=scale).then_inc(self.scaled, 1)
                act.wait_ge(self.scaled, scales)
            act.activation(high, raw, ACT.Copy).then_inc(self.rounded, 1)

    def low_parts(self, dve, g):
        first = self.until(g) - len(self.groups[g])
        for i, (_, high, low, raw, _) in enumerate(self.groups[g]):
            dve.wait_ge(self.rounded, first + i + 1)
            dve.tensor_tensor(low, raw, high.bitcast(F32), ALU.subtract).then_inc(self.split, 1)


class Kernel:
    def __init__(self, nc, ins, out):
        self.nc, self.ins, self.out = nc, ins, out
        self.ctx = ExitStack()
        dram = lambda name, shape: nc.dram_tensor(name, shape, F32, kind="Internal").ap()
        self.rows = [dram(f"rows{n}", [B * S, D]) for n in range(2)]
        self.qk = [{n: dram(f"{n}{layer}", [B * D, S]) for n in ("qh", "ql", "kh", "kl")} for layer in range(2)]
        self.v = [dram(f"v{layer}", [NBG, S, P]) for layer in range(2)]
        self.attended = [dram(f"attended{layer}", [B * D, S]) for layer in range(2)]

    def constants_by(self, loads):
        self.constant_loads += loads
        return self.constants_in, DMA * self.constant_loads

    def split_tensor(self, memory, name, shape):
        high = memory.enter_context(self.nc.sbuf_tensor(f"{name}_h", shape, F32R))
        with self.nc.sbuf_tensor(f"{name}_raw", shape, F32) as raw:
            pass
        low = memory.enter_context(self.nc.sbuf_tensor(f"{name}_l", shape, F32R))
        return high, low, raw

    def sem(self, name):
        return self.ctx.enter_context(self.nc.semaphore(name))

    def build(self):
        nc = self.nc
        with self.ctx:
            sb = lambda name, shape, dt: self.ctx.enter_context(nc.sbuf_tensor(name, shape, dt))
            self.constants_in, self.constant_loads = self.sem("constants_in"), 0
            self.ada_moved = self.sem("ada_moved")
            self.weights_loaded = [self.sem(f"weights_loaded{g}") for g in range(5)]
            self.weights_scaled, self.weights_rounded = self.sem("weights_scaled"), self.sem("weights_rounded")
            self.weights_split = self.sem("weights_split")
            self.weight_loads, self.weight_scales, self.weight_pieces = [0] * 5, 0, 0
            self.ident = sb("ident", [P, P], F32)
            self.ident16 = sb("ident16", [P, P], BF16)
            self.psum = self.ctx.enter_context(nc.psum_tensor("psum", [P, 8, 512], F32))
            with ExitStack() as memory:
                self.constants(memory)
                self.front(memory)
            with ExitStack() as memory:
                self.attention(memory, 0)
            with ExitStack() as memory:
                self.feed_forward(memory, 0)
            with ExitStack() as memory:
                self.project(memory)
            with ExitStack() as memory:
                self.attention(memory, 1)
            with ExitStack() as memory:
                self.feed_forward(memory, 1)


    def constants(self, memory):
        nc, ins = self.nc, self.ins
        sb = lambda name, shape, dt=F32: memory.enter_context(nc.sbuf_tensor(name, shape, dt))
        self.scale1 = sb("ada_scale", [P, B, D])
        self.shift = sb("ada_shift", [P, B, D])
        self.rot_own = sb("rot_own", [P, B, D])
        self.rot_other = sb("rot_other", [P, B, D])
        self.rot_beta = sb("rot_beta", [P, B, D])
        self.expert_h = sb("expert_h", [P, B, A], F32R)
        self.expert_l = sb("expert_l", [P, B, A], F32R)
        self.expert_bias = sb("expert_bias", [P, B])
        NA = 4 * B + 2 * B
        with ExitStack() as own:
            tb = lambda name, shape, dt=F32: own.enter_context(nc.sbuf_tensor(f"const_{name}", shape, dt))
            w_ada = tb("w_ada", [P, DC, 2 * D])
            b_ada = tb("b_ada", [P, 2 * D])
            gamma = tb("gamma0", [P, D])
            beta = tb("beta0", [P, D])
            experts = tb("experts", [P, E, A])
            expert_b = tb("expert_b", [P, E])
            domain = tb("domain", [P, E])
            freqs = tb("freqs", [P, 4])
            iota = tb("iota", [P, E])
            steps_i = tb("steps_i", [P, B], I32)
            steps = tb("steps", [P, B])
            ids_i = tb("ids_i", [P, B], I32)
            ids = tb("ids", [P, B])
            clipped = tb("clipped", [P, B])
            valid = tb("valid", [P, B])
            valid2 = tb("valid2", [P, B])
            onehot = tb("onehot", [P, B, E])
            onehot_valid = tb("onehot_valid", [P, B, E])
            angle = tb("angle", [P, NA])
            turns = tb("turns", [P, NA])
            reduced = tb("reduced", [P, NA])
            flipped = tb("flipped", [P, NA])
            sine = tb("sine", [P, NA])
            cosine = tb("cosine", [P, NA])
            minus_sine = tb("minus_sine", [P, NA])
            emb = tb("emb", [P, 4, B])
            emb_act = tb("emb_act", [P, 4, B])
            ada = tb("ada", [P, 2, D])
            chosen = tb("chosen", [P, B, A])
            part = tb("part", [P, E])
            bsum = tb("bsum", [P, 2 * B])
            ident_steps = self.sem("ident_steps")
            vec = self.sem("const_vector")
            reduced_done = self.sem("angles_reduced")
            sines_done = self.sem("sines_done")
            emb_ready = self.sem("emb_ready")
            ada_done = self.sem("ada_products")
            ada_made = self.sem("ada_made")
            ada_dram = nc.dram_tensor("ada_rows", [B, 2 * D], F32, kind="Internal").ap()
            loads = [
                (steps_i[:, :], ins["timestep"].partition_broadcast(P)),
                (ids_i[:, :], ins["domain_id"].partition_broadcast(P)),
                (angle[:, 16:20], ins["theta"].partition_broadcast(P)),
                (angle[:, 20:24], ins["phi"].partition_broadcast(P)),
                (freqs[:, :], ins["freqs"]),
                (iota[:, :], ins["iota"].partition_broadcast(P)),
                (gamma[:, :], ins["L0_ln_gamma"].partition_broadcast(P)),
                (beta[:, :], ins["L0_ln_beta"].partition_broadcast(P)),
                (expert_b[:, :], ins["L0_expert_bT"]),
                (domain[:, :], ins["L0_domain_embT"]),
                (b_ada[:, :], ins["L2_b_ada"].partition_broadcast(P)),
            ]
            large_loads = [
                (experts[:, :, :], ins["L0_expert_WT"]),
                (w_ada[:, :, :], ins["L2_W_ada"].rearrange("(c p) n -> p c n", p=P)),
            ]
            loaded, all_loaded = self.constants_by(len(loads))
            large_in = self.weights_loaded[4]
            self.weight_loads[4] += len(large_loads)
            ident, ident16, psum = self.ident, self.ident16, self.psum
            lanes = lambda ap: ap.rearrange("p (n f) -> p n f", f=4)

            def rotation(b, lane):
                col = 16 + B * (lane // 2) + b
                return cosine[:, col:col + 1], (sine if lane % 2 == 0 else minus_sine)[:, col:col + 1]

            with nc.Block() as block:

                @block.sync
                def _(sp):
                    for dst, src in loads:
                        sp.dma_start(dst, src).then_inc(loaded, DMA)
                    for dst, src in large_loads:
                        sp.dma_start(dst, src).then_inc(large_in, DMA)
                    sp.wait_ge(ada_made, 2)
                    sp.dma_start(ada_dram, ada[0:B, :, :].rearrange("b h d -> b (h d)")).then_inc(self.ada_moved, DMA)
                    sp.wait_ge(self.ada_moved, DMA)
                    for at, dst in ((0, self.scale1), (D, self.shift)):
                        sp.dma_start(dst[:, :, :], ada_dram[:, at:at + D].partition_broadcast(P)
                                     ).then_inc(self.ada_moved, DMA)

                @block.gpsimd
                def _(pool):
                    pool.memset(ident[:, :], 0.0).then_inc(ident_steps, 1)
                    pool.memset(ident16[:, :], 0.0).then_inc(ident_steps, 1)
                    pool.wait_ge(ident_steps, 2)
                    for m in (ident, ident16):
                        pool.affine_select(out=m[:, :], in_=m[:, :], compare_op=ALU.not_equal, fill=1.0, base=0,
                                           pattern=[[-1, P]], channel_multiplier=1).then_inc(ident_steps, 1)
                    pool.wait_ge(loaded, all_loaded)
                    pool.wait_ge(sines_done, 3)
                    for b in range(B):
                        for lane in range(4):
                            cos, sin = rotation(b, lane)
                            for target, source_lane, factor in ((self.rot_own, lane, cos), (self.rot_other, lane ^ 1, sin)):
                                pool.tensor_scalar(lanes(target[:, b, :])[:, :, lane],
                                                   lanes(gamma[:, :])[:, :, source_lane], factor, 1.0, ALU.mult, ALU.mult)

                @block.vector
                def _(dve):
                    chain = Chain(dve, vec)
                    link = chain.link
                    dve.wait_ge(loaded, all_loaded)
                    dve.wait_ge(ident_steps, 4)
                    link(dve.tensor_copy(steps[:, :], steps_i[:, :]))
                    link(dve.tensor_scalar(steps[:, :], steps[:, :], 40.0, None, ALU.mult))
                    for b in range(B):
                        link(dve.tensor_scalar(angle[:, 0:16].rearrange("p (c b) -> p c b", b=B)[:, :, b],
                                               freqs[:, :], steps[:, b:b + 1], None, ALU.mult))
                    link(dve.tensor_scalar(turns[:, :], angle[:, :], 1 / (2 * math.pi), 12582912.0, ALU.mult, ALU.add))
                    link(dve.tensor_scalar(turns[:, :], turns[:, :], 12582912.0, None, ALU.subtract))
                    link(dve.scalar_tensor_tensor(out=reduced[:, :], in0=turns[:, :], scalar=-6.28125, in1=angle[:, :],
                                                  op0=ALU.mult, op1=ALU.add))
                    link(dve.scalar_tensor_tensor(out=reduced[:, :], in0=turns[:, :], scalar=-(2 * math.pi - 6.28125),
                                                  in1=reduced[:, :], op0=ALU.mult, op1=ALU.add))
                    link(dve.tensor_scalar(reduced[:, :], reduced[:, :], 3.1415925, -3.1415925, ALU.min, ALU.max))
                    link(dve.tensor_scalar(flipped[:, :], reduced[:, :], -1.0, None, ALU.mult))
                    link(dve.tensor_tensor(flipped[:, :], flipped[:, :], reduced[:, :], ALU.max))
                    dve.tensor_scalar(flipped[:, :], flipped[:, :], -1.0, math.pi / 2, ALU.mult,
                                      ALU.add).then_inc(reduced_done, 1)
                    link(dve.tensor_copy(ids[:, :], ids_i[:, :]))
                    link(dve.tensor_scalar(clipped[:, :], ids[:, :], 0.0, float(E - 1), ALU.max, ALU.min))
                    link(dve.tensor_tensor(valid[:, :], clipped[:, :], ids[:, :], ALU.is_equal))
                    link(dve.tensor_scalar(valid2[:, :], valid[:, :], -1.0, 1.0, ALU.mult, ALU.add))
                    for b in range(B):
                        link(dve.tensor_scalar(onehot[:, b, :], iota[:, :], clipped[:, b:b + 1], None, ALU.is_equal))
                        link(dve.tensor_scalar(onehot_valid[:, b, :], onehot[:, b, :], valid[:, b:b + 1], None,
                                               ALU.mult))
                        link(dve.tensor_scalar(chosen[:, b, :], ident[:, :], valid2[:, b:b + 1], None, ALU.mult))
                    dve.wait_ge(sines_done, 2)
                    link(dve.tensor_copy(emb[:, 0:2, :].rearrange("p c b -> p (c b)"), sine[:, 0:8]))
                    dve.tensor_copy(emb[:, 2:4, :].rearrange("p c b -> p (c b)"), cosine[:, 8:16]).then_inc(emb_ready, 1)
                    dve.wait_ge(large_in, DMA * len(large_loads))
                    for e in range(E):
                        for b in range(B):
                            last = dve.scalar_tensor_tensor(out=chosen[:, b, :], in0=experts[:, e, :],
                                                            scalar=onehot_valid[:, b, e:e + 1], in1=chosen[:, b, :],
                                                            op0=ALU.mult, op1=ALU.add)
                            last.then_inc(vec, 1)
                            chain.count += 1
                        chain.wait()
                    for b in range(B):
                        link(dve.tensor_copy(self.expert_h[:, b, :], chosen[:, b, :]))
                        link(dve.tensor_tensor(self.expert_l[:, b, :], chosen[:, b, :],
                                               self.expert_h[:, b, :].bitcast(F32), ALU.subtract))
                        link(dve.tensor_tensor_reduce(out=part[:, :], in0=expert_b[:, :], in1=onehot_valid[:, b, :],
                                                      scale=1.0, scalar=0.0, op0=ALU.mult, op1=ALU.add,
                                                      accum_out=bsum[:, b:b + 1]))
                        link(dve.tensor_tensor_reduce(out=part[:, :], in0=domain[:, :], in1=onehot[:, b, :],
                                                      scale=1.0, scalar=0.0, op0=ALU.mult, op1=ALU.add,
                                                      accum_out=bsum[:, B + b:B + b + 1]))
                    link(dve.tensor_tensor(self.expert_bias[:, :], bsum[:, 0:B], bsum[:, B:2 * B], ALU.add))
                    dve.wait_ge(sines_done, 3)
                    for b in range(B):
                        for lane in range(4):
                            cos, sin = rotation(b, lane)
                            own_b, other_b = lanes(beta[:, :])[:, :, lane], lanes(beta[:, :])[:, :, lane ^ 1]
                            target = lanes(self.rot_beta[:, b, :])[:, :, lane]
                            link(dve.tensor_scalar(target, own_b, cos, None, ALU.mult))
                            dve.scalar_tensor_tensor(out=target, in0=other_b, scalar=sin, in1=target,
                                                     op0=ALU.mult, op1=ALU.add)
                        if b == 0:
                            dve.wait_ge(ada_done, 1)
                            dve.scalar_tensor_tensor(out=ada[0:B, 0, :], in0=psum[0:B, 0, :], scalar=1.0,
                                                     in1=b_ada[0:B, 0:D], op0=ALU.add, op1=ALU.add).then_inc(ada_made, 1)
                            dve.tensor_tensor(ada[0:B, 1, :], psum[0:B, 1, :], b_ada[0:B, D:2 * D], ALU.add
                                              ).then_inc(ada_made, 1)

                @block.scalar
                def _(act):
                    act.wait_ge(reduced_done, 1)
                    act.activation(sine[:, :], reduced[:, :], ACT.Sin).then_inc(sines_done, 1)
                    act.activation(cosine[:, :], flipped[:, :], ACT.Sin).then_inc(sines_done, 1)
                    act.wait_ge(sines_done, 1)
                    act.activation(minus_sine[:, :], sine[:, :], ACT.Copy, scale=-1.0).then_inc(sines_done, 1)
                    act.wait_ge(emb_ready, 1)
                    act.activation(emb_act[:, :, :], emb[:, :, :], ACT.Silu).then_inc(sines_done, 1)

                @block.tensor
                def _(pe):
                    pe.wait_ge(large_in, DMA * len(large_loads))
                    pe.wait_ge(sines_done, 4)
                    for half in range(2):
                        for c in range(DC):
                            mm = pe.matmul(psum[0:B, half, :], emb_act[:, c, :], w_ada[:, c, D * half:D * (half + 1)],
                                           start=c == 0, stop=c == DC - 1)
                    mm.then_inc(ada_done, 1)



    def attention(self, memory, layer):
        nc, psum, ident, ident16 = self.nc, self.psum, self.ident, self.ident16
        causal = layer == 1
        qk, v_dram, attended = self.qk[layer], self.v[layer], self.attended[layer]
        U = 8 * QP
        phases = [(3, 0), (2, 1)] if causal else [(0,), (1,), (2,), (3,)]
        WIDE = len(phases[0])
        NU = 8 * WIDE

        def place(u):
            phase, at = divmod(u, NU)
            return phase, phases[phase][at % WIDE], at // WIDE // 2, at // WIDE % 2

        def keys(u):
            _, pair, _, half = place(u)
            return 2 * pair + half + 1 if causal else KT

        SCORE, BIAS, EXP, INVERT, NORM = (6, 5, 4, 3, 2) if causal else (4, 3, 2, 2, 1)
        SLOTS = 4 if causal else 2
        halves = lambda u: (keys(u) + 3) // 4
        by_dve = lambda u, half: half == 1 or causal and keys(u) < 4
        turn_bank = lambda u, half: TURN[half if WIDE == 1 or u % WIDE == 0 else 2]
        copies = lambda u, dve: sum(by_dve(x, half) == dve for x in range(u) for half in range(halves(x)))
        sb = lambda name, shape, dt=F32: memory.enter_context(nc.sbuf_tensor(f"{name}{layer}", shape, dt))
        q_stack = sb("q_stack", [P, HG, S], F32R)
        k_stack = sb("k_stack", [P, HG, S], F32R)
        values = sb("values", [P, KT, P])
        shifted = sb("shifted", [P, SLOTS, S])
        least = sb("least", [P, 8])
        weights = sb("weights", [P, SLOTS, S])
        total = sb("total", [P, 8])
        inverse = sb("inverse", [P, 8])
        normal = sb("normal", [P, SLOTS, S])
        base = lambda pair: next((2 * (ph[0] + 1) if causal and pair == ph[-1] else 0) for ph in phases if pair in ph)
        turned = sb("turned", [P, 2, HG, 10 if causal else KT, 256])
        result = sb("result", [P, 2, 256])
        v_bias = sb("v_bias", [P, NBG])
        constants_in, constants_all = self.constants_by(B)
        if causal:
            ahead = sb("ahead", [P, S])
        else:
            NBIAS = 4
            bias = sb("bias", [P, NBIAS, S])
            mask_u8 = sb("mask_u8", [P, KT, S], U8)
            mask = sb("mask", [P, KT, S], BF16)

        sem = lambda name: self.sem(f"{name}{layer}")
        qk_in = [sem(f"qk_in{j}") for j in range(HG)]
        values_in = sem("values_in")
        bias_in = [sem(f"bias_in{i}") for i in range(4)] if not causal else None
        mask_in, mask_made = sem("mask_in"), sem("mask_made")
        scored = sem("scored")
        biased = sem("biased")
        exped = sem("exped")
        inverted = sem("inverted")
        normed = sem("normed")
        transposed = sem("transposed")
        act_out = sem("act_out")
        dve_out = sem("dve_out")
        weighted = sem("weighted")
        result_out = sem("result_out")
        stored = [sem(f"attended_stored{i}") for i in range(2)]
        QK_DMAS = 8
        PIECES = 11 if causal else 5
        SCORES = (0, 2)
        TURN = (4, 5, 3)
        WEIGHT = (6, 7)

        def ahead_of(it, u, by):
            over, u2 = divmod(u + by, U)
            it2 = it + over
            return it2, u2, it2 * U + u2

        def copied(it, u, dve):
            return it * copies(U, dve) + copies(u, dve)

        def transposes_before(it, u):
            return copied(it, u, True) + copied(it, u, False)

        def turns(body):
            def run(eng):
                body(eng, 0, True, False)
                with eng.Fori(1, NBG - 1) as it:
                    body(eng, it, False, False)
                body(eng, NBG - 1, False, True)
            return run

        with nc.Block() as block:

            @block.sync
            def _(sp):
                def load_head(it, j):
                    for group in range(4):
                        part = slice(DH * group, DH * (group + 1))
                        rows = bass.ds(it * P + DH * j, DH)
                        q = qk["qh" if group < 2 else "ql"]
                        k = qk["kh" if group % 2 == 0 else "kl"]
                        sp.dma_start(q_stack[part, j, :].bitcast(F32), q[rows, :]).then_inc(qk_in[j], DMA)
                        sp.dma_start(k_stack[part, j, :].bitcast(F32), k[rows, :]).then_inc(qk_in[j], DMA)

                def load_values(it):
                    sp.dma_start(values[:, :, :],
                                 v_dram[it].rearrange("(k p) f -> p k f", p=P)).then_inc(values_in, DMA)

                def load_bias(it, u, number):
                    if causal:
                        return
                    need(sp, biased, number - 3)
                    _, pair, j, half = place(u)
                    tile, head = 2 * pair + half, 4 * it + j
                    sp.dma_start(bias[:, u % 4, :], self.ins["bias"][head, P * tile:P * (tile + 1), :]
                                 ).then_inc(bias_in[u % 4], DMA)

                def load_mask(it):
                    sp.dma_start(mask_u8[:, :, :].bitcast(I32), self.ins["mask"][it // G].rearrange("(t p) k -> p t k", p=P)
                                 ).then_inc(mask_in, DMA)

                def store(it, number):
                    pair = phases[number // WIDE][number % WIDE]
                    sp.wait_ge(result_out, it * QP + number + 1)
                    apart(sp)
                    sp.dma_start(attended[bass.ds(it * P, P), 256 * pair:256 * (pair + 1)],
                                 result[:, number % 2, :]).then_inc(stored[number % 2], DMA)

                def next_head(it, j):
                    sp.wait_ge(scored, (it - 1) * U + U - NU + 2 * WIDE * (j + 1))
                    apart(sp)
                    load_head(it, j)

                def next_values(it):
                    sp.wait_ge(weighted, it * QP)
                    apart(sp)
                    load_values(it)

                def body(sp, it, first, last):
                    for u in range(U):
                        if causal:
                            if u >= U - NU and u % 4 == 0 and not last:
                                next_head(it + 1, (u - (U - NU)) // 4)
                            if u % NU == PIECES:
                                for which in range(WIDE):
                                    if u >= NU:
                                        store(it, (u // NU - 1) * WIDE + which)
                                    elif not first:
                                        store(it - 1, QP - WIDE + which)
                            if u == PIECES and not first:
                                next_values(it)
                            continue
                        if not (first and u < 4):
                            load_bias(it, u, it * U + u)
                        if u in (29, 31) and not last:
                            next_head(it + 1, (u - 29) // 2)
                        if u in (1, 3) and not first:
                            next_head(it, 2 + (u - 1) // 2)
                        if u == 12 and not first:
                            next_values(it)
                        if u == 8 and not last:
                            sp.wait_ge(mask_made, KT * (it + 1))
                            load_mask(it + 1)
                        if u % 8 == 5:
                            pair = u // 8 - 2
                            if pair >= 0:
                                store(it, pair)
                            elif not first:
                                store(it - 1, pair + QP)

                if not causal:
                    load_mask(0)
                for j in range(HG):
                    load_head(0, j)
                    if j < 2:
                        for u in (2 * j, 2 * j + 1):
                            load_bias(0, u, u)
                load_values(0)
                for b in range(B):
                    sp.dma_start(v_bias[:, G * b:G * (b + 1)], self.ins[f"L{3 if causal else 2}_bv"]
                                 ).then_inc(constants_in, DMA)
                turns(body)(sp)
                for number in range(QP - 2, QP):
                    store(NBG - 1, number)
                for i in range(2):
                    sp.wait_ge(stored[i], DMA * NBG * QP // 2)

            @block.tensor
            def _(pe):
                def scores(it, u, number):
                    phase, pair, j, half = place(u)
                    tile, n = 2 * pair + half, keys(u) * P
                    if phase == 0 and half == 0 and u % WIDE == 0:
                        pe.wait_ge(qk_in[j], DMA * QK_DMAS * (it + 1))
                    need(pe, biased, number - 1)
                    if not causal and j == 0:
                        pe.wait_ge(mask_made, it * KT + tile + 1)
                    bank = SCORES[u % 2]
                    spans = [(at, min(at + 512, n)) for at in range(0, n, 512)]
                    if not causal:
                        for i, (at, to) in enumerate(spans):
                            pe.matmul(psum[:, bank + i, 0:to - at], ident16[:, :], mask[:, tile, at:to], start=True,
                                      stop=False)
                    for i, (at, to) in enumerate(spans):
                        mm = pe.matmul(psum[:, bank + i, 0:to - at], q_stack[:, j, P * tile:P * (tile + 1)],
                                       k_stack[:, j, at:to], start=causal, stop=True)
                    mm.then_inc(scored, 1)

                def transpose(it, u, number):
                    pe.wait_ge(normed, number + 1)
                    for half in range(halves(u)):
                        by, what = 1, None
                        while what is None:
                            turn2, u2, _ = ahead_of(it, u, -by)
                            what = next((h for h in range(halves(u2)) if turn_bank(u2, h) == turn_bank(u, half)), None)
                            by += 1
                        dve = by_dve(u2, what)
                        need(pe, dve_out if dve else act_out,
                             copied(turn2, u2, dve) + sum(by_dve(u2, h) == dve for h in range(what + 1)))
                        tiles = range(4 * half, min(4 * half + 4, keys(u)))
                        for k in tiles:
                            at = P * (k - tiles[0])
                            mm = pe.transpose(psum[:, turn_bank(u, half), at:at + P], normal[:, u % SLOTS, P * k:P * (k + 1)],
                                              ident[:, :])
                        mm.then_inc(transposed, 1)

                def weigh(it, phase, piece):
                    if piece == 0:
                        for dve in (False, True):
                            need(pe, dve_out if dve else act_out, copied(it, NU * (phase + 1), dve))
                        if phase == 0:
                            pe.wait_ge(values_in, DMA * (it + 1))
                    tiles = lambda pair: 2 * (pair + 1) if causal else KT
                    parts = [(which, pair, k) for which, pair in enumerate(phases[phase]) for k in range(tiles(pair))]
                    for which, pair, k in parts[len(parts) * piece // PIECES:len(parts) * (piece + 1) // PIECES]:
                        number = phase * WIDE + which
                        if k == 0:
                            need(pe, result_out, it * QP + number - 1)
                        at = P if causal and k == tiles(pair) - 1 else 0
                        for j in range(HG):
                            mm = pe.matmul(psum[DH * j:DH * (j + 1), WEIGHT[number % 2], at:256],
                                           values[:, k, DH * j:DH * (j + 1)],
                                           turned[:, phase % 2, j, base(pair) + k, at:256],
                                           start=k == 0, stop=k == tiles(pair) - 1,
                                           tile_position=(0, DH * j))
                        if k == tiles(pair) - 1:
                            mm.then_inc(weighted, 1)

                def body(pe, it, first, last):
                    for u in range(U):
                        transpose(it, u, it * U + u)
                        if not (last and u + SCORE >= U):
                            scores(*ahead_of(it, u, SCORE))
                        if u % NU < PIECES:
                            if u >= NU:
                                weigh(it, u // NU - 1, u % NU)
                            elif not first:
                                weigh(it - 1, len(phases) - 1, u % NU)

                for u in range(SCORE):
                    scores(0, u, u)
                turns(body)(pe)
                for piece in range(PIECES):
                    weigh(NBG - 1, len(phases) - 1, piece)

            @block.vector
            def _(dve):
                def add_bias(it, u, number):
                    n = keys(u) * P
                    dve.wait_ge(scored, number + 1)
                    need(dve, exped, number + 1 - SLOTS)
                    if causal:
                        what = ahead[:, S - n:S]
                    else:
                        dve.wait_ge(bias_in[u % 4], DMA * (it * (U // 4) + u // 4 + 1))
                        what = bias[:, u % 4, 0:n]
                    bank = SCORES[u % 2]
                    apart(dve)
                    dve.tensor_tensor_reduce(
                        out=shifted[:, u % SLOTS, 0:n], in0=psum[:, bank:bank + 2, :].rearrange("p b n -> p (b n)")[:, 0:n],
                        in1=what, scale=-1.0, scalar=3e38, op0=ALU.add, op1=ALU.min,
                        accum_out=least[:, u % 8:u % 8 + 1]).then_inc(biased, 1)

                def copy_transposed(it, u, number):
                    phase, pair, j, half_of_pair = place(u)
                    for half in range(halves(u)):
                        if not by_dve(u, half):
                            continue
                        dve.wait_ge(transposed, transposes_before(it, u) + half + 1)
                        need(dve, weighted, it * QP + (phase - 1) * WIDE)
                        n, at = min(keys(u) - 4 * half, 4), base(pair) + 4 * half
                        dve.tensor_copy(turned[:, phase % 2, j, at:at + n, P * half_of_pair:P * (half_of_pair + 1)],
                                        psum[:, turn_bank(u, half), 0:P * n].rearrange("p (k q) -> p k q", k=n)
                                        ).then_inc(dve_out, 1)

                def invert(it, u, number):
                    dve.wait_ge(exped, number + 1)
                    dve.reciprocal(inverse[:, u % 8:u % 8 + 1], total[:, u % 8:u % 8 + 1]).then_inc(inverted, 1)

                def body(dve, it, first, last):
                    for u in range(U):
                        if not (last and u + BIAS >= U):
                            add_bias(*ahead_of(it, u, BIAS))
                        copy_transposed(it, u, it * U + u)
                        if not (last and u + INVERT >= U):
                            invert(*ahead_of(it, u, INVERT))

                if causal:
                    dve.wait_ge(mask_made, 2)
                for u in range(BIAS):
                    add_bias(0, u, u)
                for u in range(INVERT):
                    invert(0, u, u)
                turns(body)(dve)

            @block.scalar
            def _(act):
                def exponentiate(it, u, number):
                    n = keys(u) * P
                    act.wait_ge(biased, number + 1)
                    need(act, normed, number + 1 - SLOTS)
                    act.activation(weights[:, u % SLOTS, 0:n], shifted[:, u % SLOTS, 0:n], ACT.Exp,
                                   bias=least[:, u % 8:u % 8 + 1], scale=-1.0,
                                   accum_out=total[:, u % 8:u % 8 + 1]).then_inc(exped, 1)

                def copy_transposed(it, u, number):
                    if by_dve(u, 0):
                        return
                    phase, pair, j, half = place(u)
                    act.wait_ge(transposed, transposes_before(it, u) + 1)
                    need(act, weighted, it * QP + (phase - 1) * WIDE)
                    n, at = min(keys(u), 4), base(pair)
                    act.activation(turned[:, phase % 2, j, at:at + n, P * half:P * (half + 1)],
                                   psum[:, turn_bank(u, 0), 0:P * n].rearrange("p (k q) -> p k q", k=n),
                                   ACT.Copy).then_inc(act_out, 1)

                def take_result(it, number):
                    if isinstance(it, int) and it == 0 and number == 0:
                        act.wait_ge(constants_in, constants_all)
                    act.wait_ge(weighted, it * QP + number + 1)
                    need(act, stored[number % 2], DMA * (it * (QP // 2) + number // 2))
                    apart(act)
                    act.activation(result[:, number % 2, :], psum[:, WEIGHT[number % 2], 0:256], ACT.Identity,
                                   bias=v_bias[:, bass.ds(it, 1)]).then_inc(result_out, 1)

                def body(act, it, first, last):
                    for u in range(U):
                        if not (last and u + EXP >= U):
                            exponentiate(*ahead_of(it, u, EXP))
                        copy_transposed(it, u, it * U + u)
                        if u % NU == PIECES:
                            for which in range(WIDE):
                                if u >= NU:
                                    take_result(it, (u // NU - 1) * WIDE + which)
                                elif not first:
                                    take_result(it - 1, QP - WIDE + which)

                for u in range(EXP):
                    exponentiate(0, u, u)
                turns(body)(act)
                for number in range(QP - WIDE, QP):
                    take_result(NBG - 1, number)

            @block.gpsimd
            def _(pool):
                def normalise(it, u, number):
                    n = keys(u) * P
                    pool.wait_ge(inverted, number + 1)
                    _, u0, _ = ahead_of(0, u, -SLOTS)
                    before = transposes_before(it + (u - SLOTS) // U, u0) + halves(u0)
                    need(pool, transposed, before)
                    apart(pool)
                    pool.tensor_scalar(normal[:, u % SLOTS, 0:n], weights[:, u % SLOTS, 0:n], inverse[:, u % 8:u % 8 + 1],
                                       1.0, ALU.mult, ALU.mult).then_inc(normed, 1)

                def make_mask(it, tile):
                    if tile == 0:
                        pool.wait_ge(mask_in, DMA * (it + 1))
                    apart(pool)
                    pool.tensor_scalar(mask[:, tile, :], mask_u8[:, tile, :], MASKED, 1.0, ALU.mult,
                                       ALU.mult).then_inc(mask_made, 1)

                def body(pool, it, first, last):
                    for u in range(U):
                        if not (last and u + NORM >= U):
                            normalise(*ahead_of(it, u, NORM))
                        if u % 8 >= 6 and not causal and not last:
                            pool.wait_ge(scored, it * U + u + 1)
                            make_mask(it + 1, 2 * (u // 8) + u % 2)

                if causal:
                    pool.memset(ahead[:, :], 0.0).then_inc(mask_in, 1)
                    pool.wait_ge(mask_in, 1)
                    pool.affine_select(out=ahead[:, S - P:S], in_=ahead[:, S - P:S], compare_op=ALU.is_ge,
                                       fill=MASKED, base=0, pattern=[[-1, P]],
                                       channel_multiplier=1).then_inc(mask_made, 2)
                else:
                    for tile in range(KT):
                        make_mask(0, tile)
                for u in range(NORM):
                    normalise(0, u, u)
                turns(body)(pool)


    def projection(self, memory, layer):
        psum = self.psum
        sb = lambda name, shape, dt=F32: memory.enter_context(self.nc.sbuf_tensor(f"{name}{layer}", shape, dt))
        sem = lambda name: self.sem(f"{name}{layer}")
        w = {}
        for name in "qkv":
            w[name] = self.split_tensor(memory, f"w{name}{layer}", [P, DC, D])
        xt = [(sb(f"xt_h_{i}_", [P, DC, TB], F32R), sb(f"xt_l_{i}_", [P, DC, TB], F32R)) for i in range(2)]
        qk_bias = sb("qk_bias", [P, 2 * DC])
        out_h = sb("out_h", [P, 2, TB], F32)
        out_l = sb("out_l", [P, 2, TB], F32)
        out_v = sb("out_v", [P, 2, D], F32)
        projected = sem("projected")
        high_out = sem("high_out")
        taken = sem("taken")
        values_out = sem("values_out")
        qk_stored = [sem(f"qk_stored{i}") for i in range(2)]
        v_stored = [sem(f"v_stored{i}") for i in range(2)]
        xt_low = sem("xt_low")
        BANKS = (6, 7)
        qk, v = self.qk[layer], self.v[layer]

        class Pieces:
            pass

        def weight_groups(prefix):
            return [[(self.ins[f"{prefix}W{which}"].rearrange("(c p) n -> p c n", p=P),
                      *(part[:, :, :] for part in w[which]), 1 / math.sqrt(DH) if which == "q" else 1.0)]
                    for which in "qkv"]

        def pe(pe, n, half, i):
            if isinstance(n, int) and n == 0 and i % 4 == 0:
                weights = pieces.weights
                pe.wait_ge(weights.split, weights.until(len(weights.groups) - 3 + i // 4))
            if i == 0:
                pe.wait_ge(xt_low, DC * (n + 1))
            if 2 <= i < 10:
                pe.wait_ge(taken, 8 * n + i - 1)
            else:
                need(pe, values_out, 4 * n + (i - 9 if i >= 10 else i - 1))
            out = psum[:, BANKS[i % 2], :]
            h, l = xt[half]
            for c in range(DC):
                if i < 8:
                    wh, wl, _ = w["qk"[i // 4]]
                    at = slice(P * (i % 4), P * (i % 4 + 1))
                    mm = product(pe, out, (wh[:, c, at], wl[:, c, at]), (h[:, c, :], l[:, c, :]), c == 0, c == DC - 1)
                else:
                    wh, wl, _ = w["v"]
                    at = slice(P * (i - 8), P * (i - 7))
                    mm = product(pe, out, (h[:, c, at], l[:, c, at]), (wh[:, c, :], wl[:, c, :]), c == 0, c == DC - 1)
            mm.then_inc(projected, 1)

        def act(act, n, half, i):
            act.wait_ge(projected, 12 * n + i + 1)
            if i >= 8:
                need(act, v_stored[i % 2], DMA * (2 * n + (i - 8) // 2))
                act.activation(out_v[:, i % 2, :], psum[:, BANKS[i % 2], :], ACT.Copy).then_inc(values_out, 1)
                return
            need(act, qk_stored[i % 2], 2 * DMA * (4 * n + i // 2))
            act.activation(out_h[:, i % 2, :].bitcast(F32R), psum[:, BANKS[i % 2], :], ACT.Identity,
                           bias=qk_bias[:, i:i + 1]).then_inc(high_out, 1)

        def dve(dve, n, half, i):
            bank = psum[:, BANKS[i % 2], :]
            if i < 8:
                dve.wait_ge(high_out, 8 * n + i + 1)
                dve.scalar_tensor_tensor(out=out_l[:, i % 2, :], in0=bank, scalar=qk_bias[:, i:i + 1],
                                         in1=out_h[:, i % 2, :], op0=ALU.add, op1=ALU.subtract).then_inc(taken, 1)

        def sp(sp, n, b, half, i):
            if i < 8:
                sp.wait_ge(taken, 8 * n + i + 1)
                rows = bass.ds(b * D + P * (i % 4), P)
                for part, src in (("h", out_h), ("l", out_l)):
                    sp.dma_start(qk["qk"[i // 4] + part][rows, TB * half:TB * (half + 1)],
                                 src[:, i % 2, :]).then_inc(qk_stored[i % 2], DMA)
            else:
                sp.wait_ge(values_out, 4 * n + i - 7)
                at = TB * half + P * (i - 8)
                sp.dma_start(v[bass.ds(b * G, G), at:at + P, :].rearrange("g p d -> p g d"),
                             out_v[:, i % 2, :].rearrange("p (g d) -> p g d", g=G)).then_inc(v_stored[i % 2], DMA)

        def sp_end(sp):
            for i in range(2):
                sp.wait_ge(qk_stored[i], 2 * DMA * 4 * NB)
                sp.wait_ge(v_stored[i], DMA * 2 * NB)

        pieces = Pieces()
        pieces.pe, pieces.act, pieces.dve, pieces.sp, pieces.sp_end = pe, act, dve, sp, sp_end
        pieces.xt, pieces.xt_low, pieces.projected = xt, xt_low, projected
        pieces.bias_scaled = sem("bias_scaled")
        pieces.weight_groups, pieces.qk_bias = weight_groups, qk_bias
        return pieces


    def front(self, memory):
        nc, ins, psum, ident = self.nc, self.ins, self.psum, self.ident
        sb = lambda name, shape, dt=F32: memory.enter_context(nc.sbuf_tensor(name, shape, dt))
        sem = self.sem
        proj = self.projection(memory, 0)
        down = self.split_tensor(memory, "down", [P, DC, A])
        up = self.split_tensor(memory, "up", [P, D])
        weights = proj.weights = Weights(self, [
            [(ins["L0_down_WT"].rearrange("(c p) a -> p c a", p=P), *(part[:, :, :] for part in down), 1.0),
             (ins["L0_up_WT"], *(part[:, :] for part in up), 1.0)]] + proj.weight_groups("L2_"))
        x_t = sb("x_t", [P, DC, TB])
        x_th, x_tl = sb("x_th", [P, DC, TB], F32R), sb("x_tl", [P, DC, TB], F32R)
        x_rows = sb("x_rows", [P, TT, D])
        y = sb("y", [P, TT, D])
        hidden = sb("hidden", [P, TB])
        hidden_h, hidden_l = sb("hidden_h", [P, TB], F32R), sb("hidden_l", [P, TB], F32R)
        mixed_h, mixed_l = sb("mixed_h", [P, TB], F32R), sb("mixed_l", [P, TB], F32R)
        expert = (sb("expert_now_h", [P, A], F32R), sb("expert_now_l", [P, A], F32R))
        scratch = sb("front_scratch", [P, 2, D])
        down_b, up_b = sb("down_b", [P, 1]), sb("up_b", [P, D])
        stats = sb("front_stats", [P, TT, 6])
        moments = sb("front_moments", [P, 2, TT, 2])
        deviation = sb("front_deviation", [P, 2, TT])
        rstd = sb("front_rstd", [P, 2, TT])

        biases_in, biases_all = self.constants_by(4)
        x_t_in, rows_in = sem("x_t_in"), sem("x_rows_in")
        x_high, x_low = sem("x_high"), sem("x_low")
        rows_biased = sem("rows_biased")
        down_done, hidden_made = sem("down_done"), sem("hidden_made")
        hidden_high, hidden_low = sem("hidden_high"), sem("hidden_low")
        expert_staged, expert_done = sem("expert_staged"), sem("expert_done")
        mixed_high, mixed_low = sem("mixed_high"), sem("mixed_low")
        up_done, up_taken = sem("up_done"), sem("up_taken")
        variance_ready, deviation_ready = sem("variance_ready"), sem("deviation_ready")
        vec = sem("front_vector")
        LINKS = 2 * 2 * TT + 2 + 5 * TT + TT
        rows_ready = sem("front_rows_ready")
        rows_stored = sem("front_rows_stored")
        turned, xt_high = sem("front_turned"), sem("front_xt_high")
        xt_low = proj.xt_low

        def ends(n):
            return tuple(isinstance(n, int) and n == edge for edge in (0, NB - 1))

        def after(n, b, half):
            return n + 1, b if half + 1 < BPS else b + 1

        with nc.Block() as block:

            def schedule(eng, front, project, splits=lambda g: None, at=5):
                splits(0)
                front(eng, 0, 0, 0, lambda k: splits(k - at + 1) if at <= k < at + 3 else None)

                def body(eng, i):
                    for half in range(BPS):
                        n = i * BPS + half
                        b, half2 = (i, half + 1) if half + 1 < BPS else (i + 1, 0)
                        front(eng, n + 1, b, half2, lambda k: project(eng, n, i, half, k))
                body(eng, 0)
                with eng.Fori(1, B - 1) as i:
                    body(eng, i)
                i, n = B - 1, (B - 1) * BPS
                front(eng, n + 1, i, 1, lambda k: project(eng, n, i, 0, k))
                for k in range(12):
                    project(eng, n + 1, i, 1, k)

            @block.sync
            def _(sp):
                sp.dma_start(down_b[:, :], ins["L0_down_b"]).then_inc(biases_in, DMA)
                sp.dma_start(up_b[:, :], ins["L0_up_b"].partition_broadcast(P)).then_inc(biases_in, DMA)
                sp.dma_start(proj.qk_bias[:, 0:DC], ins["L2_bq"]).then_inc(biases_in, DMA)
                sp.dma_start(proj.qk_bias[:, DC:2 * DC], ins["L2_bk"]).then_inc(biases_in, DMA)

                def load_transposed(sp, n):
                    tokens = bass.ds(n * TB, TB)
                    need(sp, x_low, n)
                    sp.dma_start(x_t[:, :, :], ins["x_T"].rearrange("(c p) t -> p c t", p=P)[:, :, tokens]
                                 ).then_inc(x_t_in, DMA)

                def load_rows(sp, n):
                    tokens = bass.ds(n * TB, TB)
                    need(sp, up_taken, n * TT)
                    sp.dma_start(x_rows[:, :, :], ins["x"][tokens, :].rearrange("(t p) d -> p t d", p=P)
                                 ).then_inc(rows_in, DMA)

                def front(sp, n, b, half, project):
                    more = not (isinstance(n, int) and n == NB - 1)
                    for k in range(10):
                        project(k)
                        if k == 1 and more:
                            load_transposed(sp, n + 1)
                        if k == 5 and more:
                            load_rows(sp, n + 1)
                    for t in range(TT):
                        sp.wait_ge(rows_ready, n * TT + t + 1)
                        sp.dma_start(self.rows[0][bass.ds(n * TB + t * P, P), :], y[:, t, :]).then_inc(rows_stored, DMA)
                        if t < 2:
                            project(10 + t)

                weights.load(sp, 0)
                load_transposed(sp, 0)
                load_rows(sp, 0)
                for g in range(1, 4):
                    weights.load(sp, g)
                schedule(sp, front, proj.sp)
                proj.sp_end(sp)
                sp.wait_ge(rows_stored, DMA * TT * NB)

            @block.tensor
            def _(pe):
                def down_product(n):
                    pe.wait_ge(x_low, n + 1)
                    need(pe, hidden_made, n)
                    for c in range(DC):
                        mm = product(pe, psum[:, 0, :], (down[0][:, c, :], down[1][:, c, :]), (x_th[:, c, :], x_tl[:, c, :]),
                                     c == 0, c == DC - 1)
                    mm.then_inc(down_done, 1)

                def expert_product(n):
                    pe.wait_ge(hidden_low, n + 1)
                    pe.wait_ge(expert_staged, 2 * (n + 1))
                    need(pe, mixed_low, n)
                    product(pe, psum[:, 1, :], (expert[0][:, :], expert[1][:, :]), (hidden_h[:, :], hidden_l[:, :]),
                            True, True).then_inc(expert_done, 1)

                def front(pe, n, b, half, project):
                    first, last = ends(n)
                    if first:
                        pe.wait_ge(weights.split, weights.until(0))
                        down_product(n)
                        expert_product(n)
                    pe.wait_ge(mixed_low, n + 1)
                    for t in range(TT):
                        need(pe, up_taken, n * TT + t - 1)
                        at = slice(P * t, P * (t + 1))
                        product(pe, psum[:, 2 + t % 2, :], (mixed_h[:, at], mixed_l[:, at]), (up[0][:, :], up[1][:, :]),
                                True, True).then_inc(up_done, 1)
                        if t >= 1:
                            project(t - 1)
                    for k in range(3, 8):
                        project(k)
                    if not last:
                        down_product(n + 1)
                    project(8)
                    if not last:
                        expert_product(n + 1)
                    for k in range(9, 12):
                        project(k)
                    pe.wait_ge(rows_ready, TT * (n + 1))
                    for c in range(DC):
                        need(pe, xt_low, n * DC + c - 1)
                        for t in range(TT):
                            mm = pe.transpose(psum[:, 4 + c % 2, P * t:P * (t + 1)], y[:, t, P * c:P * (c + 1)],
                                              ident[:, :])
                        mm.then_inc(turned, 1)

                schedule(pe, front, lambda pe, n, b, half, k: proj.pe(pe, n, half, k))

            @block.scalar
            def _(act):
                def split_input(act, n):
                    act.wait_ge(x_t_in, DMA * (n + 1))
                    need(act, down_done, n)
                    act.activation(x_th[:, :, :], x_t[:, :, :], ACT.Copy).then_inc(x_high, 1)

                def take_hidden(n):
                    act.wait_ge(down_done, n + 1)
                    need(act, hidden_low, n)
                    act.activation(hidden[:, :], psum[:, 0, :], ACT.Gelu, bias=down_b[:, 0:1]).then_inc(hidden_made, 1)
                    act.wait_ge(hidden_made, n + 1)
                    need(act, expert_done, n)
                    act.activation(hidden_h[:, :], hidden[:, :], ACT.Copy).then_inc(hidden_high, 1)

                def take_mixed(n, b):
                    act.wait_ge(expert_done, n + 1)
                    need(act, up_done, n * TT)
                    apart(act)
                    act.activation(mixed_h[:, :], psum[:, 1, :], ACT.Identity,
                                   bias=self.expert_bias[:, bass.ds(b, 1)]).then_inc(mixed_high, 1)

                def deviation_of(n, i):
                    act.wait_ge(variance_ready, 2 * n + i + 1)
                    act.activation(deviation[:, i, :], deviation[:, i, :], ACT.Sqrt).then_inc(deviation_ready, 1)

                def front(act, n, b, half, project):
                    first, last = ends(n)
                    if first:
                        split_input(act, n)
                        take_hidden(n)
                        take_mixed(n, b)
                    for k in range(3):
                        project(k)
                    deviation_of(n, 0)
                    project(3)
                    if not last:
                        split_input(act, n + 1)
                    for k in range(4, 8):
                        project(k)
                    if not last:
                        take_hidden(n + 1)
                    project(8)
                    if not last:
                        take_mixed(*after(n, b, half))
                    deviation_of(n, 1)
                    for k in range(9, 12):
                        project(k)
                    for c in range(DC):
                        act.wait_ge(turned, n * DC + c + 1)
                        if c == 0:
                            need(act, proj.projected, 12 * (n - 1))
                        act.activation(proj.xt[half][0][:, c, :], psum[:, 4 + c % 2, :], ACT.Copy).then_inc(xt_high, 1)

                act.wait_ge(biases_in, biases_all)
                act.wait_ge(proj.bias_scaled, 1)
                schedule(act, front, lambda act, n, b, half, k: proj.act(act, n, half, k),
                         lambda g: weights.high_parts(act, g))

            @block.gpsimd
            def _(pool):
                def split_input(pool, n):
                    pool.wait_ge(x_high, n + 1)
                    need(pool, down_done, n)
                    pool.tensor_tensor(x_tl[:, :, :], x_t[:, :, :], x_th[:, :, :].bitcast(F32), ALU.subtract
                                       ).then_inc(x_low, 1)

                def stage_expert(n, b):
                    need(pool, expert_done, n)
                    apart(pool)
                    pool.tensor_copy(expert[0][:, :], self.expert_h[:, b, :].bitcast(F32)).then_inc(expert_staged, 1)
                    pool.tensor_copy(expert[1][:, :], self.expert_l[:, b, :].bitcast(F32)).then_inc(expert_staged, 1)

                def front(pool, n, b, half, project):
                    first, last = ends(n)
                    if first:
                        split_input(pool, n)
                        stage_expert(n, b)
                    pool.wait_ge(rows_in, DMA * (n + 1))
                    for t in range(TT):
                        pool.tensor_tensor(x_rows[:, t, :], x_rows[:, t, :], up_b[:, :], ALU.add
                                           ).then_inc(rows_biased, 1)
                    if not last:
                        split_input(pool, n + 1)
                        stage_expert(*after(n, b, half))

                pool.wait_ge(biases_in, biases_all)
                schedule(pool, front, lambda *a: None)

            @block.vector
            def _(dve):
                def front(dve, n, b, half, project):
                    chain = Chain(dve, vec, n * LINKS)
                    link = chain.link

                    def moments_of(i, t):
                        link(dve.bn_stats(stats[:, t, :], y[:, t, :]))
                        apart(dve)
                        link(dve.bn_aggr(moments[:, i, t, :], stats[:, t, :]))

                    def variance(i):
                        dve.tensor_scalar(deviation[:, i, :], moments[:, i, :, 1], EPS, None, ALU.add
                                          ).then_inc(variance_ready, 1)

                    def inverse_deviation(i):
                        dve.wait_ge(deviation_ready, 2 * n + i + 1)
                        link(dve.reciprocal(rstd[:, i, :], deviation[:, i, :]))

                    def split_hidden(n):
                        dve.wait_ge(hidden_high, n + 1)
                        dve.tensor_tensor(hidden_l[:, :], hidden[:, :], hidden_h[:, :].bitcast(F32), ALU.subtract
                                          ).then_inc(hidden_low, 1)

                    def split_mixed(n, b):
                        dve.wait_ge(mixed_high, n + 1)
                        dve.scalar_tensor_tensor(out=mixed_l[:, :], in0=psum[:, 1, :],
                                                 scalar=self.expert_bias[:, bass.ds(b, 1)],
                                                 in1=mixed_h[:, :].bitcast(F32), op0=ALU.add, op1=ALU.subtract
                                                 ).then_inc(mixed_low, 1)

                    first, last = ends(n)
                    if first:
                        split_hidden(n)
                        split_mixed(n, b)
                    need(dve, turned, n * DC)
                    need(dve, rows_stored, DMA * TT * n)
                    for t in range(TT):
                        dve.wait_ge(up_done, n * TT + t + 1)
                        dve.wait_ge(rows_biased, n * TT + t + 1)
                        dve.tensor_tensor(y[:, t, :], psum[:, 2 + t % 2, :], x_rows[:, t, :], ALU.add
                                          ).then_inc(up_taken, 1)
                        dve.wait_ge(up_taken, n * TT + t + 1)
                        moments_of(0, t)
                        if t in (1, 3):
                            project(t // 2)
                    variance(0)
                    project(2)
                    inverse_deviation(0)
                    for t in range(TT):
                        mean = moments[:, 0, t, 0:1]
                        own, other = scratch[:, 0, :], scratch[:, 1, :]
                        pairs = lambda ap: ap.rearrange("p (n two) -> p n two", two=2)
                        dve.scalar_tensor_tensor(out=own, in0=y[:, t, :], scalar=mean, in1=self.rot_own[:, b, :],
                                                 op0=ALU.subtract, op1=ALU.mult).then_inc(vec, 1)
                        chain.count += 1
                        for lane in range(2):
                            dve.scalar_tensor_tensor(out=pairs(other)[:, :, lane], in0=pairs(y[:, t, :])[:, :, 1 - lane],
                                                     scalar=mean, in1=pairs(self.rot_other[:, b, :])[:, :, lane],
                                                     op0=ALU.subtract, op1=ALU.mult).then_inc(vec, 1)
                            chain.count += 1
                        if t < 3:
                            project(3 + 2 * t)
                        chain.wait()
                        link(dve.tensor_tensor(own, own, other, ALU.add))
                        link(dve.scalar_tensor_tensor(out=y[:, t, :], in0=own, scalar=rstd[:, 0, t:t + 1],
                                                      in1=self.rot_beta[:, b, :], op0=ALU.mult, op1=ALU.add))
                        moments_of(1, t)
                        if t < 2:
                            project(4 + 2 * t)
                    if not last:
                        split_hidden(n + 1)
                    variance(1)
                    if not last:
                        split_mixed(*after(n, b, half))
                    project(8)
                    inverse_deviation(1)
                    for t in range(TT):
                        shifted = scratch[:, t % 2, :]
                        if t == 0 and isinstance(n, int) and n == 0:
                            dve.wait_ge(self.ada_moved, 3 * DMA)
                        link(dve.scalar_tensor_tensor(out=shifted, in0=y[:, t, :], scalar=moments[:, 1, t, 0:1],
                                                      in1=self.scale1[:, b, :], op0=ALU.subtract, op1=ALU.mult))
                        dve.scalar_tensor_tensor(out=y[:, t, :], in0=shifted, scalar=rstd[:, 1, t:t + 1],
                                                 in1=self.shift[:, b, :], op0=ALU.mult, op1=ALU.add
                                                 ).then_inc(rows_ready, 1)
                    for c in range(DC):
                        dve.wait_ge(xt_high, n * DC + c + 1)
                        dve.tensor_tensor(proj.xt[half][1][:, c, :], psum[:, 4 + c % 2, :],
                                          proj.xt[half][0][:, c, :].bitcast(F32), ALU.subtract).then_inc(xt_low, 1)
                    project(9)
                    project(10)
                    assert chain.count == LINKS, chain.count

                dve.wait_ge(biases_in, biases_all)
                dve.tensor_scalar(proj.qk_bias[:, 0:DC], proj.qk_bias[:, 0:DC], 1 / math.sqrt(DH), None, ALU.mult
                                  ).then_inc(proj.bias_scaled, 1)
                dve.wait_ge(proj.bias_scaled, 1)
                schedule(dve, front, lambda dve, n, b, half, k: proj.dve(dve, n, half, k),
                         lambda g: weights.low_parts(dve, g), at=8)


    def project(self, memory):
        nc, ins, psum, ident = self.nc, self.ins, self.psum, self.ident
        sb = lambda name, shape, dt=F32: memory.enter_context(nc.sbuf_tensor(name, shape, dt))
        sem = self.sem
        proj = self.projection(memory, 1)
        weights = proj.weights = Weights(self, proj.weight_groups("L3_"))
        rows = sb("project_rows", [P, 2, TT, D])
        gamma, beta = sb("project_gamma", [P, DC]), sb("project_beta", [P, DC])
        affine = sb("project_affine", [P, 2, TB])
        stats = sb("project_stats", [P, TT, 6])
        moments = sb("project_moments", [P, TT, 2])
        deviation, rstd = sb("project_deviation", [P, TT]), sb("project_rstd", [P, TT])
        constants_in, constants_all = self.constants_by(4)
        rows_in = [sem(f"project_rows_in{i}") for i in range(2)]
        variance_ready, deviation_ready = sem("project_variance"), sem("project_deviation_ready")
        normed = sem("project_normed")
        turned = sem("project_turned")
        affine_made, high = sem("project_affine_made"), sem("project_high")
        vec = sem("project_vector")
        LINKS = 2 * TT + 1
        xt_low = proj.xt_low

        with nc.Block() as block:

            def schedule(eng, front, project, splits=lambda g: None, at=5):
                front(eng, 0, 0, 0, lambda k: splits(k - at) if at <= k < at + 3 else None)

                def body(eng, i):
                    for half in range(BPS):
                        n = i * BPS + half
                        front(eng, n + 1, i + half, 1 - half, lambda k: project(eng, n, i, half, k))
                body(eng, 0)
                with eng.Fori(1, B - 1) as i:
                    body(eng, i)
                i, n = B - 1, (B - 1) * BPS
                front(eng, n + 1, i, 1, lambda k: project(eng, n, i, 0, k))
                for k in range(12):
                    project(eng, n + 1, i, 1, k)

            @block.sync
            def _(sp):
                def load_weights(g):
                    if g == 0:
                        for dst, src in ((gamma[:, :], ins["L3_gamma1"]), (beta[:, :], ins["L3_beta1"]),
                                         (proj.qk_bias[:, 0:DC], ins["L3_bq"]), (proj.qk_bias[:, DC:2 * DC], ins["L3_bk"])):
                            sp.dma_start(dst, src).then_inc(constants_in, DMA)
                    weights.load(sp, g)

                def front(sp, n, turn, half, project):
                    need(sp, turned, DC * (n - 1))
                    sp.dma_start(rows[:, half, :, :],
                                 self.rows[1][bass.ds(n * TB, TB), :].rearrange("(t p) d -> p t d", p=P)
                                 ).then_inc(rows_in[half], DMA)
                    for k in range(12):
                        project(k)

                schedule(sp, front, proj.sp, load_weights)
                proj.sp_end(sp)

            @block.vector
            def _(dve):
                def front(dve, n, turn, half, project):
                    chain = Chain(dve, vec, n * LINKS)
                    link = chain.link
                    project(0)
                    dve.wait_ge(rows_in[half], DMA * (turn + 1))
                    for t in range(TT):
                        link(dve.bn_stats(stats[:, t, :], rows[:, half, t, :]))
                        apart(dve)
                        link(dve.bn_aggr(moments[:, t, :], stats[:, t, :]))
                        project(1 + t)
                    need(dve, deviation_ready, n)
                    dve.tensor_scalar(deviation[:, :], moments[:, :, 1], EPS, None, ALU.add).then_inc(variance_ready, 1)
                    project(5)
                    dve.wait_ge(deviation_ready, n + 1)
                    link(dve.reciprocal(rstd[:, :], deviation[:, :]))
                    for t in range(TT):
                        dve.tensor_scalar(rows[:, half, t, :], rows[:, half, t, :], moments[:, t, 0:1], rstd[:, t:t + 1],
                                          ALU.subtract, ALU.mult).then_inc(normed, 1)
                        if t < 2:
                            project(6 + t)
                    for k in range(8, 11):
                        project(k)
                    for c in range(DC):
                        dve.wait_ge(high, n * DC + c + 1)
                        dve.tensor_tensor(proj.xt[half][1][:, c, :], affine[:, c % 2, :],
                                          proj.xt[half][0][:, c, :].bitcast(F32), ALU.subtract).then_inc(xt_low, 1)
                    assert chain.count == LINKS

                def splits(g):
                    if g == 0:
                        dve.wait_ge(constants_in, constants_all)
                        dve.tensor_scalar(proj.qk_bias[:, 0:DC], proj.qk_bias[:, 0:DC], 1 / math.sqrt(DH), None,
                                          ALU.mult).then_inc(proj.bias_scaled, 1)
                    weights.low_parts(dve, g)

                schedule(dve, front, lambda dve, n, b, half, k: proj.dve(dve, n, half, k), splits, at=8)

            @block.scalar
            def _(act):
                def front(act, n, turn, half, project):
                    for k in range(5):
                        project(k)
                    act.wait_ge(variance_ready, n + 1)
                    act.activation(deviation[:, :], deviation[:, :], ACT.Sqrt).then_inc(deviation_ready, 1)
                    for k in range(5, 9):
                        project(k)
                    for c in range(DC):
                        act.wait_ge(turned, n * DC + c + 1)
                        need(act, xt_low, n * DC + c - 1)
                        act.activation(affine[:, c % 2, :], psum[:, 4 + c % 2, :], ACT.Identity, bias=beta[:, c:c + 1],
                                       scale=gamma[:, c:c + 1]).then_inc(affine_made, 1)
                        if c < 3:
                            project(9 + c)

                def splits(g):
                    if g == 0:
                        act.wait_ge(constants_in, constants_all)
                        act.wait_ge(proj.bias_scaled, 1)
                    weights.high_parts(act, g)

                schedule(act, front, lambda act, n, b, half, k: proj.act(act, n, half, k), splits)

            @block.gpsimd
            def _(pool):
                def front(pool, n, turn, half, project):
                    for c in range(DC):
                        pool.wait_ge(affine_made, n * DC + c + 1)
                        if c == 0:
                            need(pool, proj.projected, 12 * (n - 1))
                        apart(pool)
                        pool.tensor_scalar(proj.xt[half][0][:, c, :], affine[:, c % 2, :], 1.0, 1.0, ALU.mult,
                                           ALU.mult).then_inc(high, 1)

                schedule(pool, front, lambda *a: None)

            @block.tensor
            def _(pe):
                def front(pe, n, turn, half, project):
                    for k in range(9):
                        project(k)
                    pe.wait_ge(normed, TT * (n + 1))
                    for c in range(DC):
                        need(pe, affine_made, n * DC + c - 1)
                        for t in range(TT):
                            mm = pe.transpose(psum[:, 4 + c % 2, P * t:P * (t + 1)], rows[:, half, t, P * c:P * (c + 1)],
                                              ident[:, :])
                        mm.then_inc(turned, 1)
                        if c < 3:
                            project(9 + c)

                schedule(pe, front, lambda pe, n, b, half, k: proj.pe(pe, n, half, k))


    def feed_forward(self, memory, layer):
        nc, ins, psum, ident = self.nc, self.ins, self.psum, self.ident
        final = layer == 1
        pre = "L3_" if final else "L2_"
        sb = lambda name, shape, dt=F32: memory.enter_context(nc.sbuf_tensor(f"ff_{name}{layer}", shape, dt))
        sem = lambda name: self.sem(f"ff_{name}{layer}")
        wo, w1, w2 = (self.split_tensor(memory, f"ff_{name}{layer}", shape) for name, shape in
                      (("wo", [P, DC, D]), ("w1", [P, DC, F]), ("w2", [P, FC, D])))
        chunks = lambda name: ins[pre + name].rearrange("(c p) n -> p c n", p=P)
        groups = [[(chunks("Wo"), *(part[:, :, :] for part in wo), 1.0)]]
        for g in range(FC // 4):
            inner_at, outer_at = slice(4 * P * g, 4 * P * (g + 1)), slice(4 * g, 4 * (g + 1))
            groups.append([(chunks("W1")[:, :, inner_at], *(part[:, :, inner_at] for part in w1), 1.0),
                           (chunks("W2")[:, outer_at, :], *(part[:, outer_at, :] for part in w2), 1.0)])
        weights = Weights(self, groups)
        ctx_t = sb("ctx_t", [P, DC, P])
        ctx_h, ctx_l = sb("ctx_h", [P, DC, P], F32R), sb("ctx_l", [P, DC, P], F32R)
        xt_h, xt_l = sb("xt_h", [P, DC, TB], F32R), sb("xt_l", [P, DC, TB], F32R)
        rows = sb("rows", [P, 2, TT, D])
        normal = sb("normal", [P, TT, D])
        act_full = sb("act_full", [P, 2, TB])
        act_h, act_l = sb("act_h", [P, 2, TB], F32R), sb("act_l", [P, 2, TB], F32R)
        bo, b2 = sb("bo", [P, D]), sb("b2", [P, D])
        b1, gamma, beta = sb("b1", [P, FC]), sb("gamma", [P, DC]), sb("beta", [P, DC])
        gate, ungated = sb("gate", [P, B]), sb("ungated", [P, B])
        stats, moments = sb("stats", [P, TT, 6]), sb("moments", [P, TT, 2])
        deviation, rstd = sb("deviation", [P, TT]), sb("rstd", [P, TT])
        ungated_made = sem("ungated_made") if final else None
        ctx_in, rows_in = sem("ctx_in"), [sem(f"rows_in{i}") for i in range(2)]
        ctx_high, ctx_low = sem("ctx_high"), sem("ctx_low")
        out_done, out_taken = sem("out_done"), sem("out_taken")
        rows_biased = None if final else sem("rows_biased")
        variance_ready, deviation_ready = sem("variance_ready"), sem("deviation_ready")
        normed, turned = sem("normed"), sem("turned")
        affine_made, affine_high, affine_low = sem("affine_made"), sem("affine_high"), sem("affine_low")
        inner_done = sem("inner_done")
        act_made, act_high, act_low = sem("act_made"), sem("act_high"), sem("act_low")
        outer_done = sem("outer_done")
        shifted = None if final else sem("shifted")
        finished = sem("finished")
        stored = sem("stored")
        vec = sem("vector")
        LINKS = (5 if final else 2) * TT + 1
        source = self.rows[1] if final else self.rows[0]
        target = self.out if final else self.rows[1]
        constants = [(bo[:, :], ins[pre + "bo"].partition_broadcast(P)), (b2[:, :], ins[pre + "b2"].partition_broadcast(P)),
                     (b1[:, :], ins[pre + "b1"]), (gamma[:, :], ins[pre + ("gamma2" if final else "g2")]),
                     (beta[:, :], ins[pre + "beta2"])]
        if final:
            constants.append((gate[:, :], ins["gate"].partition_broadcast(P)))
        constants_in, constants_all = self.constants_by(len(constants))
        INNER, TURN, OUTPUT = (4, 5), (6, 7), 7
        AFTER = FC

        with nc.Block() as block:

            def schedule(eng, ahead, step, end=lambda *a: None, splits=lambda g: None):
                def body(eng, i, half, last):
                    n = i * BPS + half
                    next_b, next_half = (i, half + 1) if half + 1 < BPS else (i + 1, 0)
                    first = isinstance(n, int) and n == 0
                    for f in range(FC):
                        if first and f % 4 == 0 and f // 4 + 2 < len(groups):
                            splits(f // 4 + 2)
                        step(eng, n, i, half, f)
                        if not last:
                            ahead(eng, n + 1, next_b, next_half, f)
                    if not last:
                        ahead(eng, n + 1, next_b, next_half, AFTER)
                    end(eng, n, i, half)

                splits(0)
                for f in range(FC):
                    ahead(eng, 0, 0, 0, f)
                    if f == 12:
                        splits(1)
                ahead(eng, 0, 0, 0, AFTER)
                for half in range(BPS):
                    body(eng, 0, half, False)
                with eng.Fori(1, B - 1) as i:
                    for half in range(BPS):
                        body(eng, i, half, False)
                for half in range(BPS):
                    body(eng, B - 1, half, half == BPS - 1)

            @block.sync
            def _(sp):
                def load_rows(sp, n, b, half):
                    need(sp, stored, DMA * TT * (n - 1))
                    sp.dma_start(rows[:, half, :, :],
                                 source[bass.ds(n * TB, TB), :].rearrange("(t p) d -> p t d", p=P)
                                 ).then_inc(rows_in[half], DMA)

                def load_ctx(sp, n, b, half, t):
                    need(sp, ctx_low, n * TT + t)
                    at = TB * half + P * t
                    sp.dma_start(ctx_t[:, :, :], self.attended[layer][bass.ds(b * D, D), at:at + P]
                                 .rearrange("(c p) t -> p c t", p=P)).then_inc(ctx_in, DMA)

                def ahead(sp, n, b, half, f):
                    if f == 0:
                        load_ctx(sp, n, b, half, 0)
                        if isinstance(n, int) and n == 0:
                            weights.load(sp, 0)
                            for dst, src in constants:
                                sp.dma_start(dst, src).then_inc(constants_in, DMA)
                        load_rows(sp, n, b, half)
                    if f in (1, 4, 7):
                        load_ctx(sp, n, b, half, (f + 2) // 3)
                        if isinstance(n, int) and n == 0 and f > 1:
                            weights.load(sp, f // 3)

                def end(sp, n, b, half):
                    for t in range(TT):
                        sp.wait_ge(finished, n * TT + t + 1)
                        sp.dma_start(target[bass.ds(n * TB + P * t, P), :], rows[:, half, t, :]).then_inc(stored, DMA)

                schedule(sp, ahead, lambda *a: None, end, splits=lambda g: weights.load(sp, g) if g > 2 else None)
                sp.wait_ge(stored, DMA * TT * NB)

            @block.tensor
            def _(pe):
                def inner(n, f):
                    if f == 0:
                        pe.wait_ge(affine_low, DC * (n + 1))
                    need(pe, act_made, n * FC + f - 1)
                    if isinstance(n, int) and n == 0 and f % 4 == 0:
                        pe.wait_ge(weights.split, weights.until(1 + f // 4))
                    at = slice(P * f, P * (f + 1))
                    for c in range(DC):
                        mm = product(pe, psum[:, INNER[f % 2], :], (w1[0][:, c, at], w1[1][:, c, at]),
                                     (xt_h[:, c, :], xt_l[:, c, :]), c == 0, c == DC - 1)
                    mm.then_inc(inner_done, 1)

                def outer(n, f):
                    pe.wait_ge(act_low, n * FC + f + 1)
                    for t in range(TT):
                        if f == 0:
                            need(pe, finished, (n - 1) * TT + t + 1)
                        at = slice(P * t, P * (t + 1))
                        mm = product(pe, psum[:, t, :], (act_h[:, f % 2, at], act_l[:, f % 2, at]),
                                     (w2[0][:, f, :], w2[1][:, f, :]), f == 0, f == FC - 1)
                    mm.then_inc(outer_done, 1)

                def output(n, t):
                    if isinstance(n, int) and n == 0 and t == 0:
                        pe.wait_ge(weights.split, weights.until(0))
                    pe.wait_ge(ctx_low, n * TT + t + 1)
                    need(pe, out_taken, n * TT + t)
                    if t == 0:
                        need(pe, affine_made, n * DC)
                    for c in range(DC):
                        mm = product(pe, psum[:, OUTPUT, :], (ctx_h[:, c, :], ctx_l[:, c, :]),
                                     (wo[0][:, c, :], wo[1][:, c, :]), c == 0, c == DC - 1)
                    mm.then_inc(out_done, 1)

                def turn(n, c):
                    if c == 0:
                        pe.wait_ge(normed, TT * (n + 1))
                    need(pe, affine_made, n * DC + c - 1)
                    for t in range(TT):
                        mm = pe.transpose(psum[:, TURN[c % 2], P * t:P * (t + 1)], normal[:, t, P * c:P * (c + 1)],
                                          ident[:, :])
                    mm.then_inc(turned, 1)

                def step(pe, n, b, half, f):
                    inner(n, f)
                    if 1 <= f < FC - 1:
                        outer(n, f - 1)

                def ahead(pe, n, b, half, f):
                    if f in (2, 5, 8, 11):
                        output(n, (f - 2) // 3)
                    if f == FC - 1:
                        turn(n, 0)
                        turn(n, 1)
                        if not (isinstance(n, int) and n == 0):
                            outer(n - 1, FC - 2)
                    if f == AFTER:
                        turn(n, 2)
                        turn(n, 3)

                def end(pe, n, b, half):
                    if isinstance(n, int) and n == NB - 1:
                        outer(n, FC - 2)
                    outer(n, FC - 1)

                schedule(pe, ahead, step, end)

            @block.scalar
            def _(act):
                def step(act, n, b, half, f):
                    act.wait_ge(inner_done, n * FC + f + 1)
                    if f < 2:
                        act.wait_ge(affine_low, DC * (n + 1))
                    need(act, act_low, n * FC + f - 1)
                    act.activation(act_full[:, f % 2, :], psum[:, INNER[f % 2], :],
                                   ACT.Gelu if final else ACT.Gelu_apprx_sigmoid, bias=b1[:, f:f + 1]
                                   ).then_inc(act_made, 1)

                def ahead(act, n, b, half, f):
                    if f in (1, 4, 7, 10):
                        t = (f - 1) // 3
                        act.wait_ge(ctx_in, DMA * (n * TT + t + 1))
                        need(act, out_done, n * TT + t)
                        act.activation(ctx_h[:, :, :], ctx_t[:, :, :], ACT.Copy).then_inc(ctx_high, 1)
                    if f == 13:
                        act.wait_ge(variance_ready, n + 1)
                        act.activation(deviation[:, :], deviation[:, :], ACT.Sqrt).then_inc(deviation_ready, 1)
                    if f == AFTER:
                        for c in range(DC):
                            act.wait_ge(turned, n * DC + c + 1)
                            if c < 2:
                                need(act, act_low, n * FC + c - 1)
                            need(act, affine_low, n * DC + c - 1)
                            act.activation(act_full[:, c % 2, :], psum[:, TURN[c % 2], :], ACT.Identity,
                                           bias=beta[:, c:c + 1], scale=gamma[:, c:c + 1]).then_inc(affine_made, 1)

                act.wait_ge(constants_in, constants_all)
                schedule(act, ahead, step, splits=lambda g: weights.high_parts(act, g))

            @block.gpsimd
            def _(pool):
                def step(pool, n, b, half, f):
                    pool.wait_ge(act_made, n * FC + f + 1)
                    need(pool, outer_done, n * FC + f - 1)
                    apart(pool)
                    pool.tensor_scalar(act_h[:, f % 2, :], act_full[:, f % 2, :], 1.0, 1.0, ALU.mult, ALU.mult
                                       ).then_inc(act_high, 1)
                    if not final and 5 <= f < 5 + TT:
                        t = f - 5
                        pool.wait_ge(normed, TT * (n + 1))
                        pool.tensor_tensor(rows[:, half, t, :], rows[:, half, t, :], b2[:, :], ALU.add
                                           ).then_inc(shifted, 1)

                def ahead(pool, n, b, half, f):
                    if not final and f in (1, 3, 5, 7):
                        if f == 1:
                            pool.wait_ge(rows_in[half], DMA * (b + 1))
                        t = f // 2
                        pool.tensor_tensor(rows[:, half, t, :], rows[:, half, t, :], bo[:, :], ALU.add
                                           ).then_inc(rows_biased, 1)
                    if f == AFTER:
                        for c in range(DC):
                            pool.wait_ge(affine_made, n * DC + c + 1)
                            if c == 0:
                                need(pool, inner_done, n * FC)
                            apart(pool)
                            pool.tensor_scalar(xt_h[:, c, :], act_full[:, c % 2, :], 1.0, 1.0, ALU.mult, ALU.mult
                                               ).then_inc(affine_high, 1)

                pool.wait_ge(constants_in, constants_all)
                schedule(pool, ahead, step)

            @block.vector
            def _(dve):
                def step(dve, n, b, half, f):
                    dve.wait_ge(act_high, n * FC + f + 1)
                    dve.tensor_tensor(act_l[:, f % 2, :], act_full[:, f % 2, :], act_h[:, f % 2, :].bitcast(F32),
                                      ALU.subtract).then_inc(act_low, 1)

                def take(n, b, half, t):
                    row, own = rows[:, half, t, :], normal[:, t, :]
                    chain = Chain(dve, vec, n * LINKS + t * (LINKS // TT))
                    link = chain.link
                    dve.wait_ge(out_done, n * TT + t + 1)
                    if t == 0:
                        need(dve, turned, n * DC)
                    if final:
                        if t == 0:
                            dve.wait_ge(rows_in[half], DMA * (b + 1))
                        dve.tensor_tensor(own, psum[:, OUTPUT, :], bo[:, :], ALU.add).then_inc(out_taken, 1)
                        dve.wait_ge(out_taken, n * TT + t + 1)
                        link(dve.scalar_tensor_tensor(out=row, in0=own, scalar=gate[:, bass.ds(b, 1)], in1=row,
                                                      op0=ALU.mult, op1=ALU.add))
                        link(dve.scalar_tensor_tensor(out=own, in0=own, scalar=ungated[:, bass.ds(b, 1)], in1=row,
                                                      op0=ALU.mult, op1=ALU.add))
                        link(dve.scalar_tensor_tensor(out=row, in0=b2[:, :], scalar=gate[:, bass.ds(b, 1)], in1=row,
                                                      op0=ALU.mult, op1=ALU.add))
                        link(dve.bn_stats(stats[:, t, :], own))
                    else:
                        dve.wait_ge(rows_biased, n * TT + t + 1)
                        dve.tensor_tensor(row, psum[:, OUTPUT, :], row, ALU.add).then_inc(out_taken, 1)
                        dve.wait_ge(out_taken, n * TT + t + 1)
                        link(dve.bn_stats(stats[:, t, :], row))
                    apart(dve)
                    link(dve.bn_aggr(moments[:, t, :], stats[:, t, :]))
                    assert chain.count == LINKS // TT

                def ahead(dve, n, b, half, f):
                    if f in (1, 4, 7, 10):
                        t = (f - 1) // 3
                        dve.wait_ge(ctx_high, n * TT + t + 1)
                        dve.tensor_tensor(ctx_l[:, :, :], ctx_t[:, :, :], ctx_h[:, :, :].bitcast(F32), ALU.subtract
                                          ).then_inc(ctx_low, 1)
                    if f in (3, 6, 9, 12):
                        take(n, b, half, f // 3 - 1)
                    if f == 12:
                        dve.tensor_scalar(deviation[:, :], moments[:, :, 1], EPS, None, ALU.add
                                          ).then_inc(variance_ready, 1)
                    if f == 14:
                        dve.wait_ge(deviation_ready, n + 1)
                        dve.reciprocal(rstd[:, :], deviation[:, :]).then_inc(vec, 1)
                        dve.wait_ge(vec, (n + 1) * LINKS)
                        for t in range(TT):
                            own = normal[:, t, :]
                            dve.tensor_scalar(own, own if final else rows[:, half, t, :], moments[:, t, 0:1],
                                              rstd[:, t:t + 1], ALU.subtract, ALU.mult).then_inc(normed, 1)
                    if f == AFTER:
                        for c in range(DC):
                            dve.wait_ge(affine_high, n * DC + c + 1)
                            dve.tensor_tensor(xt_l[:, c, :], act_full[:, c % 2, :], xt_h[:, c, :].bitcast(F32),
                                              ALU.subtract).then_inc(affine_low, 1)

                def end(dve, n, b, half):
                    dve.wait_ge(outer_done, FC * (n + 1))
                    for t in range(TT):
                        row = rows[:, half, t, :]
                        if final:
                            dve.scalar_tensor_tensor(out=row, in0=psum[:, t, :], scalar=gate[:, bass.ds(b, 1)], in1=row,
                                                     op0=ALU.mult, op1=ALU.add).then_inc(finished, 1)
                        else:
                            dve.wait_ge(shifted, n * TT + t + 1)
                            dve.tensor_tensor(row, psum[:, t, :], row, ALU.add).then_inc(finished, 1)

                dve.wait_ge(constants_in, constants_all)
                if final:
                    dve.tensor_scalar(ungated[:, :], gate[:, :], -1.0, 1.0, ALU.mult, ALU.add).then_inc(ungated_made, 1)
                    dve.wait_ge(ungated_made, 1)
                schedule(dve, ahead, step, end, splits=lambda g: weights.low_parts(dve, g))


def program(nc, ins, out):
    Kernel(nc, ins, out).build()


def kernel(**inputs):
    import concourse.bacc as bacc
    from concourse.bass_utils import run_bass_kernel_spmd

    a = {k: np.asarray(v) for k, v in inputs.items()}
    columns = lambda v: np.ascontiguousarray(v.reshape(-1, P).T)
    l0 = lambda name: a["L0_cond_" + name]
    half = D // 2
    freqs = np.exp(np.arange(half, dtype=np.float32) * np.float32(-math.log(10000.0) / (half - 1)))
    data = {
        "x": a["x"].reshape(B * S, D),
        "x_T": a["x"].reshape(B * S, D).T,
        "timestep": a["itok_B_34_63"], "domain_id": a["itok_B_0_15"],
        "theta": a["condB_theta"], "phi": a["condB_phi"], "gate": a["condB_gatescore"],
        "bias": a["fside_Bx16xSxS_0"].reshape(B * H, S, S),
        "mask": a["mask_Bx1xSxS_bk0"].reshape(B, S, S).view(np.int32),
        "freqs": np.tile(columns(freqs), (1, 2)), "iota": np.arange(E, dtype=np.float32),
        "L0_down_WT": l0("down_W").T, "L0_down_b": l0("down_b").reshape(A, 1),
        "L0_up_WT": l0("up_W").T, "L0_up_b": l0("up_b"),
        "L0_expert_WT": l0("expert_W").transpose(2, 0, 1), "L0_expert_bT": l0("expert_b").T,
        "L0_domain_embT": l0("domain_emb").T, "L0_ln_gamma": l0("ln_gamma"), "L0_ln_beta": l0("ln_beta"),
    }
    for name in ("W_ada", "b_ada", "Wq", "Wk", "Wv", "Wo", "W1", "W2", "bo", "b2"):
        data["L2_" + name] = a["L2_cond_" + name]
    for name in ("Wq", "Wk", "Wv", "Wo", "W1", "W2", "bo", "b2"):
        data["L3_" + name] = a["L3_cond_" + name]
    for name in ("bq", "bk", "bv", "b1", "g2", "beta2"):
        data["L2_" + name] = columns(a["L2_cond_" + name])
    for name in ("bq", "bk", "bv", "b1", "gamma1", "beta1", "gamma2", "beta2"):
        data["L3_" + name] = columns(a["L3_cond_" + name])
    data = {k: np.ascontiguousarray(v) for k, v in data.items()}

    nc = bacc.Bacc("TRN2", target_bir_lowering=False, num_devices=1)
    ins = {k: nc.dram_tensor(k, v.shape, mybir.dt.from_np(v.dtype), kind="ExternalInput").ap() for k, v in data.items()}
    out = nc.dram_tensor("out", (B * S, D), F32, kind="ExternalOutput").ap()
    program(nc, ins, out)
    result = run_bass_kernel_spmd(nc, [data], core_ids=[0])
    return result.results[0]["out"].reshape(B, S, D)
```
